# Optimizing a Trainium2 kernel written in Bass

```python
import numpy as np
import jax
import jax.numpy as jnp

def _softmax(x, axis=-1):
    return jax.nn.softmax(x, axis=axis)

def _gelu(x):
    return jax.nn.gelu(x, approximate=True)

def _silu(x):
    return jax.nn.silu(x)

def _sigmoid(x):
    return jax.nn.sigmoid(x)

def _layernorm(x, axis=-1, eps=1e-05):
    m = jnp.mean(x, axis=axis, keepdims=True)
    v = jnp.var(x, axis=axis, keepdims=True)
    return (x - m) / jnp.sqrt(v + eps)

def _scatter_add(tgt, idx, src, axis=0):
    return tgt.at[idx].add(src)

def _segment_sum(src, seg, n):
    return jax.ops.segment_sum(src, seg, n)
kernel_name = 'mk_hybrid_d1_jaxref_r8_97f304'

def setup_inputs(seed: int=0):
    np.random.seed(seed)
    _w = jnp.asarray

    def _L0_attn_a_setup():
        import jax, jax.numpy as jnp
        import numpy as np
        N_HEAD = 16

        def _rope_cache(T, head_dim):
            half = head_dim // 2
            inv_freq = 1.0 / 10000.0 ** (jnp.arange(half, dtype=jnp.float32) / half)
            t = jnp.arange(T, dtype=jnp.float32)
            freqs = jnp.einsum('i,j->ij', t, inv_freq)
            cos = jnp.repeat(jnp.cos(freqs), 2, axis=-1)
            sin = jnp.repeat(jnp.sin(freqs), 2, axis=-1)
            return (cos, sin)

        def _apply_rope(x, cos, sin):
            x1 = x[..., ::2]
            x2 = x[..., 1::2]
            x_rot = jnp.stack([-x2, x1], axis=-1).reshape(x.shape)
            return x * cos[None, None] + x_rot * sin[None, None]
        key = jax.random.key(seed)
        k1, k2, k3 = jax.random.split(key, 3)
        B, T, C = (2, 256, 128)
        x = jax.random.normal(k1, (B, T, C), dtype=jnp.float32)
        Wqkv = jax.random.normal(k2, (C, 3 * C), dtype=jnp.float32) * 0.02
        Wo = jax.random.normal(k3, (C, C), dtype=jnp.float32) * 0.02
        bo = jnp.zeros((C,), dtype=jnp.float32)
        return {'x': x, 'Wqkv': Wqkv, 'Wo': Wo, 'bo': bo}
    _L0_attn_a_in = _L0_attn_a_setup()

    def _L0_attn_b_setup():
        import jax, jax.numpy as jnp
        import numpy as np
        N_HEADS = 16
        D_MODEL = 128
        D_HEAD = 64
        MAX_SEQ_LEN = 128

        def _pos_bias(rel_pos_bias, T):
            i = jnp.arange(T)[:, None]
            j = jnp.arange(T)[None, :]
            idx = jnp.clip(MAX_SEQ_LEN - 1 - (i - j), 0, MAX_SEQ_LEN - 1)
            bias = rel_pos_bias[:, idx]
            return jnp.where((j <= i)[None], bias, 0.0)
        key = jax.random.key(seed)
        ks = jax.random.split(key, 7)
        std = np.sqrt(2.0 / (D_MODEL + D_HEAD)).astype(np.float32)
        hd = N_HEADS * D_HEAD
        Wq = jax.random.normal(ks[0], (D_MODEL, hd), jnp.float32) * std
        Wk = jax.random.normal(ks[1], (D_MODEL, hd), jnp.float32) * std
        Wv = jax.random.normal(ks[2], (D_MODEL, hd), jnp.float32) * std
        Wo = jax.random.normal(ks[3], (hd, D_MODEL), jnp.float32) * (1.0 / np.sqrt(hd))
        bo = jnp.zeros((D_MODEL,), jnp.float32)
        rel_pos_bias = jax.random.normal(ks[4], (N_HEADS, MAX_SEQ_LEN), jnp.float32) * 0.02
        x = jax.random.normal(ks[5], (4, 128, D_MODEL), jnp.float32)
        return {'x': x, 'Wq': Wq, 'Wk': Wk, 'Wv': Wv, 'Wo': Wo, 'bo': bo, 'rel_pos_bias': rel_pos_bias}
    _L0_attn_b_in = _L0_attn_b_setup()

    def _L0_ffn_setup():
        import jax, jax.numpy as jnp
        import numpy as np
        DIM = 128
        HIDDEN = 384
        SCALE = 1.0 / 127.0

        def _dequant(w_int, dtype):
            return w_int.astype(dtype) * jnp.asarray(SCALE, dtype)
        key = jax.random.key(seed)
        k_x, k_g, k_u, k_d = jax.random.split(key, 4)
        x = jax.random.normal(k_x, (4, 256, DIM), dtype=jnp.float32)
        w_gate = jax.random.randint(k_g, (HIDDEN, DIM), -127, 128, dtype=jnp.int32)
        w_up = jax.random.randint(k_u, (HIDDEN, DIM), -127, 128, dtype=jnp.int32)
        w_down = jax.random.randint(k_d, (DIM, HIDDEN), -127, 128, dtype=jnp.int32)
        return {'x': x, 'w_gate': w_gate, 'w_up': w_up, 'w_down': w_down}
    _L0_ffn_in = _L0_ffn_setup()
    _d = {'L0_attn_a_x': _L0_attn_a_in['x'], 'L0_attn_a_Wqkv': _L0_attn_a_in['Wqkv'], 'L0_attn_a_Wo': _L0_attn_a_in['Wo'], 'L0_attn_a_bo': _L0_attn_a_in['bo'], 'L0_attn_b_Wq': _L0_attn_b_in['Wq'], 'L0_attn_b_Wk': _L0_attn_b_in['Wk'], 'L0_attn_b_Wv': _L0_attn_b_in['Wv'], 'L0_attn_b_Wo': _L0_attn_b_in['Wo'], 'L0_attn_b_bo': _L0_attn_b_in['bo'], 'L0_attn_b_rel_pos_bias': _L0_attn_b_in['rel_pos_bias'], 'L0_ffn_w_gate': _L0_ffn_in['w_gate'], 'L0_ffn_w_up': _L0_ffn_in['w_up'], 'L0_ffn_w_down': _L0_ffn_in['w_down']}
    _x0 = _d['L0_attn_a_x']
    _d['L0_attn_a_x'] = jax.random.normal(jax.random.fold_in(jax.random.key(seed), 1), (4, 1024, 128), dtype=_x0.dtype)
    del _x0
    return _d

def reference(L0_attn_a_x, L0_attn_a_Wqkv, L0_attn_a_Wo, L0_attn_a_bo, L0_attn_b_Wq, L0_attn_b_Wk, L0_attn_b_Wv, L0_attn_b_Wo, L0_attn_b_bo, L0_attn_b_rel_pos_bias, L0_ffn_w_gate, L0_ffn_w_up, L0_ffn_w_down):

    def _L0_attn_a_ref(x, Wqkv, Wo, bo):
        import jax, jax.numpy as jnp
        import numpy as np
        N_HEAD = 16

        def _rope_cache(T, head_dim):
            half = head_dim // 2
            inv_freq = 1.0 / 10000.0 ** (jnp.arange(half, dtype=jnp.float32) / half)
            t = jnp.arange(T, dtype=jnp.float32)
            freqs = jnp.einsum('i,j->ij', t, inv_freq)
            cos = jnp.repeat(jnp.cos(freqs), 2, axis=-1)
            sin = jnp.repeat(jnp.sin(freqs), 2, axis=-1)
            return (cos, sin)

        def _apply_rope(x, cos, sin):
            x1 = x[..., ::2]
            x2 = x[..., 1::2]
            x_rot = jnp.stack([-x2, x1], axis=-1).reshape(x.shape)
            return x * cos[None, None] + x_rot * sin[None, None]
        B, T, C = x.shape
        H = N_HEAD
        D = C // H
        scale = D ** (-0.5)
        qkv = x @ Wqkv
        qkv = qkv.reshape(B, T, 3, H, D).transpose(2, 0, 3, 1, 4)
        q, k, v = (qkv[0], qkv[1], qkv[2])
        cos, sin = _rope_cache(T, D)
        q = _apply_rope(q, cos, sin)
        k = _apply_rope(k, cos, sin)
        att = jnp.einsum('bhqd,bhkd->bhqk', q, k) * scale
        causal = jnp.tril(jnp.ones((T, T), dtype=bool))
        att = jnp.where(causal[None, None], att, -jnp.inf)
        att = jax.nn.softmax(att, axis=-1)
        out = jnp.einsum('bhqk,bhkd->bhqd', att, v)
        out = out.transpose(0, 2, 1, 3).reshape(B, T, C)
        return out @ Wo + bo

    def _L0_attn_b_ref(x, Wq, Wk, Wv, Wo, bo, rel_pos_bias):
        import jax, jax.numpy as jnp
        import numpy as np
        N_HEADS = 16
        D_MODEL = 128
        D_HEAD = 64
        MAX_SEQ_LEN = 128

        def _pos_bias(rel_pos_bias, T):
            i = jnp.arange(T)[:, None]
            j = jnp.arange(T)[None, :]
            idx = jnp.clip(MAX_SEQ_LEN - 1 - (i - j), 0, MAX_SEQ_LEN - 1)
            bias = rel_pos_bias[:, idx]
            return jnp.where((j <= i)[None], bias, 0.0)
        B, T, _ = x.shape
        H, dh = (N_HEADS, D_HEAD)
        q = (x @ Wq).reshape(B, T, H, dh).transpose(0, 2, 1, 3)
        k = (x @ Wk).reshape(B, T, H, dh).transpose(0, 2, 1, 3)
        v = (x @ Wv).reshape(B, T, H, dh).transpose(0, 2, 1, 3)
        logits = jnp.einsum('bhqd,bhkd->bhqk', q, k)
        i = jnp.arange(T)[:, None]
        j = jnp.arange(T)[None, :]
        causal = jnp.where(j > i, -jnp.inf, 0.0)
        logits = logits + causal[None, None] + _pos_bias(rel_pos_bias, T)[None]
        logits = logits / dh
        probs = jax.nn.softmax(logits, axis=-1)
        out = jnp.einsum('bhqk,bhkd->bhqd', probs, v)
        out = out.transpose(0, 2, 1, 3).reshape(B, T, H * dh)
        return out @ Wo + bo

    def _L0_ffn_ref(x, w_gate, w_up, w_down):
        import jax, jax.numpy as jnp
        import numpy as np
        DIM = 128
        HIDDEN = 384
        SCALE = 1.0 / 127.0

        def _dequant(w_int, dtype):
            return w_int.astype(dtype) * jnp.asarray(SCALE, dtype)
        wg = _dequant(w_gate, x.dtype)
        wu = _dequant(w_up, x.dtype)
        wd = _dequant(w_down, x.dtype)
        gate = jnp.einsum('bsd,hd->bsh', x, wg)
        up = jnp.einsum('bsd,hd->bsh', x, wu)
        h = jax.nn.silu(gate) * up
        return jnp.einsum('bsh,dh->bsd', h, wd)
    x = L0_attn_a_x
    x = x + _L0_attn_a_ref(_layernorm(x, axis=-1), L0_attn_a_Wqkv, L0_attn_a_Wo, L0_attn_a_bo)
    x = x + _L0_ffn_ref(_layernorm(x, axis=-1), L0_ffn_w_gate, L0_ffn_w_up, L0_ffn_w_down)
    x = x + _L0_attn_b_ref(_layernorm(x, axis=-1), L0_attn_b_Wq, L0_attn_b_Wk, L0_attn_b_Wv, L0_attn_b_Wo, L0_attn_b_bo, L0_attn_b_rel_pos_bias)
    x = x + _L0_ffn_ref(_layernorm(x, axis=-1), L0_ffn_w_gate, L0_ffn_w_up, L0_ffn_w_down)
    return x

_drawn_inputs = setup_inputs


def setup_inputs(seed=0):
    import zlib

    import numpy as np

    out = dict(_drawn_inputs(seed))
    spreads = {'L0_attn_a_bo': (0.0, 0.1), 'L0_attn_b_bo': (0.0, 0.8)}
    factors = {'L0_attn_a_Wqkv': 7.321,
     'L0_attn_a_Wo': 7.588,
     'L0_attn_b_Wq': 8.0,
     'L0_attn_b_Wk': 8.0,
     'L0_attn_b_Wv': 8.0,
     'L0_attn_b_Wo': 8.0,
     'L0_attn_b_rel_pos_bias': 8.0}
    for name, (base, spread) in spreads.items():
        noise = np.random.default_rng([zlib.crc32(name.encode()), seed]).standard_normal(out[name].shape)
        drawn = base * np.exp(spread * noise) if base else spread * noise
        out[name] = jnp.asarray(drawn.astype(out[name].dtype))
    for name, factor in factors.items():
        out[name] = (out[name] * factor).astype(out[name].dtype)
    return out
```

```python
import numpy as np
import concourse.bass as bass
from concourse import mybir
from concourse.alu_op_type import AluOpType as ALU
from contextlib import ExitStack

F32 = mybir.dt.float32
BF16 = mybir.dt.bfloat16
I32 = mybir.dt.int32
ACT = mybir.ActivationFunctionType
AX = mybir.AxisListType
ds = bass.ds

P = 128
B, T, D = 4, 1024, 128
NT = B * T // P
CH = 512
NC = B * T // CH
TPC = CH // P
NQ = T // P
HEADS = 16
HD_A = D // HEADS
HD_B = 64
HID = 384
NH = HID // P
EPS = 1e-5
W_SCALE = float(np.float32(1.0 / 127.0))
LOW = -3.0e38
RANGE = 128
LROW = 3 * RANGE

G4 = 4
UNITS = B * HEADS // G4
NPROD = 9
ROW_M = NPROD * HD_A
ROWS = 96
VW = HD_A + 1
VU = NQ * G4 * VW

PAIRS = HEADS // 2
ITERS = B * PAIRS


def tok_tiles(x):
    return x.rearrange("b (n p) d -> p (b n) d", p=P)


def rope_tables():
    half = HD_A // 2
    inv = (np.float32(1.0) / np.power(np.float32(10000.0), np.arange(half, dtype=np.float32) / np.float32(half))).astype(np.float32)
    ang = (np.arange(T, dtype=np.float32)[:, None] * inv[None, :]).astype(np.float32)
    both = np.stack([np.cos(ang.astype(np.float64)), np.sin(ang.astype(np.float64))])
    return np.ascontiguousarray(np.repeat(both, 2, axis=-1).transpose(0, 2, 1)).astype(np.float32)


def wait_alone(eng, sem, value, seen):
    eng.wait_ge(sem, value)
    eng.sem_inc(seen, 1)


def prepare(nc, g, x, wqkv, rel, w_gate, w_up, w_down, wo_a, bo_a, bo_b, tables):
    with ExitStack() as c:
        sb = lambda name, shape, dt=F32: c.enter_context(nc.sbuf_tensor(name, shape, dt))
        sem = lambda name: g.ctx.enter_context(nc.semaphore(name))
        w3 = sb("w_qkv", [P, 3, P])
        wrot = sb("w_rot", [P, 2, P])
        cos = sb("cos", [P, T])
        sin = sb("sin", [P, T])
        wi = sb("w_int", [P, 3, HID], I32)
        wf = sb("w_float", [P, 3, HID])
        relrow = sb("rel_rows", [HEADS, RANGE])
        lrow = sb("bias_rows", [HEADS, LROW])
        stat = sb("stat", [P, TPC, 6])
        mv = sb("mean_var", [P, TPC, 2])
        ve = sb("var_eps", [P, TPC])
        rstd = sb("rstd", [P, TPC])
        xn = sb("xn", [P, TPC, P])
        xnT = sb("xnT", [P, CH])
        tc = sb("times_cos", [P, 2, CH])
        tsn = sb("times_sin", [P, 2, CH])
        qk = sb("qk_roped", [P, 2, CH])
        rest = sb("qk_rest", [P, 2, CH])
        parts = sb("qk_parts", [P, 3, 2, CH], BF16)

        x_loaded, w_loaded, tab_loaded = sem("x_loaded"), sem("w_loaded"), sem("tab_loaded")
        int_loaded, rel_loaded, later_loaded = sem("int_loaded"), sem("rel_loaded"), sem("later_loaded")
        zeroed, consts, ones_set = sem("zeroed"), g.consts, sem("ones_set")
        rot_ready, wf_ready, ffn_T, ffn_stored = sem("rot_ready"), sem("wf_ready"), sem("ffn_T"), sem("ffn_stored")
        lrow_ready, lrow_stored = sem("lrow_ready"), sem("lrow_stored")
        stats_done, aggr_done, var_ready, rstd_ready = sem("stats_done"), sem("aggr_done"), sem("var_ready"), sem("rstd_ready")
        xn_ready, xn_T, xnT_ready = sem("xn_ready"), sem("xn_T"), sem("xnT_ready")
        qk_mm, v_mm, v_stored = sem("qk_mm"), sem("v_mm"), sem("v_stored")
        rope_read, q_ready, p1_ready, rest_ready, p2_ready, split_done = (
            sem("rope_read"), sem("q_ready"), sem("p1_ready"), sem("rest_ready"), sem("p2_ready"), sem("split_done"))
        parts_stored = sem("parts_stored")
        psT = g.ps[:, 0:CH]
        psV = g.ps[:, CH:2 * CH]
        psM = g.ps[:, 2 * CH:4 * CH]
        psR = g.ps[:, 4 * CH:6 * CH]
        psW = g.ps[:, 6 * CH:8 * CH]

        with nc.Block() as block:

            @block.sync
            def _(sp):
                for b in range(B):
                    sp.dma_start(g.X[:, b * NQ:(b + 1) * NQ, :], tok_tiles(x)[:, b * NQ:(b + 1) * NQ, :]).then_inc(x_loaded, 16)
                for n, w in enumerate((w_gate, w_up)):
                    sp.dma_start(wi[:, n, :].rearrange("p (t d) -> p t d", t=NH), w.rearrange("(t p) d -> p t d", p=P)).then_inc(int_loaded, 16)
                sp.dma_start(wi[:, 2, :], w_down).then_inc(int_loaded, 16)
                sp.dma_start(relrow[:, :], rel).then_inc(rel_loaded, 16)
                sp.dma_start(g.wo_a[:, :], wo_a).then_inc(later_loaded, 16)
                for dst, src in ((g.bo_a, bo_a), (g.bo_b, bo_b)):
                    sp.dma_start(dst[:, :], bass.AP(src.tensor, src.offset, [[0, P], [1, P]])).then_inc(later_loaded, 16)
                sp.wait_ge(lrow_ready, 3)
                sp.dma_start(g.lrep, lrow[:, :].unsqueeze(1).broadcast_to([HEADS, P, LROW])).then_inc(lrow_stored, 16)
                with sp.Fori(0, NC) as n:
                    sp.wait_ge(split_done, n + 1)
                    sp.dma_start(g.qs.rearrange("s k p t -> p (s k) t")[:, :, ds(n * CH, CH)],
                                 parts[:, :, :, :].rearrange("p s k t -> p (s k) t")).then_inc(parts_stored, 16)
                sp.wait_ge(parts_stored, 16 * NC)
                sp.wait_ge(lrow_stored, 16)
                sp.wait_ge(later_loaded, 48)

            @block.gpsimd
            def _(pool):
                pool.memset(g.identf[:, :], 0.0).then_inc(zeroed, 1)
                pool.memset(g.identb[:, :], 0.0).then_inc(zeroed, 1)
                pool.memset(g.expo[:, :], -0.5).then_inc(zeroed, 1)
                pool.wait_ge(zeroed, 3)
                for m in (g.identf, g.identb):
                    pool.affine_select(out=m[:, :], in_=m[:, :], compare_op=ALU.not_equal, fill=1.0, base=0,
                                       pattern=[[-1, P]], channel_multiplier=1).then_inc(consts, 1)
                pool.memset(g.maskq[:, :], 0.0).then_inc(zeroed, 1)
                pool.memset(g.maskk[:, :], 0.0).then_inc(zeroed, 1)
                pool.memset(g.zero_one[:, 0, :, :], 0.0).then_inc(zeroed, 1)
                pool.memset(g.zero_one[:, 1, :, :], 1.0).then_inc(zeroed, 1)
                pool.memset(g.V[:, :], 1.0).then_inc(ones_set, 1)
                pool.wait_ge(zeroed, 7)
                pool.affine_select(out=g.maskq[:, CH - P:CH], in_=g.maskq[:, CH - P:CH], compare_op=ALU.is_ge, fill=LOW, base=0,
                                   pattern=[[-1, P]], channel_multiplier=1).then_inc(consts, 1)
                pool.affine_select(out=g.maskk[:, :], in_=g.maskk[:, :], compare_op=ALU.is_ge, fill=LOW, base=0,
                                   pattern=[[1, P]], channel_multiplier=-1).then_inc(consts, 1)

                def rstd_of(n):
                    pool.wait_ge(var_ready, n + 1)
                    pool.tensor_tensor(rstd[:, :], ve[:, :], g.expo[:, :], ALU.pow).then_inc(rstd_ready, 1)

                def rope_sum(n):
                    pool.wait_ge(rope_read, n + 1)
                    pool.wait_ge(split_done, n)
                    pool.tensor_tensor(qk[:, :, :], tc[:, :, :], tsn[:, :, :], ALU.add).then_inc(q_ready, 1)

                rstd_of(0)
                with pool.Fori(0, NC - 1) as n:
                    rstd_of(n + 1)
                    rope_sum(n)
                rope_sum(NC - 1)

            @block.scalar
            def _(act):
                act.dma_start(w3[:, :, :].rearrange("p k m -> p (k m)"), wqkv).then_inc(w_loaded, 16)
                for dst, k in ((cos, 0), (sin, 1)):
                    for h in range(HEADS):
                        act.dma_start(dst[h * HD_A:(h + 1) * HD_A, :], tables[k, :, :]).then_inc(tab_loaded, 16)
                act.wait_ge(w_loaded, 16)
                pairs = w3[:, 0:2, :].rearrange("p k (m two) -> p k m two", two=2)
                rot = wrot[:, :, :].rearrange("p k (m two) -> p k m two", two=2)
                act.mul(rot[:, :, :, 0], pairs[:, :, :, 1], -1.0)
                act.copy(rot[:, :, :, 1], pairs[:, :, :, 0]).then_inc(rot_ready, 1)
                for n, dst in enumerate((g.wgT, g.wuT, g.wdT)):
                    act.wait_ge(ffn_T, n + 1)
                    act.copy(dst[:, :], psW[:, (n % 2) * CH:(n % 2) * CH + HID]).then_inc(ffn_stored, 1)
                act.wait_ge(ones_set, 1)
                with act.Fori(0, NC) as n:
                    act.wait_ge(xn_T, n + 1)
                    act.wait_ge(v_mm, n)
                    act.copy(xnT[:, :], psT).then_inc(xnT_ready, 1)
                    act.wait_ge(v_mm, n + 1)
                    vb = g.V[:, ds((n // 2) * (4 * VU) + (n % 2) * (TPC * G4 * VW), 3 * VU + TPC * G4 * VW)]
                    for u in range(4):
                        dst = vb[:, u * VU:u * VU + TPC * G4 * VW].rearrange("p (t j w) -> p t j w", t=TPC, j=G4)[:, :, :, 0:HD_A]
                        src = psV.rearrange("p (t u j d) -> p t u j d", t=TPC, u=4, j=G4)[:, :, u, :, :]
                        ins = act.copy(dst, src)
                    ins.then_inc(v_stored, 1)
                    act.wait_ge(q_ready, n + 1)
                    act.wait_ge(parts_stored, 16 * n)
                    act.copy(parts[:, 0, :, :], qk[:, :, :]).then_inc(p1_ready, 1)

            @block.vector
            def _(dve):
                dve.wait_ge(int_loaded, 48)
                dve.tensor_scalar(wf[:, :, :], wi[:, :, :], W_SCALE, None, ALU.mult).then_inc(wf_ready, 1)
                dve.wait_ge(rel_loaded, 16)
                dve.memset(lrow[:, 0:RANGE], 0.0).then_inc(lrow_ready, 1)
                dve.tensor_scalar(lrow[:, RANGE:2 * RANGE], relrow[:, :], relrow[:, 0:1], None, ALU.subtract).then_inc(lrow_ready, 1)
                dve.memset(lrow[:, 2 * RANGE:LROW], LOW).then_inc(lrow_ready, 1)
                dve.wait_ge(x_loaded, 64)

                def stats(n):
                    for t in range(TPC):
                        ins = dve.bn_stats(stat[:, t, :], g.X[:, ds(n * TPC + t, 1), :].rearrange("p a d -> p (a d)"))
                    ins.then_inc(stats_done, 1)
                    wait_alone(dve, stats_done, n + 1, g.seen_dve)
                    for t in range(TPC):
                        ins = dve.bn_aggr(mv[:, t, :], stat[:, t, :])
                    ins.then_inc(aggr_done, 1)
                    dve.wait_ge(aggr_done, n + 1)
                    dve.tensor_scalar_add(ve[:, :], mv[:, :, 1], EPS).then_inc(var_ready, 1)

                def norm(n):
                    dve.wait_ge(rstd_ready, n + 1)
                    dve.wait_ge(xn_T, n)
                    for t in range(TPC):
                        ins = dve.tensor_scalar(xn[:, t, :], g.X[:, ds(n * TPC + t, 1), :].rearrange("p a d -> p (a d)"),
                                                mv[:, t, 0:1], rstd[:, t:t + 1], ALU.subtract, ALU.mult)
                    ins.then_inc(xn_ready, 1)

                def rope(n):
                    dve.wait_ge(qk_mm, n + 1)
                    dve.wait_ge(q_ready, n)
                    for k in range(2):
                        dve.tensor_tensor(tc[:, k, :], psM[:, k * CH:(k + 1) * CH], cos[:, ds((n % 2) * CH, CH)], ALU.mult)
                    for k in range(2):
                        ins = dve.tensor_tensor(tsn[:, k, :], psR[:, k * CH:(k + 1) * CH], sin[:, ds((n % 2) * CH, CH)], ALU.mult)
                    ins.then_inc(rope_read, 1)

                def split(n):
                    dve.wait_ge(p1_ready, n + 1)
                    dve.tensor_tensor(rest[:, :, :], qk[:, :, :], parts[:, 0, :, :], ALU.subtract).then_inc(rest_ready, 1)
                    dve.wait_ge(rest_ready, n + 1)
                    dve.tensor_copy(parts[:, 1, :, :], rest[:, :, :]).then_inc(p2_ready, 1)
                    dve.wait_ge(p2_ready, n + 1)
                    dve.tensor_tensor(parts[:, 2, :, :], rest[:, :, :], parts[:, 1, :, :], ALU.subtract).then_inc(split_done, 1)

                stats(0)
                norm(0)
                dve.wait_ge(tab_loaded, 2 * 16 * HEADS)
                with dve.Fori(0, NC - 1) as n:
                    stats(n + 1)
                    rope(n)
                    norm(n + 1)
                    split(n)
                rope(NC - 1)
                split(NC - 1)

            @block.tensor
            def _(pe):
                pe.wait_ge(consts, 2)
                pe.wait_ge(wf_ready, 1)
                for n in range(3):
                    if n == 2:
                        pe.wait_ge(ffn_stored, 1)
                    for t in range(NH):
                        ins = pe.transpose(psW[:, (n % 2) * CH + t * P:(n % 2) * CH + (t + 1) * P], wf[:, n, t * P:(t + 1) * P], g.identf[:, :])
                    ins.then_inc(ffn_T, 1)
                pe.wait_ge(rot_ready, 1)
                with pe.Fori(0, NC) as n:
                    pe.wait_ge(xn_ready, n + 1)
                    pe.wait_ge(xnT_ready, n)
                    for t in range(TPC):
                        ins = pe.transpose(psT[:, t * P:(t + 1) * P], xn[:, t, :], g.identf[:, :])
                    ins.then_inc(xn_T, 1)
                    pe.wait_ge(xnT_ready, n + 1)
                    pe.wait_ge(rope_read, n)
                    for k in range(2):
                        pe.matmul(psM[:, k * CH:(k + 1) * CH], w3[:, k, :], xnT[:, :], start=True, stop=True)
                    for k in range(2):
                        ins = pe.matmul(psR[:, k * CH:(k + 1) * CH], wrot[:, k, :], xnT[:, :], start=True, stop=True)
                    ins.then_inc(qk_mm, 1)
                    pe.wait_ge(v_stored, n)
                    for t in range(TPC):
                        ins = pe.matmul(psV[:, t * P:(t + 1) * P], xnT[:, t * P:(t + 1) * P], w3[:, 2, :], start=True, stop=True)
                    ins.then_inc(v_mm, 1)


FIRST_PASS = []
for _qt in range(NQ):
    _w = (_qt + 1) * P
    if _w > CH:
        FIRST_PASS.append((_qt, 0, CH, 1))
    FIRST_PASS.append((_qt, (_w - 1) // CH * CH, (_w - 1) % CH + 1, 0))
SECOND_PASS = [(qc, kt, max(0, kt * P - qc * CH)) for qc in range(T // CH) for kt in range((qc + 1) * TPC)]
STEPS = len(SECOND_PASS)
TILES = G4 * len(FIRST_PASS)


def interleave():
    tiles = [w for _ in range(G4) for _, _, w, _ in FIRST_PASS]
    total = sum(tiles)
    out, at, cols, seen = [], 0, 0, 0
    whole = sum(CH - off for _, _, off in SECOND_PASS)
    for _, _, off in SECOND_PASS:
        seen += CH - off
        while at < len(tiles) and cols < AHEAD * total * seen / whole:
            cols += tiles[at]
            at += 1
        out.append(at)
    assert out[-1] == len(tiles)
    return out


AHEAD = 1.2
UPTO = interleave()


def rope_attention(nc, g):
    with ExitStack() as c:
        sb = lambda name, shape, dt=F32: c.enter_context(nc.sbuf_tensor(name, shape, dt))
        sem = lambda name: g.ctx.enter_context(nc.semaphore(name))
        stack = [sb(f"stack{i}", [ROWS, 2, G4, T], BF16) for i in range(3)]
        vu = [sb(f"v_unit{i}", [P, NQ, G4, VW]) for i in range(3)]
        pt = [sb(f"probs{i}", [P, G4, CH]) for i in range(3)]
        junk = sb("junk", [P, 2, CH], BF16)
        mx = sb("row_max", [P, 2, G4, NQ])
        mneg = sb("neg_max_parts", [P, 3, G4 * NQ], BF16)
        mrest = sb("max_rest", [P, G4 * NQ])
        mrow = sb("max_rows", [3 * G4 * NQ, P], BF16)
        oT = sb("oT", [P, CH])
        rden = sb("rden", [P, TPC, G4])

        st_zeroed = sem("st_zeroed")
        ones_in = sem("ones_in")
        st_loaded = [sem(f"st_loaded{i}") for i in range(3)]
        p1_done, p1_max = sem("p1_done"), sem("p1_max")
        far_joined, mneg1, mrest1, mneg2, mneg3, m_T, m_row, m_loaded = (
            sem("far_joined"), sem("mneg1"), sem("mrest1"), sem("mneg2"), sem("mneg3"), sem("m_T"), sem("m_row"), sem("m_loaded"))
        v_unit, s2_done, exp_done, pv_done = sem("v_unit"), sem("s2_done"), sem("exp_done"), sem("pv_done")
        o_cleared, o_out, o_T, o_rden, o_norm = sem("o_cleared"), sem("o_out"), sem("o_T"), sem("o_rden"), sem("o_norm")

        bank = lambda n, k=1: g.ps[:, n * CH:(n + k) * CH]
        psS = [bank(0, 2).rearrange("p (j q) -> p j q", j=2), bank(2, 2).rearrange("p (j q) -> p j q", j=2)]
        ps1 = [bank(4), bank(5)]
        psO = bank(6)
        psX = bank(7)
        LOADS = 7 * 16

        def q_side(i):
            return stack[i][:, 0, :, :]

        def k_side(i):
            return stack[i][:, 1, :, :]

        with nc.Block() as block:

            @block.sync
            def _(sp):
                def load(u, i):
                    rows = (u // 4) * T
                    for qp in range(3):
                        src = g.qs[qp, 0, ds((u % 4) * (G4 * HD_A), G4 * HD_A), ds(rows, T)].rearrange("(h d) t -> d h t", d=HD_A)
                        for kp in range(3):
                            r = (qp * 3 + kp) * HD_A
                            sp.dma_start(stack[i][r:r + HD_A, 0, :, :], src).then_inc(st_loaded[i], 16)
                    for kp in range(3):
                        src = g.qs[kp, 1, ds((u % 4) * (G4 * HD_A), G4 * HD_A), ds(rows, T)].rearrange("(h d) t -> d h t", d=HD_A)
                        for qp in range(3):
                            r = (qp * 3 + kp) * HD_A
                            sp.dma_start(stack[i][r:r + HD_A, 1, :, :], src).then_inc(st_loaded[i], 16)
                    sp.dma_start(q_side(i)[ROW_M:ROW_M + 3, :, :], g.zero_one[:, 0, :, :]).then_inc(st_loaded[i], 16)

                sp.wait_ge(st_zeroed, 3)
                for i in range(3):
                    sp.dma_start(k_side(i)[ROW_M:ROW_M + 3, :, :], g.zero_one[:, 1, :, :]).then_inc(ones_in, 16)
                    load(i, i)

                def max_rows(u, i):
                    sp.wait_ge(m_row, u + 1)
                    sp.dma_start(q_side(i)[ROW_M:ROW_M + 3, :, :], mrow[:, :]).then_inc(m_loaded, 16)

                def half(u, i, ahead):
                    if ahead:
                        max_rows(u + 1, (i + 1) % 3)
                    sp.wait_ge(s2_done, 2 * STEPS * (u + 1))
                    load((u + 3) % UNITS, i)

                max_rows(0, 0)
                half(0, 0, True)
                with sp.Fori(0, (UNITS - 4) // 3) as v:
                    for k in range(3):
                        half(v * 3 + (k + 1), (k + 1) % 3, True)
                half(UNITS - 3, (UNITS - 3) % 3, True)
                half(UNITS - 2, (UNITS - 2) % 3, True)
                for i in range(3):
                    sp.wait_ge(st_loaded[i], 16 * 19 * len([u for u in range(UNITS + 2) if u % 3 == i]))

            @block.gpsimd
            def _(pool):
                for i in range(3):
                    pool.memset(stack[i][64:ROWS, :, :, :].rearrange("p a h t -> p (a h t)").bitcast(F32), 0.0).then_inc(st_zeroed, 1)

            @block.scalar
            def _(act):
                def values(u, i):
                    act.wait_ge(pv_done, STEPS * (u - 2) if not isinstance(u, int) else max(0, STEPS * (u - 2)))
                    act.copy(vu[i][:, :, :, :].rearrange("p t j w -> p (t j w)"), g.V[:, ds(u * VU, VU)]).then_inc(v_unit, 1)

                def o_evac(n, pv):
                    act.wait_ge(pv_done, pv)
                    act.wait_ge(o_T, n)
                    act.copy(oT[:, :], psO).then_inc(o_out, 1)

                def half(u, i, first, ahead):
                    if ahead:
                        values(u + 1, (i + 1) % 3)
                    for s, (qc, kt, off) in enumerate(SECOND_PASS):
                        for x in range(2):
                            act.wait_ge(s2_done, u * (2 * STEPS) + (2 * s + x + 1))
                            if x == 0 and not (first and s < 3):
                                act.wait_ge(pv_done, u * STEPS + (s - 2))
                            act.activation(pt[s % 3][:, 2 * x:2 * x + 2, off:CH], psS[x][:, :, off:CH], ACT.Exp,
                                           scale=float(HD_A) ** -0.5).then_inc(exp_done, 1)
                        if s == 0 and not first:
                            o_evac(u * 2 - 1, u * STEPS)
                        if s == TPC:
                            o_evac(u * 2, u * STEPS + TPC)
                    if ahead:
                        max_row(u + 1)

                def max_row(u):
                    act.wait_ge(m_T, u + 1)
                    act.wait_ge(m_loaded, 16 * u)
                    act.copy(mrow[:, :], psX[0:3 * G4 * NQ, 0:P // 2].bitcast(BF16)).then_inc(m_row, 1)

                act.copy(vu[0][:, :, :, :].rearrange("p t j w -> p (t j w)"), g.V[:, 0:VU]).then_inc(v_unit, 1)
                max_row(0)
                half(0, 0, True, True)
                with act.Fori(0, (UNITS - 4) // 3) as v:
                    for k in range(3):
                        half(v * 3 + (k + 1), (k + 1) % 3, False, True)
                half(UNITS - 3, (UNITS - 3) % 3, False, True)
                half(UNITS - 2, (UNITS - 2) % 3, False, True)
                half(UNITS - 1, (UNITS - 1) % 3, False, False)
                o_evac(2 * UNITS - 1, UNITS * STEPS)

            @block.vector
            def _(dve):
                def tiles(u, lo, hi):
                    for n in range(lo, hi):
                        h, (qt, k0, w, far) = n // len(FIRST_PASS), FIRST_PASS[n % len(FIRST_PASS)]
                        if far:
                            dve.wait_ge(p1_done, u * TILES + (n + 1))
                        else:
                            wait_alone(dve, p1_done, u * TILES + (n + 1), g.seen_dve)
                        if far:
                            ins = dve.reduce_max(mx[:, 1, h, qt:qt + 1], ps1[n % 2][:, 0:w], AX.X)
                        else:
                            ins = dve.tensor_tensor_reduce(out=junk[:, n % 2, 0:w], in0=ps1[n % 2][:, 0:w], in1=g.maskq[:, CH - w:CH],
                                                           scale=1.0, scalar=LOW, op0=ALU.add, op1=ALU.max,
                                                           accum_out=mx[:, 0, h, qt:qt + 1])
                        ins.then_inc(p1_max, 1)

                def split_max(u):
                    near = NQ - TPC
                    dve.wait_ge(p1_max, TILES * (u + 1))
                    dve.tensor_tensor(mx[:, 0, :, near:NQ], mx[:, 0, :, near:NQ], mx[:, 1, :, near:NQ], ALU.max).then_inc(far_joined, 1)
                    dve.wait_ge(far_joined, u + 1)
                    m = mx[:, 0, :, :].rearrange("p h q -> p (h q)")
                    dve.wait_ge(m_T, u)
                    dve.tensor_scalar(mneg[:, 0, :], m, -1.0, None, ALU.mult).then_inc(mneg1, 1)
                    dve.wait_ge(mneg1, u + 1)
                    dve.scalar_tensor_tensor(mrest[:, :], m, -1.0, mneg[:, 0, :], ALU.mult, ALU.subtract).then_inc(mrest1, 1)
                    dve.wait_ge(mrest1, u + 1)
                    dve.tensor_copy(mneg[:, 1, :], mrest[:, :]).then_inc(mneg2, 1)
                    dve.wait_ge(mneg2, u + 1)
                    dve.tensor_tensor(mneg[:, 2, :], mrest[:, :], mneg[:, 1, :], ALU.subtract).then_inc(mneg3, 1)

                def normalise(u, n, qc):
                    dve.wait_ge(o_T, n + 1)
                    o = psX.rearrange("p (t j w) -> p t j w", t=TPC, j=G4)
                    dve.reciprocal(rden[:, :, :], o[:, :, :, HD_A]).then_inc(o_rden, 1)
                    dve.wait_ge(o_rden, n + 1)
                    first = (u // 4) * (NQ * D) + (u % 4) * (G4 * HD_A) + qc * (TPC * D)
                    out = g.O[:, ds(first, (TPC - 1) * D + G4 * HD_A)]
                    for t in range(TPC):
                        ins = dve.tensor_tensor(out[:, t * D:t * D + G4 * HD_A].rearrange("p (j d) -> p j d", j=G4), o[:, t, :, 0:HD_A],
                                                rden[:, t, :].unsqueeze(2).broadcast_to([P, G4, HD_A]), ALU.mult)
                    ins.then_inc(o_norm, 1)

                def half(u, first, ahead):
                    at = 0
                    for s in range(STEPS):
                        if ahead:
                            tiles(u + 1, at, UPTO[s])
                            at = UPTO[s]
                        if s == 1 and not first:
                            normalise(u - 1, u * 2 - 1, 1)
                        if s == TPC + 1:
                            normalise(u, u * 2, 0)
                        if ahead and s == LAST_TILES:
                            split_max(u + 1)

                dve.memset(psO, 0.0).then_inc(o_cleared, 1)
                dve.wait_ge(g.consts, 4)
                tiles(0, 0, TILES)
                split_max(0)
                half(0, True, True)
                with dve.Fori(0, (UNITS - 4) // 3) as v:
                    for k in range(3):
                        half(v * 3 + (k + 1), False, True)
                half(UNITS - 3, False, True)
                half(UNITS - 2, False, True)
                half(UNITS - 1, False, False)
                normalise(UNITS - 1, 2 * UNITS - 1, 1)

            @block.tensor
            def _(pe):
                def loaded(i, n):
                    pe.wait_ge(st_loaded[i], n * (16 * 19))

                def scores1(u, i, lo, hi):
                    for n in range(lo, hi):
                        h, (qt, k0, w, far) = n // len(FIRST_PASS), FIRST_PASS[n % len(FIRST_PASS)]
                        if not (isinstance(u, int) and u == 0 and n < 2):
                            pe.wait_ge(p1_max, u * TILES + (n - 1))
                        pe.matmul(ps1[n % 2][:, 0:w], q_side(i)[:, h, qt * P:(qt + 1) * P], k_side(i)[:, h, k0:k0 + w],
                                  start=True, stop=True).then_inc(p1_done, 1)

                def scores2(u, i, s, x, first):
                    qc, kt, off = SECOND_PASS[s]
                    if not (first and s == 0):
                        pe.wait_ge(exp_done, u * (2 * STEPS) + (2 * s + x - 1))
                    diagonal = kt >= qc * TPC
                    for j in range(2):
                        h = 2 * x + j
                        ins = pe.matmul(psS[x][:, j, off:CH], k_side(i)[:, h, kt * P:(kt + 1) * P], q_side(i)[:, h, qc * CH + off:(qc + 1) * CH],
                                        start=True, stop=not diagonal)
                        if diagonal:
                            ins = pe.matmul(psS[x][:, j, off:off + P], g.identb[:, :], g.maskk[:, :], start=False, stop=True)
                    ins.then_inc(s2_done, 1)

                def weighted(u, i, s, first):
                    qc, kt, off = SECOND_PASS[s]
                    last = (qc + 1) * TPC - 1
                    pe.wait_ge(exp_done, u * (2 * STEPS) + (2 * s + 2))
                    if s == 0:
                        pe.wait_ge(v_unit, u + 1)
                    if kt == 0 and not (first and s == 0):
                        pe.wait_ge(o_out, u * 2 + qc)
                    for h in range(G4):
                        ins = pe.matmul(psO[32 * h:32 * h + VW, off:CH], vu[i][:, kt, h, :], pt[s % 3][:, h, off:CH],
                                        start=kt == 0, stop=kt == last)
                    ins.then_inc(pv_done, 1)

                def o_transposed(n, others):
                    pe.wait_ge(o_out, n + 1)
                    others()
                    for t in range(TPC):
                        ins = pe.transpose(psX[:, t * P:(t + 1) * P], oT[:, t * P:(t + 1) * P], g.identf[:, :])
                    ins.then_inc(o_T, 1)

                def max_transposed(u):
                    pe.wait_ge(mneg3, u + 1)
                    if not (isinstance(u, int) and u == 0):
                        pe.wait_ge(o_norm, 2 * u - 1)
                    pe.transpose(psX[0:3 * G4 * NQ, 0:P // 2].bitcast(BF16), mneg[:, :, :].rearrange("p s n -> p (s n)"), g.identb[:, :]).then_inc(m_T, 1)

                def half(u, i, first, ahead, filled=0):
                    at = 0
                    if ahead:
                        loaded((i + 1) % 3, filled)
                    pe.wait_ge(m_loaded, 16 * (u + 1))
                    for s in range(STEPS):
                        upto = UPTO[s] if ahead else 0
                        mid = (at + upto) // 2
                        scores2(u, i, s, 0, first)
                        if ahead:
                            scores1(u + 1, (i + 1) % 3, at, mid)
                        scores2(u, i, s, 1, first)
                        if ahead:
                            scores1(u + 1, (i + 1) % 3, mid, upto)
                        at = upto
                        if s > 0:
                            weighted(u, i, s - 1, first)
                        elif not first:
                            weighted(u - 1, (i + 2) % 3, STEPS - 1, False)
                        if s == 1 and not first:
                            o_transposed(u * 2 - 1, lambda: pe.wait_ge(m_row, u + 1))
                        if s == TPC + 1:
                            o_transposed(u * 2, (lambda: pe.wait_ge(m_row, u + 1)) if first else (lambda: pe.wait_ge(o_norm, u * 2)))
                    if ahead:
                        max_transposed(u + 1)

                pe.wait_ge(ones_in, 48)
                pe.wait_ge(st_zeroed, 3)
                pe.wait_ge(o_cleared, 1)
                loaded(0, 1)
                scores1(0, 0, 0, TILES)
                max_transposed(0)
                half(0, 0, True, True, 1)
                with pe.Fori(0, (UNITS - 4) // 3) as v:
                    for k in range(3):
                        half(v * 3 + (k + 1), (k + 1) % 3, False, True, v + (2 + k) // 3 + 1)
                half(UNITS - 3, (UNITS - 3) % 3, False, True, (UNITS - 2) // 3 + 1)
                half(UNITS - 2, (UNITS - 2) % 3, False, True, (UNITS - 1) // 3 + 1)
                half(UNITS - 1, (UNITS - 1) % 3, False, False)
                weighted(UNITS - 1, (UNITS - 1) % 3, STEPS - 1, False)
                o_transposed(2 * UNITS - 1, lambda: pe.wait_ge(o_norm, 2 * UNITS - 1))


LAST_TILES = next(s for s in range(STEPS) if UPTO[s] == TILES)


def ffn(nc, g, second, out):
    with ExitStack() as c:
        tag = "2" if second else "1"
        sb = lambda name, shape, dt=F32: c.enter_context(nc.sbuf_tensor(name + tag, shape, dt))
        sem = lambda name: g.ctx.enter_context(nc.semaphore(name + tag))
        att = sb("att", [P, CH])
        attT = sb("attT", [P, CH])
        xb = sb("x_bias", [P, TPC, P])
        xc = [sb(f"x_mid{i}", [P, TPC, P]) for i in range(2)]
        x2 = sb("x_end", [P, TPC, P])
        stat = sb("f_stat", [P, TPC, 6])
        mv = sb("f_mean_var", [P, TPC, 2])
        ve = sb("f_var_eps", [P, TPC])
        rstd = sb("f_rstd", [P, TPC])
        stat2 = sb("f_stat_e", [P, TPC, 6])
        mv2 = sb("f_mean_var_e", [P, TPC, 2])
        ve2 = sb("f_var_eps_e", [P, TPC])
        rstd2 = sb("f_rstd_e", [P, TPC])
        xn = sb("f_xn", [P, TPC, P])
        xnT = sb("f_xnT", [P, CH])
        xe = sb("f_xn_e", [P, TPC, P])
        gate = sb("gate", [P, 2, CH])
        h = sb("hidden", [P, NH, CH])
        y = sb("f_yT", [P, CH])

        att_loaded, att_T, attT_ready, added_mm, xb_ready = (
            sem("att_loaded"), sem("att_T"), sem("attT_ready"), sem("added_mm"), sem("xb_ready"))
        xc_ready, stats_done, aggr_done, var_ready, rstd_ready, xn_ready = (
            sem("xc_ready"), sem("f_stats"), sem("f_aggr"), sem("f_var"), sem("f_rstd"), sem("f_xn"))
        xn_T, xnT_ready, gate_mm, up_mm, silu_done, h_ready = (
            sem("f_xn_T"), sem("f_xnT"), sem("gate_mm"), sem("up_mm"), sem("silu_done"), sem("h_ready"))
        y_mm, y_ready, y_T, x2_ready, x_kept = sem("y_mm"), sem("y_ready"), sem("y_T"), sem("x2_ready"), sem("x_kept")
        stats2_done, aggr2_done, var2_ready, rstd2_ready, xe_ready, xe_T, xeT_ready = (
            sem("e_stats"), sem("e_aggr"), sem("e_var"), sem("e_rstd"), sem("e_xn"), sem("e_T"), sem("e_xnT"))
        bank = lambda n: g.ps[:, n * CH:(n + 1) * CH]
        psG, psU = [bank(0), bank(1)], [bank(2), bank(3)]
        psY, psF, psA, psT = bank(4), bank(5), bank(6), bank(7)
        bias = g.bo_b if second else g.bo_a
        tiles = lambda ap: ap.rearrange("p (t d) -> p t d", t=TPC)
        flat = lambda ap: ap.rearrange("p t d -> p (t d)")

        def run(eng, front, body):
            front(0, 0)
            body(0, 0, True, True)
            with eng.Fori(0, (NC - 2) // 2) as v:
                for k in range(2):
                    body(v * 2 + (k + 1), (k + 1) % 2, False, True)
            body(NC - 1, (NC - 1) % 2, False, False)

        with nc.Block() as block:

            @block.sync
            def _(sp):
                def load(n):
                    sp.wait_ge(att_T, n)
                    src = g.yT if second else g.O
                    sp.dma_start(att[:, :], src[:, ds(n * CH, CH)]).then_inc(att_loaded, 16)

                def keep(n):
                    sp.wait_ge(x2_ready, n + 1)
                    if second:
                        dst = tok_tiles(out)[:, ds(n * TPC, TPC), :]
                        sp.dma_start(dst, x2[:, :, :]).then_inc(x_kept, 16)
                    else:
                        sp.dma_start(g.X[:, ds(n * TPC, TPC), :], x2[:, :, :]).then_inc(x_kept, 16)

                load(0)
                with sp.Fori(0, NC - 1) as n:
                    load(n + 1)
                    keep(n)
                keep(NC - 1)
                sp.wait_ge(x_kept, 16 * NC)

            @block.gpsimd
            def _(pool):
                def front(n, i):
                    pool.wait_ge(xc_ready, n)
                    pool.tensor_tensor(xb[:, :, :], g.X[:, ds(n * TPC, TPC), :],
                                       bias[:, :].unsqueeze(1).broadcast_to([P, TPC, P]), ALU.add).then_inc(xb_ready, 1)
                    pool.wait_ge(var_ready, n + 1)
                    pool.tensor_tensor(rstd[:, :], ve[:, :], g.expo[:, :], ALU.pow).then_inc(rstd_ready, 1)

                def body(n, i, first, ahead):
                    if ahead:
                        front(n + 1, 1 - i)
                    if not second:
                        pool.wait_ge(var2_ready, n + 1)
                        pool.tensor_tensor(rstd2[:, :], ve2[:, :], g.expo[:, :], ALU.pow).then_inc(rstd2_ready, 1)

                run(pool, front, body)

            @block.scalar
            def _(act):
                def front_a(n):
                    if not second:
                        act.wait_ge(att_T, n + 1)
                        act.wait_ge(added_mm, n)
                        act.copy(attT[:, :], psF).then_inc(attT_ready, 1)

                def front_b(n):
                    act.wait_ge(xn_T, n + 1)
                    act.copy(xnT[:, :], psT).then_inc(xnT_ready, 1)

                def tail(n):
                    act.wait_ge(xe_T, n + 1)
                    act.copy(g.xnT[:, ds(n * CH, CH)], psT).then_inc(xeT_ready, 1)

                def front(n, i):
                    front_a(n)
                    front_b(n)

                def body(n, i, first, ahead):
                    for j in range(NH):
                        act.wait_ge(gate_mm, n * NH + (j + 1))
                        if not (first and j < 2):
                            act.wait_ge(h_ready, n * NH + (j - 1 if j else 0))
                        act.activation(gate[:, j % 2, :], psG[j % 2], ACT.Silu).then_inc(silu_done, 1)
                    if ahead:
                        front_a(n + 1)
                    if not second and not first:
                        tail(n - 1)
                    act.wait_ge(y_mm, n + 1)
                    act.copy(y[:, :], psY).then_inc(y_ready, 1)
                    if ahead:
                        front_b(n + 1)

                run(act, front, body)
                if not second:
                    tail(NC - 1)

            @block.vector
            def _(dve):
                def stats(n, x, st, m, v, s1, s2, s3):
                    for t in range(TPC):
                        ins = dve.bn_stats(st[:, t, :], x[:, t, :])
                    ins.then_inc(s1, 1)
                    wait_alone(dve, s1, n + 1, g.seen_dve)
                    for t in range(TPC):
                        ins = dve.bn_aggr(m[:, t, :], st[:, t, :])
                    ins.then_inc(s2, 1)
                    dve.wait_ge(s2, n + 1)
                    dve.tensor_scalar_add(v[:, :], m[:, :, 1], EPS).then_inc(s3, 1)

                def norm(dst, x, m, r, done):
                    for t in range(TPC):
                        ins = dve.tensor_scalar(dst[:, t, :], x[:, t, :], m[:, t, 0:1], r[:, t:t + 1], ALU.subtract, ALU.mult)
                    ins.then_inc(done, 1)

                def front_a(n, i):
                    dve.wait_ge(att_T if second else added_mm, n + 1)
                    dve.wait_ge(xb_ready, n + 1)
                    dve.tensor_tensor(xc[i][:, :, :], tiles(psA), xb[:, :, :], ALU.add).then_inc(xc_ready, 1)
                    dve.wait_ge(xc_ready, n + 1)
                    stats(n, xc[i], stat, mv, ve, stats_done, aggr_done, var_ready)

                def front_b(n, i):
                    dve.wait_ge(rstd_ready, n + 1)
                    dve.wait_ge(xn_T, n)
                    norm(xn, xc[i], mv, rstd, xn_ready)

                def tail(n):
                    dve.wait_ge(rstd2_ready, n + 1)
                    dve.wait_ge(xe_T, n)
                    norm(xe, x2, mv2, rstd2, xe_ready)

                def front(n, i):
                    front_a(n, i)
                    front_b(n, i)

                def body(n, i, first, ahead):
                    if not second and not first:
                        tail(n - 1)
                    for j in range(NH):
                        dve.wait_ge(silu_done, n * NH + (j + 1))
                        dve.wait_ge(up_mm, n * NH + (j + 1))
                        if j == 0:
                            dve.wait_ge(y_mm, n)
                        dve.tensor_tensor(h[:, j, :], psU[j % 2], gate[:, j % 2, :], ALU.mult).then_inc(h_ready, 1)
                    if ahead:
                        front_a(n + 1, 1 - i)
                    if ahead:
                        front_b(n + 1, 1 - i)
                    dve.wait_ge(y_T, n + 1)
                    dve.wait_ge(x_kept, 16 * n)
                    if not second and not first:
                        dve.wait_ge(xe_ready, n)
                    dve.tensor_tensor(x2[:, :, :], tiles(psF), xc[i][:, :, :], ALU.add).then_inc(x2_ready, 1)
                    if not second:
                        dve.wait_ge(x2_ready, n + 1)
                        stats(n, x2, stat2, mv2, ve2, stats2_done, aggr2_done, var2_ready)

                run(dve, front, body)
                if not second:
                    tail(NC - 1)

            @block.tensor
            def _(pe):
                def front_a(n, first):
                    pe.wait_ge(att_loaded, 16 * (n + 1))
                    dst = psA if second else psF
                    if not first:
                        pe.wait_ge(x2_ready, n - 1)
                        pe.wait_ge(xc_ready, n)
                    for t in range(TPC):
                        ins = pe.transpose(dst[:, t * P:(t + 1) * P], att[:, t * P:(t + 1) * P], g.identf[:, :])
                    ins.then_inc(att_T, 1)
                    if second:
                        return
                    pe.wait_ge(attT_ready, n + 1)
                    for t in range(TPC):
                        ins = pe.matmul(psA[:, t * P:(t + 1) * P], attT[:, t * P:(t + 1) * P], g.wo_a[:, :], start=True, stop=True)
                    ins.then_inc(added_mm, 1)

                def front_b(n, first):
                    pe.wait_ge(xn_ready, n + 1)
                    if not first:
                        pe.wait_ge(xnT_ready, n)
                        if not second:
                            pe.wait_ge(xeT_ready, n - 1)
                    for t in range(TPC):
                        ins = pe.transpose(psT[:, t * P:(t + 1) * P], xn[:, t, :], g.identf[:, :])
                    ins.then_inc(xn_T, 1)

                def tail(n, last):
                    pe.wait_ge(xe_ready, n + 1)
                    pe.wait_ge(xnT_ready, n + 2 if not last else n + 1)
                    for t in range(TPC):
                        ins = pe.transpose(psT[:, t * P:(t + 1) * P], xe[:, t, :], g.identf[:, :])
                    ins.then_inc(xe_T, 1)

                def front(n, i):
                    front_a(n, True)
                    front_b(n, True)

                def body(n, i, first, ahead):
                    pe.wait_ge(xnT_ready, n + 1)
                    for j in range(NH):
                        if not (first and j < 2):
                            pe.wait_ge(silu_done, n * NH + (j - 1 if j else 0))
                        pe.matmul(psG[j % 2], g.wgT[:, j * P:(j + 1) * P], xnT[:, :], start=True, stop=True).then_inc(gate_mm, 1)
                        if not (first and j < 2):
                            pe.wait_ge(h_ready, n * NH + (j - 1 if j else 0))
                        pe.matmul(psU[j % 2], g.wuT[:, j * P:(j + 1) * P], xnT[:, :], start=True, stop=True).then_inc(up_mm, 1)
                    if ahead:
                        front_a(n + 1, False)
                    pe.wait_ge(h_ready, (n + 1) * NH)
                    pe.wait_ge(y_ready, n)
                    for j in range(NH):
                        ins = pe.matmul(psY, g.wdT[:, j * P:(j + 1) * P], h[:, j, :], start=j == 0, stop=j == NH - 1)
                    ins.then_inc(y_mm, 1)
                    if not second and not first:
                        tail(n - 1, False)
                    if ahead:
                        front_b(n + 1, False)
                    pe.wait_ge(y_ready, n + 1)
                    if second:
                        pe.wait_ge(x2_ready, n)
                    else:
                        pe.wait_ge(attT_ready, n + 2 if ahead else n + 1)
                    for t in range(TPC):
                        ins = pe.transpose(psF[:, t * P:(t + 1) * P], y[:, t * P:(t + 1) * P], g.identf[:, :])
                    ins.then_inc(y_T, 1)

                run(pe, front, body)
                if not second:
                    tail(NC - 1, True)


ORDER = [7, 0, 6, 1, 5, 2, 4, 3]
SLOTS = 4
GROUP = 4
GROUPS = [-(-(qt + 1) // GROUP) for qt in ORDER]
GROUPS_BEFORE = [2 * sum(GROUPS[:t]) for t in range(NQ + 1)]
JOBS = 8
QX, QC, KA, KB, KC = range(5)
PASSES = ((QX, KA), (QX, KB), (QC, KC))


def bias_attention(nc, g, wq, wk, wv, wo):
    with ExitStack() as c:
        sb = lambda name, shape, dt=F32: c.enter_context(nc.sbuf_tensor(name, shape, dt))
        sem = lambda name: g.ctx.enter_context(nc.semaphore(name))
        w3 = sb("w_pair", [P, 3, P])
        wo_p = sb("wo_pair", [P, P])
        nat = sb("pair_parts", [P, 6, T], BF16)
        rest = sb("pair_rest", [P, 2, CH])
        stack = [sb(f"pair_stack{i}", [P, 2, 5, T], BF16) for i in range(2)]
        vT = sb("pair_vT", [P, T])
        v = [sb(f"pair_v{i}", [P, NQ, P]) for i in range(2)]
        band = [sb(f"band{i}", [P, 2, T]) for i in range(2)]
        sc = sb("scores", [P, SLOTS, 2, T])
        pT = [sb(f"probsT{i}", [P, 2, NQ, P]) for i in range(2)]
        oT = [sb(f"pair_oT{i}", [P, T]) for i in range(2)]
        mx = sb("b_max", [P, SLOTS, 2])
        mneg = sb("b_neg_max", [P, SLOTS, 2])
        den = sb("b_den", [P, SLOTS, 2])
        rden = sb("b_rden", [P, SLOTS, 2])

        w_loaded, wo_loaded = sem("b_w_loaded"), sem("b_wo_loaded")
        st_loaded = [sem(f"b_st_loaded{i}") for i in range(2)]
        band_loaded = [sem(f"band_loaded{i}") for i in range(2)]
        band_zeroed, y_zeroed = sem("band_zeroed"), sem("y_zeroed")
        job_mm, job_free = sem("job_mm"), sem("job_free")
        p1_ready, rest_ready, p2_ready, p3_ready, vT_ready = (
            sem("b_p1"), sem("b_rest"), sem("b_p2"), sem("b_p3"), sem("b_vT"))
        s_done, max_done, neg_done, exp_done, rden_done, norm_done = (
            sem("b_scores"), sem("b_max_done"), sem("b_neg_done"), sem("b_exp"), sem("b_rden_done"), sem("b_norm"))
        t_done, pv_done, o_out = sem("b_transposed"), sem("b_pv"), sem("b_o_out")
        t_out = [sem("b_t_out_act"), sem("b_t_out_dve")]
        psS = [g.ps[:, 0:T], g.ps[:, T:2 * T]]
        psT = [g.ps[:, 2 * T:2 * T + CH], g.ps[:, 2 * T + CH:3 * T]]
        psO = g.ps[:, 3 * T:3 * T + CH]
        psJ = g.ps[:, 3 * T + CH:4 * T]
        TILES2 = 2 * NQ
        NG = GROUPS_BEFORE[NQ]

        def jobs_before(i):
            if isinstance(i, int):
                return JOBS if i == 0 else (JOBS + 2) * i + JOBS - 2
            return i * (JOBS + 2) + (JOBS - 2)

        def pv_free(i, t):
            return max(0, NQ * i + t - 1) if isinstance(i, int) else i * NQ + (t - 1)

        def run(eng, body):
            body(0, 0, True, True)
            with eng.Fori(0, (ITERS - 2) // 2) as n:
                for k in range(2):
                    body(n * 2 + (k + 1), (k + 1) % 2, False, True)
            body(ITERS - 1, (ITERS - 1) % 2, False, False)

        with nc.Block() as block:

            @block.sync
            def _(sp):
                def load_w(i):
                    cols = ds((i % PAIRS) * P, P)
                    for k, w in enumerate((wq, wk, wv)):
                        sp.dma_start(w3[:, k, :], w[:, cols]).then_inc(w_loaded, 16)

                def load_wo(i):
                    sp.dma_start(wo_p[:, :], wo[ds((i % PAIRS) * P, P), :]).then_inc(wo_loaded, 16)

                def load_band(i, par):
                    for h in range(2):
                        src = g.lrep_flat[ds(((i % PAIRS) * 2 + h) * (P * LROW) + (P - 1), P * (LROW - 1))].rearrange("(q n) -> q n", n=LROW - 1)
                        sp.dma_start(band[par][:, h, T - 2 * P:T], src[:, 0:2 * P]).then_inc(band_loaded[par], 16)

                def gather(par, q_side):
                    for h in range(2):
                        rows = slice(HD_B * h, HD_B * (h + 1))
                        top, low = stack[par][0:HD_B, h, :, :], stack[par][HD_B:P, h, :, :]
                        if q_side:
                            copies = ((top[:, QX, :], 0, 1), (top[:, QC, :], 0, 1), (low[:, QX:QC + 1, :], 1, 2))
                        else:
                            copies = ((top[:, KA:KC + 1, :], 3, 3), (low[:, KA:KB + 1, :], 3, 2), (low[:, KC, :], 3, 1))
                        for dst, part, n in copies:
                            src = nat[rows, part, :] if n == 1 else nat[rows, part:part + n, :]
                            sp.dma_start(dst, src).then_inc(st_loaded[par], 16)

                def next_pair(i, par, base):
                    sp.wait_ge(p3_ready, i * 4 + 2)
                    gather(par, True)
                    sp.wait_ge(p3_ready, i * 4 + 4)
                    gather(par, False)
                    sp.wait_ge(job_mm, base + 6)

                def body(i, par, first, ahead):
                    if not ahead:
                        return
                    if not first:
                        sp.wait_ge(max_done, i * TILES2)
                        sp.wait_ge(s_done, i * TILES2)
                    load_band(i + 1, 1 - par)
                    next_pair(i + 1, 1 - par, jobs_before(i))
                    load_w(i + 2)
                    if not first:
                        sp.wait_ge(job_mm, jobs_before(i) + JOBS + 2)
                        load_wo(i)

                load_w(0)
                sp.wait_ge(band_zeroed, 2)
                load_band(0, 0)
                load_wo(0)
                next_pair(0, 0, 0)
                load_w(1)
                run(sp, body)
                sp.wait_ge(job_mm, jobs_before(ITERS - 1) + 2)
                load_wo(ITERS - 1)
                sp.wait_ge(w_loaded, 48 * (ITERS + 1))
                sp.wait_ge(wo_loaded, 16 * ITERS)
                for par in range(2):
                    sp.wait_ge(band_loaded[par], 32 * ITERS // 2)

            @block.gpsimd
            def _(pool):
                def third(i, k):
                    pool.wait_ge(p2_ready, i * 4 + (k + 1))
                    x, half = k // 2, k % 2
                    pool.tensor_tensor(nat[:, 3 * x + 2, half * CH:(half + 1) * CH], rest[:, half, :],
                                       nat[:, 3 * x + 1, half * CH:(half + 1) * CH], ALU.subtract).then_inc(p3_ready, 1)

                def divide(n, t):
                    w = (ORDER[t % NQ] + 1) * P
                    for h in range(2):
                        wait_alone(pool, rden_done, n + (h + 1), g.seen_pool)
                        p = sc[:, t % SLOTS, h, 0:w]
                        pool.tensor_scalar(p, p, rden[:, t % SLOTS, h:h + 1], 1.0, ALU.mult, ALU.mult).then_inc(norm_done, 1)

                def body(i, par, first, ahead):
                    for t in range(NQ):
                        if t + 1 < NQ or ahead:
                            divide(i * TILES2 + 2 * (t + 1), t + 1)
                        if ahead and t < 2:
                            third(i + 1, 2 * t)
                            third(i + 1, 2 * t + 1)

                for par in range(2):
                    pool.memset(band[par][:, :, :], 0.0).then_inc(band_zeroed, 1)
                for k in range(4):
                    third(0, k)
                divide(0, 0)
                run(pool, body)

            @block.scalar
            def _(act):
                def job_out(i, k, base):
                    act.wait_ge(job_mm, base + (k + 1))
                    half = slice((k % 2) * CH, (k % 2 + 1) * CH)
                    if k < 4:
                        if k == 0:
                            if not (isinstance(i, int) and i == 0):
                                act.wait_ge(st_loaded[0], gathered(0, i))
                                act.wait_ge(st_loaded[1], gathered(1, i))
                        act.copy(nat[:, 3 * (k // 2), half], psJ).then_inc(p1_ready, 1)
                    elif k < 6:
                        act.copy(vT[:, half], psJ).then_inc(job_free, 1)

                def gathered(par, i):
                    if par == 0:
                        return ((i + 1) // 2) * (12 * 16)
                    return (i // 2) * (12 * 16)

                def exponent(n, t, h):
                    w = (ORDER[t % NQ] + 1) * P
                    act.wait_ge(neg_done, n + 1)
                    p = sc[:, t % SLOTS, h, 0:w]
                    act.activation(p, p, ACT.Exp, bias=mneg[:, t % SLOTS, h:h + 1], scale=1.0 / HD_B,
                                   accum_out=den[:, t % SLOTS, h:h + 1]).then_inc(exp_done, 1)

                def evac(i, t, h, mine=0):
                    g0 = GROUPS_BEFORE[t] + h * GROUPS[t]
                    for q in range(GROUPS[t]):
                        if (g0 + q) % 2 != mine:
                            continue
                        nb = min(GROUP, ORDER[t] + 1 - q * GROUP)
                        act.wait_ge(t_done, i * NG + (g0 + q + 1))
                        act.wait_ge(pv_done, pv_free(i, t))
                        act.copy(pT[t % 2][:, h, q * GROUP:q * GROUP + nb, :].rearrange("p n q -> p (n q)"),
                                 psT[(g0 + q) % 2][:, 0:nb * P]).then_inc(t_out[mine], 1)

                def body(i, par, first, ahead):
                    base = jobs_before(i)
                    for t in range(NQ):
                        ks = (2 * t, 2 * t + 1) if ahead and t < 3 else (None, None)
                        if ks[0] is not None:
                            job_out(i + 1, ks[0], base)
                        evac(i, t, 0)
                        if t + 2 < NQ or ahead:
                            exponent(i * TILES2 + 2 * (t + 2), t + 2, 0)
                        if ks[1] is not None:
                            job_out(i + 1, ks[1], base)
                        evac(i, t, 1)
                        if t + 2 < NQ or ahead:
                            exponent(i * TILES2 + (2 * (t + 2) + 1), t + 2, 1)

                for k in range(6):
                    job_out(0, k, 0)
                for t in range(2):
                    for h in range(2):
                        exponent(2 * t + h, t, h)
                run(act, body)

            @block.vector
            def _(dve):
                def job_out(i, k, base, q4):
                    half = slice((k % 2) * CH, (k % 2 + 1) * CH)
                    x = k // 2
                    if k < 4:
                        n = i * 4 + k
                        dve.wait_ge(p1_ready, n + 1)
                        dve.wait_ge(p3_ready, max(0, n - 1) if isinstance(n, int) else n - 1)
                        dve.tensor_tensor(rest[:, k % 2, :], psJ, nat[:, 3 * x, half], ALU.subtract).then_inc(job_free, 1)
                        dve.wait_ge(job_free, base + (k + 1))
                        dve.tensor_copy(nat[:, 3 * x + 1, half], rest[:, k % 2, :]).then_inc(p2_ready, 1)
                    elif k >= 6 and k < JOBS:
                        dve.wait_ge(job_mm, base + (k + 1))
                        dve.tensor_copy(q4[:, (k - 6) * TPC:(k - 5) * TPC, :].rearrange("p n d -> p (n d)"), psJ).then_inc(job_free, 1)

                def y_out(i, half, count):
                    dve.wait_ge(job_mm, count)
                    y = g.yT[:, ds((i // PAIRS) * T + half * CH, CH)]
                    dve.tensor_tensor(y, psJ, y, ALU.add).then_inc(job_free, 1)

                def maximum(n, t, h, par):
                    w = (ORDER[t % NQ] + 1) * P
                    slot = t % SLOTS
                    wait_alone(dve, s_done, n + 1, g.seen_dve)
                    dve.tensor_tensor_reduce(out=sc[:, slot, h, 0:w], in0=psS[h][:, 0:w], in1=band[par][:, h, T - w:T],
                                             scale=1.0, scalar=LOW, op0=ALU.add, op1=ALU.max,
                                             accum_out=mx[:, slot, h:h + 1]).then_inc(max_done, 1)
                    dve.wait_ge(max_done, n + 1)
                    dve.tensor_scalar(mneg[:, slot, h:h + 1], mx[:, slot, h:h + 1], -1.0 / HD_B, None, ALU.mult).then_inc(neg_done, 1)

                def reciprocal(n, t, h):
                    dve.wait_ge(exp_done, n + 1)
                    dve.reciprocal(rden[:, t % SLOTS, h:h + 1], den[:, t % SLOTS, h:h + 1]).then_inc(rden_done, 1)

                def evac(i, t, h, mine=1):
                    g0 = GROUPS_BEFORE[t] + h * GROUPS[t]
                    for q in range(GROUPS[t]):
                        if (g0 + q) % 2 != mine:
                            continue
                        nb = min(GROUP, ORDER[t] + 1 - q * GROUP)
                        dve.wait_ge(t_done, i * NG + (g0 + q + 1))
                        dve.wait_ge(pv_done, pv_free(i, t))
                        dve.tensor_copy(pT[t % 2][:, h, q * GROUP:q * GROUP + nb, :].rearrange("p n q -> p (n q)"),
                                        psT[(g0 + q) % 2][:, 0:nb * P]).then_inc(t_out[mine], 1)

                def o_evac(n, t, par):
                    dve.wait_ge(pv_done, n + 1)
                    qt = ORDER[t]
                    dve.tensor_copy(oT[par][:, qt * P:(qt + 1) * P], psO[:, (t % GROUP) * P:(t % GROUP + 1) * P]).then_inc(o_out, 1)

                def body(i, par, first, ahead):
                    base = jobs_before(i)
                    for t in range(NQ):
                        after = t + 2 < NQ or ahead
                        band_par = par if t + 2 < NQ else 1 - par
                        if t + 1 < NQ or ahead:
                            for h in range(2):
                                reciprocal(i * TILES2 + (2 * (t + 1) + h), t + 1, h)
                        if ahead and t + 2 == NQ:
                            dve.wait_ge(band_loaded[1 - par], bands(i + 1))
                        for h in range(2):
                            if ahead and t < 4:
                                job_out(i + 1, 2 * t + h, base, v[1 - par])
                            if ahead and not first and t == 4:
                                y_out(i - 1, h, base + (JOBS + h + 1))
                            if not ahead and t == 1:
                                y_out(i - 1, h, base + (h + 1))
                            if after:
                                maximum(i * TILES2 + (2 * (t + 2) + h), t + 2, h, band_par)
                            evac(i, t, h)
                        if t > 0:
                            o_evac(i * NQ + (t - 1), t - 1, par)
                        elif not first:
                            o_evac(i * NQ - 1, NQ - 1, 1 - par)

                def bands(i):
                    return (i // 2 + 1) * 32

                dve.memset(g.yT[:, :], 0.0).then_inc(y_zeroed, 1)
                for k in range(JOBS):
                    job_out(0, k, 0, v[0])
                dve.wait_ge(band_zeroed, 2)
                dve.wait_ge(band_loaded[0], 32)
                dve.wait_ge(y_zeroed, 1)
                for t in range(2):
                    for h in range(2):
                        maximum(2 * t + h, t, h, 0)
                for h in range(2):
                    reciprocal(h, 0, h)
                run(dve, body)
                o_evac(ITERS * NQ - 1, NQ - 1, (ITERS - 1) % 2)
                for h in range(2):
                    y_out(ITERS - 1, h, jobs_before(ITERS - 1) + 2 + h + 1)

            @block.tensor
            def _(pe):
                def job(i, k, base):
                    if k == 0:
                        pe.wait_ge(w_loaded, (i + 1) * 48)
                    if not (isinstance(i, int) and i == 0 and k == 0):
                        pe.wait_ge(job_free, base + k)
                    if k < 6:
                        x = g.xnT[:, ds((i // PAIRS) * T + (k % 2) * CH, CH)]
                        ins = pe.matmul(psJ, w3[:, k // 2, :], x, start=True, stop=True)
                    else:
                        for n in range(TPC):
                            at = (k - 6) * CH + n * P
                            ins = pe.transpose(psJ[:, n * P:(n + 1) * P], vT[:, at:at + P], g.identf[:, :])
                    ins.then_inc(job_mm, 1)

                def out_job(i, par, half, count):
                    if half == 0:
                        pe.wait_ge(wo_loaded, (i + 1) * 16)
                        pe.wait_ge(o_out, (i + 1) * NQ)
                    pe.wait_ge(job_free, count)
                    pe.matmul(psJ, wo_p[:, :], oT[par][:, half * CH:(half + 1) * CH], start=True, stop=True).then_inc(job_mm, 1)

                def scores(n, t, h, par, opening):
                    qt = ORDER[t % NQ]
                    w = (qt + 1) * P
                    if not opening:
                        pe.wait_ge(max_done, n - 1)
                    for lo in range(0, w, CH):
                        hi = min(w, lo + CH)
                        for p, (q, k) in enumerate(PASSES):
                            ins = pe.matmul(psS[h][:, lo:hi], stack[par][:, h, q, qt * P:(qt + 1) * P], stack[par][:, h, k, lo:hi],
                                            start=p == 0, stop=p == len(PASSES) - 1)
                    ins.then_inc(s_done, 1)

                def transposed(i, t, h, first):
                    pe.wait_ge(norm_done, i * TILES2 + (2 * t + h + 1))
                    for q in range(GROUPS[t]):
                        n = GROUPS_BEFORE[t] + h * GROUPS[t] + q
                        if not (first and n < 2):
                            pe.wait_ge(t_out[n % 2], i * (NG // 2) + n // 2)
                        for b in range(q * GROUP, min(ORDER[t] + 1, (q + 1) * GROUP)):
                            ins = pe.transpose(psT[n % 2][:, (b % GROUP) * P:(b % GROUP + 1) * P], sc[:, t % SLOTS, h, b * P:(b + 1) * P], g.identf[:, :])
                        ins.then_inc(t_done, 1)

                def product(i, t, par, first):
                    done = GROUPS_BEFORE[t + 1]
                    pe.wait_ge(t_out[0], i * (NG // 2) + (done + 1) // 2)
                    pe.wait_ge(t_out[1], i * (NG // 2) + done // 2)
                    if not (first and t == 0):
                        pe.wait_ge(o_out, i * NQ + t)
                    at = (t % GROUP) * P
                    for b in range(ORDER[t] + 1):
                        for h in range(2):
                            ins = pe.matmul(psO[h * HD_B:(h + 1) * HD_B, at:at + P], v[par][:, b, h * HD_B:(h + 1) * HD_B], pT[t % 2][:, h, b, :],
                                            start=b == 0, stop=b == ORDER[t])
                    ins.then_inc(pv_done, 1)

                def body(i, par, first, ahead):
                    base = jobs_before(i)
                    for t in range(NQ):
                        if ahead and t + 2 == NQ:
                            pe.wait_ge(st_loaded[1 - par], stacks(i + 1))
                        for h in range(2):
                            if t + 2 < NQ or ahead:
                                scores(i * TILES2 + (2 * (t + 2) + h), t + 2, h, par if t + 2 < NQ else 1 - par, False)
                            if ahead and t < 4:
                                job(i + 1, 2 * t + h, base)
                            if ahead and not first and t == 4:
                                out_job(i - 1, 1 - par, h, base + (JOBS + h))
                            if not ahead and t == 1:
                                out_job(i - 1, 1 - par, h, base + h)
                            transposed(i, t, h, first)
                        if t > 0:
                            product(i, t - 1, par, first)
                        elif not first:
                            product(i - 1, NQ - 1, 1 - par, False)

                def stacks(i):
                    return (i // 2 + 1) * (12 * 16)

                for k in range(JOBS):
                    job(0, k, 0)
                pe.wait_ge(st_loaded[0], 12 * 16)
                for t in range(2):
                    for h in range(2):
                        scores(2 * t + h, t, h, 0, t == 0)
                run(pe, body)
                product(ITERS - 1, NQ - 1, (ITERS - 1) % 2, False)
                for h in range(2):
                    out_job(ITERS - 1, (ITERS - 1) % 2, h, jobs_before(ITERS - 1) + 2 + h)


def build(nc, x, wqkv, wo_a, bo_a, wq, wk, wv, wo_b, bo_b, rel, w_gate, w_up, w_down, out):
    with ExitStack() as ctx:
        class g:
            pass
        g.ctx = ctx
        g.seen_dve = ctx.enter_context(nc.semaphore("seen_dve"))
        g.seen_pool = ctx.enter_context(nc.semaphore("seen_pool"))
        g.consts = ctx.enter_context(nc.semaphore("consts"))
        sb = lambda name, shape, dt=F32: ctx.enter_context(nc.sbuf_tensor(name, shape, dt))
        g.ps = ctx.enter_context(nc.psum_tensor("ps", [P, 8 * CH], F32))
        g.X = sb("x_stream", [P, NT, P])
        g.identf = sb("identf", [P, P])
        g.identb = sb("identb", [P, P], BF16)
        g.expo = sb("minus_half", [P, TPC])
        g.wgT = sb("w_gateT", [P, HID])
        g.wuT = sb("w_upT", [P, HID])
        g.wdT = sb("w_downT", [P, HID])
        g.wo_a = sb("wo_a", [P, P])
        g.bo_a = sb("bo_a", [P, P])
        g.bo_b = sb("bo_b", [P, P])
        g.qs = nc.dram_tensor("qk_parts_dram", (3, 2, P, B * T), BF16, kind="Internal").ap()
        lrep = nc.dram_tensor("bias_rows_dram", (HEADS * P * LROW + P,), F32, kind="Internal").ap()
        g.lrep = lrep[0:HEADS * P * LROW].rearrange("(h q n) -> h q n", h=HEADS, q=P)
        g.lrep_flat = lrep
        tables = nc.inline_tensor(rope_tables(), "rope_tables").ap()
        g.yT = sb("att_bT", [P, B * T])
        with ExitStack() as c1:
            g.xnT = c1.enter_context(nc.sbuf_tensor("x_normT", [P, B * T], F32))
            with ExitStack() as c2:
                g.O = c2.enter_context(nc.sbuf_tensor("att_a", [P, NT * D], F32))
                with ExitStack() as c3:
                    sb = lambda name, shape, dt=F32: c3.enter_context(nc.sbuf_tensor(name, shape, dt))
                    g.maskq = sb("mask_query_key", [P, CH])
                    g.maskk = sb("mask_key_query", [P, P], BF16)
                    g.zero_one = sb("zero_one", [3, 2, G4, T], BF16)
                    g.V = sb("values_a", [P, UNITS * VU])
                    prepare(nc, g, x, wqkv, rel, w_gate, w_up, w_down, wo_a, bo_a, bo_b, tables)
                    rope_attention(nc, g)
                ffn(nc, g, False, out)
            bias_attention(nc, g, wq, wk, wv, wo_b)
        ffn(nc, g, True, out)


_NAMES = ["L0_attn_a_x", "L0_attn_a_Wqkv", "L0_attn_a_Wo", "L0_attn_a_bo", "L0_attn_b_Wq", "L0_attn_b_Wk", "L0_attn_b_Wv",
          "L0_attn_b_Wo", "L0_attn_b_bo", "L0_attn_b_rel_pos_bias", "L0_ffn_w_gate", "L0_ffn_w_up", "L0_ffn_w_down"]


def kernel(**inputs):
    import concourse.bacc as bacc
    from concourse.bass_utils import run_bass_kernel_spmd

    nc = bacc.Bacc("TRN2", target_bir_lowering=False, num_devices=1)
    arrays, args = {}, []
    for name in _NAMES:
        a = np.ascontiguousarray(inputs[name])
        arrays[name] = a
        args.append(nc.dram_tensor(name, a.shape, mybir.dt.from_np(a.dtype), kind="ExternalInput").ap())
    out = nc.dram_tensor("out", (B, T, D), F32, kind="ExternalOutput").ap()
    build(nc, *args, out)
    r = run_bass_kernel_spmd(nc, [arrays], core_ids=[0])
    return r.results[0]["out"]
```

```python
import numpy as np
import concourse.bass as bass
from concourse import mybir
from concourse.alu_op_type import AluOpType as ALU
from contextlib import ExitStack

F32 = mybir.dt.float32
BF16 = mybir.dt.bfloat16
I32 = mybir.dt.int32
ACT = mybir.ActivationFunctionType
AX = mybir.AxisListType
ds = bass.ds

P = 128
B, T, D = 4, 1024, 128
NT = B * T // P
CH = 512
NC = B * T // CH
TPC = CH // P
NQ = T // P
HEADS = 16
HD_A = D // HEADS
HD_B = 64
HID = 384
NH = HID // P
EPS = 1e-5
W_SCALE = float(np.float32(1.0 / 127.0))
LOW = -3.0e38
RANGE = 128
LROW = 3 * RANGE

G4 = 4
UNITS = B * HEADS // G4
NPROD = 9
ROW_M = NPROD * HD_A
ROWS = 96
VW = HD_A + 1
VU = NQ * G4 * VW

PAIRS = HEADS // 2
ITERS = B * PAIRS


def tok_tiles(x):
    return x.rearrange("b (n p) d -> p (b n) d", p=P)


def rope_tables():
    half = HD_A // 2
    inv = (np.float32(1.0) / np.power(np.float32(10000.0), np.arange(half, dtype=np.float32) / np.float32(half))).astype(np.float32)
    ang = (np.arange(T, dtype=np.float32)[:, None] * inv[None, :]).astype(np.float32)
    both = np.stack([np.cos(ang.astype(np.float64)), np.sin(ang.astype(np.float64))])
    return np.ascontiguousarray(np.repeat(both, 2, axis=-1).transpose(0, 2, 1)).astype(np.float32)


def wait_alone(eng, sem, value, seen):
    eng.wait_ge(sem, value)
    eng.sem_inc(seen, 1)


def load_stack(sp, g, u, i):
    rows = (u // 4) * T
    for qp in range(3):
        src = g.qs[qp, 0, ds((u % 4) * (G4 * HD_A), G4 * HD_A), ds(rows, T)].rearrange("(h d) t -> d h t", d=HD_A)
        for kp in range(3):
            r = (qp * 3 + kp) * HD_A
            sp.dma_start(g.stack[i][r:r + HD_A, 0, :, :], src).then_inc(g.st_loaded[i], 16)
    for kp in range(3):
        src = g.qs[kp, 1, ds((u % 4) * (G4 * HD_A), G4 * HD_A), ds(rows, T)].rearrange("(h d) t -> d h t", d=HD_A)
        for qp in range(3):
            r = (qp * 3 + kp) * HD_A
            sp.dma_start(g.stack[i][r:r + HD_A, 1, :, :], src).then_inc(g.st_loaded[i], 16)
    sp.dma_start(g.stack[i][ROW_M:ROW_M + 3, 0, :, :], g.zero_one[:, 0, :, :]).then_inc(g.st_loaded[i], 16)


def prepare(nc, g, x, wqkv, rel, w_gate, w_up, w_down, wo_a, bo_a, bo_b, tables):
    with ExitStack() as c:
        sb = lambda name, shape, dt=F32: c.enter_context(nc.sbuf_tensor(name, shape, dt))
        sem = lambda name: g.ctx.enter_context(nc.semaphore(name))
        w3 = sb("w_qkv", [P, 3, P])
        wrot = sb("w_rot", [P, 2, P])
        cos, sin = g.O[:, 0:T], g.O[:, T:2 * T]
        wi = sb("w_int", [P, 3, HID], I32)
        wf = sb("w_float", [P, 3, HID])
        relrow = sb("rel_rows", [HEADS, RANGE])
        lrow = sb("bias_rows", [HEADS, LROW])
        stat = sb("stat", [P, TPC, 6])
        mv = sb("mean_var", [P, TPC, 2])
        ve = sb("var_eps", [P, TPC])
        rstd = sb("rstd", [P, TPC])
        xn = sb("xn", [P, TPC, P])
        xnT = [sb(f"xnT{i}", [P, CH]) for i in range(2)]
        tc = sb("times_cos", [P, 2, CH])
        tsn = sb("times_sin", [P, 2, CH])
        qk = sb("qk_roped", [P, 2, CH])
        rest = sb("qk_rest", [P, 2, CH])
        parts = [sb(f"qk_parts{i}", [P, 3, 2, CH], BF16) for i in range(2)]

        x_loaded = [sem(f"x_loaded{i}") for i in range(3)]
        w_loaded, tab_loaded = sem("w_loaded"), sem("tab_loaded")
        int_loaded, rel_loaded, later_loaded = sem("int_loaded"), sem("rel_loaded"), sem("later_loaded")
        zeroed, consts, ones_set = sem("zeroed"), g.consts, sem("ones_set")
        rot_ready, wf_ready, ffn_T, ffn_stored = sem("rot_ready"), sem("wf_ready"), sem("ffn_T"), sem("ffn_stored")
        lrow_ready, lrow_stored = sem("lrow_ready"), sem("lrow_stored")
        stats_done, aggr_done, var_ready, rstd_ready = sem("stats_done"), sem("aggr_done"), sem("var_ready"), sem("rstd_ready")
        xn_ready, xn_T, xnT_ready = sem("xn_ready"), sem("xn_T"), sem("xnT_ready")
        qk_mm, v_mm, v_stored = sem("qk_mm"), sem("v_mm"), sem("v_stored")
        rope_read, q_ready, p1_ready, rest_ready, p2_ready, split_done = (
            sem("rope_read"), sem("q_ready"), sem("p1_ready"), sem("rest_ready"), sem("p2_ready"), sem("split_done"))
        parts_stored = [sem(f"parts_stored{i}") for i in range(2)]
        psT = g.ps[:, 0:CH]
        psV = g.ps[:, CH:2 * CH]
        psQ = [g.ps[:, (2 + j) * CH:(3 + j) * CH] for j in range(4)]
        psW = g.ps[:, 6 * CH:8 * CH]

        def run(eng, body, between=lambda n: None):
            for n in range(2):
                body(n, n % 2)
                between(n)
            with eng.Fori(0, (NC - 4) // 2) as m:
                for k in range(2):
                    body(m * 2 + (k + 2), k % 2)
            body(NC - 2, 0)
            body(NC - 1, 1)

        def known(n, least):
            return isinstance(n, int) and n < least

        def is_last(n):
            return isinstance(n, int) and n == NC - 1

        with nc.Block() as block:

            @block.sync
            def _(sp):
                for n in range(2):
                    sp.dma_start(g.X[:, n * TPC:(n + 1) * TPC, :], tok_tiles(x)[:, n * TPC:(n + 1) * TPC, :]).then_inc(x_loaded[n], 16)
                for b in range(1, B):
                    sp.dma_start(g.X[:, b * NQ:(b + 1) * NQ, :], tok_tiles(x)[:, b * NQ:(b + 1) * NQ, :]).then_inc(x_loaded[2], 16)
                for n, w in enumerate((w_gate, w_up)):
                    sp.dma_start(wi[:, n, :].rearrange("p (t d) -> p t d", t=NH), w.rearrange("(t p) d -> p t d", p=P)).then_inc(int_loaded, 16)
                sp.dma_start(wi[:, 2, :], w_down).then_inc(int_loaded, 16)
                sp.dma_start(relrow[:, :], rel).then_inc(rel_loaded, 16)
                sp.dma_start(g.wo_a[:, :], wo_a).then_inc(later_loaded, 16)
                for dst, src in ((g.bo_a, bo_a), (g.bo_b, bo_b)):
                    sp.dma_start(dst[:, :], bass.AP(src.tensor, src.offset, [[0, P], [1, P]])).then_inc(later_loaded, 16)

                def store(n, par):
                    sp.wait_ge(split_done, n + 1)
                    sp.dma_start(g.qs.rearrange("s k p t -> p (s k) t")[:, :, ds(n * CH, CH)],
                                 parts[par][:, :, :, :].rearrange("p s k t -> p (s k) t")).then_inc(parts_stored[par], 16)

                def between(n):
                    if n == 0:
                        sp.wait_ge(lrow_ready, 3)
                        sp.dma_start(g.lrep, lrow[:, :].unsqueeze(1).broadcast_to([HEADS, P, LROW])).then_inc(lrow_stored, 16)
                    else:
                        for par in range(2):
                            sp.wait_ge(parts_stored[par], 16)
                        sp.wait_ge(g.st_zeroed, 3)
                        sp.wait_ge(g.zero_one_set, 2)
                        for i in range(3):
                            sp.dma_start(g.stack[i][ROW_M:ROW_M + 3, 1, :, :], g.zero_one[:, 1, :, :]).then_inc(g.ones_in, 16)
                        load_stack(sp, g, 0, 0)

                run(sp, store, between)
                for par in range(2):
                    sp.wait_ge(parts_stored[par], 16 * NC // 2)
                sp.wait_ge(lrow_stored, 16)
                sp.wait_ge(later_loaded, 48)

            @block.gpsimd
            def _(pool):
                pool.memset(g.identf[:, :], 0.0).then_inc(zeroed, 1)
                pool.memset(g.expo[:, :], -0.5).then_inc(zeroed, 1)
                pool.wait_ge(zeroed, 2)
                pool.affine_select(out=g.identf[:, :], in_=g.identf[:, :], compare_op=ALU.not_equal, fill=1.0, base=0,
                                   pattern=[[-1, P]], channel_multiplier=1).then_inc(consts, 1)

                def rstd_of(n):
                    pool.wait_ge(var_ready, n + 1)
                    pool.tensor_tensor(rstd[:, :], ve[:, :], g.expo[:, :], ALU.pow).then_inc(rstd_ready, 1)

                def rope_sum(n):
                    for k in range(2):
                        pool.wait_ge(rope_read, n * 4 + (2 * k + 2))
                        if not known(n, 1):
                            pool.wait_ge(rest_ready, n)
                        pool.tensor_tensor(qk[:, k, :], tc[:, k, :], tsn[:, k, :], ALU.add).then_inc(q_ready, 1)

                def third(n, par):
                    pool.wait_ge(p2_ready, n + 1)
                    pool.tensor_tensor(parts[par][:, 2, :, :], rest[:, :, :], parts[par][:, 1, :, :], ALU.subtract).then_inc(split_done, 1)

                def body(n, par):
                    if not is_last(n):
                        rstd_of(n + 1)
                    if not known(n, 1):
                        third(n - 1, 1 - par)
                    rope_sum(n)

                rstd_of(0)
                pool.memset(g.V[:, :], 1.0).then_inc(ones_set, 1)

                def between(n):
                    if n == 1:
                        return
                    pool.memset(g.identb[:, :], 0.0).then_inc(zeroed, 1)
                    pool.memset(g.maskq[:, :], 0.0).then_inc(zeroed, 1)
                    pool.wait_ge(zeroed, 4)
                    pool.affine_select(out=g.identb[:, :], in_=g.identb[:, :], compare_op=ALU.not_equal, fill=1.0, base=0,
                                       pattern=[[-1, P]], channel_multiplier=1).then_inc(consts, 1)
                    pool.affine_select(out=g.maskq[:, :], in_=g.maskq[:, :], compare_op=ALU.is_ge, fill=LOW, base=0,
                                       pattern=[[0, TPC], [-1, P]], channel_multiplier=1).then_inc(consts, 1)
                    pool.wait_ge(consts, 3)
                    for k in range(2):
                        pool.memset(g.zero_one[:, k, :, :], float(k)).then_inc(g.zero_one_set, 1)
                    pool.wait_ge(g.zero_one_set, 2)
                    for i in range(3):
                        pool.memset(g.stack[i][64:ROWS, :, :, :].rearrange("p a h t -> p (a h t)").bitcast(F32), 0.0).then_inc(g.st_zeroed, 1)
                    pool.wait_ge(g.st_zeroed, 3)

                run(pool, body, between)
                third(NC - 1, 1)

            @block.scalar
            def _(act):
                act.dma_start(w3[:, :, :].rearrange("p k m -> p (k m)"), wqkv).then_inc(w_loaded, 16)
                for dst, k in ((cos, 0), (sin, 1)):
                    act.dma_start(dst, tables[k, :, :].unsqueeze(0).broadcast_to([HEADS, HD_A, T])).then_inc(tab_loaded, 16)
                act.wait_ge(w_loaded, 16)
                pairs = w3[:, 0:2, :].rearrange("p k (m two) -> p k m two", two=2)
                rot = wrot[:, :, :].rearrange("p k (m two) -> p k m two", two=2)
                act.mul(rot[:, :, :, 0], pairs[:, :, :, 1], -1.0)
                act.copy(rot[:, :, :, 1], pairs[:, :, :, 0]).then_inc(rot_ready, 1)

                def normal_T(n, par):
                    act.wait_ge(xn_T, n + 1)
                    if not known(n, 2):
                        act.wait_ge(v_mm, n - 1)
                    act.copy(xnT[par][:, :], psT).then_inc(xnT_ready, 1)

                def values(n):
                    act.wait_ge(v_mm, n + 1)
                    vb = g.V[:, ds((n // 2) * (4 * VU) + (n % 2) * (TPC * G4 * VW), 3 * VU + TPC * G4 * VW)]
                    for u in range(4):
                        dst = vb[:, u * VU:u * VU + TPC * G4 * VW].rearrange("p (t j w) -> p t j w", t=TPC, j=G4)[:, :, :, 0:HD_A]
                        src = psV.rearrange("p (t u j d) -> p t u j d", t=TPC, u=4, j=G4)[:, :, u, :, :]
                        ins = act.copy(dst, src)
                    ins.then_inc(v_stored, 1)

                def first(n, par, k):
                    act.wait_ge(q_ready, n * 2 + (k + 1))
                    if not known(n, 2):
                        act.wait_ge(parts_stored[par], (n // 2) * 16)
                    act.copy(parts[par][:, 0, k, :], qk[:, k, :]).then_inc(p1_ready, 1)

                def second(n, par):
                    act.wait_ge(rest_ready, n + 1)
                    act.copy(parts[par][:, 1, :, :], rest[:, :, :]).then_inc(p2_ready, 1)

                def body(n, par):
                    if not known(n, 1):
                        second(n - 1, 1 - par)
                    values(n)
                    first(n, par, 0)
                    if not is_last(n):
                        normal_T(n + 1, 1 - par)
                    first(n, par, 1)

                def between(n):
                    for k, dst in enumerate((g.wgT, g.wuT, g.wdT)):
                        if (k == 2) == (n == 1):
                            act.wait_ge(ffn_T, k + 1)
                            act.copy(dst[:, :], psW[:, (k % 2) * CH:(k % 2) * CH + HID]).then_inc(ffn_stored, 1)

                normal_T(0, 0)
                act.wait_ge(ones_set, 1)
                run(act, body, between)
                second(NC - 1, 1)

            @block.vector
            def _(dve):
                def stats(n):
                    if known(n, 2):
                        dve.wait_ge(x_loaded[n], 16)
                    elif isinstance(n, int) and n == 2:
                        dve.wait_ge(x_loaded[2], 16 * (B - 1))
                    for t in range(TPC):
                        ins = dve.bn_stats(stat[:, t, :], g.X[:, ds(n * TPC + t, 1), :].rearrange("p a d -> p (a d)"))
                    ins.then_inc(stats_done, 1)
                    wait_alone(dve, stats_done, n + 1, g.seen_dve)
                    for t in range(TPC):
                        ins = dve.bn_aggr(mv[:, t, :], stat[:, t, :])
                    ins.then_inc(aggr_done, 1)
                    dve.wait_ge(aggr_done, n + 1)
                    dve.tensor_scalar_add(ve[:, :], mv[:, :, 1], EPS).then_inc(var_ready, 1)

                def norm(n):
                    dve.wait_ge(rstd_ready, n + 1)
                    if not known(n, 1):
                        dve.wait_ge(xn_T, n)
                    for t in range(TPC):
                        ins = dve.tensor_scalar(xn[:, t, :], g.X[:, ds(n * TPC + t, 1), :].rearrange("p a d -> p (a d)"),
                                                mv[:, t, 0:1], rstd[:, t:t + 1], ALU.subtract, ALU.mult)
                    ins.then_inc(xn_ready, 1)

                def rope(n):
                    for j in range(4):
                        dve.wait_ge(qk_mm, n * 4 + (j + 1))
                        if not known(n, 1):
                            dve.wait_ge(q_ready, n * 2 + (j // 2 - 1))
                        dst, table = ((tc, cos), (tsn, sin))[j % 2]
                        dve.tensor_tensor(dst[:, j // 2, :], psQ[j], table[:, ds((n % 2) * CH, CH)], ALU.mult).then_inc(rope_read, 1)

                def split(n, par):
                    dve.wait_ge(p1_ready, n * 2 + 2)
                    if not known(n, 1):
                        dve.wait_ge(split_done, n)
                    dve.tensor_tensor(rest[:, :, :], qk[:, :, :], parts[par][:, 0, :, :], ALU.subtract).then_inc(rest_ready, 1)

                def body(n, par):
                    if not is_last(n):
                        stats(n + 1)
                    if not known(n, 1):
                        split(n - 1, 1 - par)
                    rope(n)
                    if not is_last(n):
                        norm(n + 1)

                def between(n):
                    if n == 1:
                        return
                    dve.wait_ge(rel_loaded, 16)
                    dve.memset(lrow[:, 0:RANGE], 0.0).then_inc(lrow_ready, 1)
                    dve.tensor_scalar(lrow[:, RANGE:2 * RANGE], relrow[:, :], relrow[:, 0:1], None, ALU.subtract).then_inc(lrow_ready, 1)
                    dve.memset(lrow[:, 2 * RANGE:LROW], LOW).then_inc(lrow_ready, 1)

                stats(0)
                norm(0)
                dve.wait_ge(int_loaded, 48)
                dve.tensor_scalar(wf[:, :, :], wi[:, :, :], W_SCALE, None, ALU.mult).then_inc(wf_ready, 1)
                dve.wait_ge(tab_loaded, 32)
                run(dve, body, between)
                split(NC - 1, 1)

            @block.tensor
            def _(pe):
                def transposed(n):
                    pe.wait_ge(xn_ready, n + 1)
                    if not known(n, 1):
                        pe.wait_ge(xnT_ready, n)
                    for t in range(TPC):
                        ins = pe.transpose(psT[:, t * P:(t + 1) * P], xn[:, t, :], g.identf[:, :])
                    ins.then_inc(xn_T, 1)

                def rotary(n, par):
                    pe.wait_ge(xnT_ready, n + 1)
                    for j in range(4):
                        if not known(n, 1):
                            pe.wait_ge(rope_read, n * 4 + (j - 3))
                        w = (w3, wrot)[j % 2]
                        pe.matmul(psQ[j], w[:, j // 2, :], xnT[par][:, :], start=True, stop=True).then_inc(qk_mm, 1)

                def values(n, par):
                    if not known(n, 1):
                        pe.wait_ge(v_stored, n)
                    for t in range(TPC):
                        ins = pe.matmul(psV[:, t * P:(t + 1) * P], xnT[par][:, t * P:(t + 1) * P], w3[:, 2, :], start=True, stop=True)
                    ins.then_inc(v_mm, 1)

                def body(n, par):
                    rotary(n, par)
                    values(n, par)
                    if not is_last(n):
                        transposed(n + 1)

                def between(n):
                    for k in range(3):
                        if (k == 2) == (n == 1):
                            if k == 2:
                                pe.wait_ge(ffn_stored, 1)
                            for t in range(NH):
                                ins = pe.transpose(psW[:, (k % 2) * CH + t * P:(k % 2) * CH + (t + 1) * P], wf[:, k, t * P:(t + 1) * P], g.identf[:, :])
                            ins.then_inc(ffn_T, 1)

                pe.wait_ge(consts, 1)
                transposed(0)
                pe.wait_ge(rot_ready, 1)
                pe.wait_ge(wf_ready, 1)
                run(pe, body, between)


DIAGONALS = [([(qt, qt, 1, qt % TPC) for qt in range(lo, lo + TPC)], [(0, TPC, 1, 0, lo)]) for lo in (0, TPC)]
BEFORE = [([(1, 0, 1, 0), (3, 0, 3, 1)], [(0, 1, 1, 1, 1), (1, 1, 3, 1, 3)]),
          ([(2, 0, 2, 0), (6, 4, 2, 2)], [(0, 1, 2, 1, 2), (2, 1, 2, 2, 6)]),
          ([(5, 4, 1, 0), (7, 4, 3, 1)], [(0, 1, 1, 2, 5), (1, 1, 3, 2, 7)])]
BEFORE += [([(qt, 0, TPC, 0)], [(0, 1, TPC, 1, qt)]) for qt in range(TPC, NQ)]
FIRST_PASS = DIAGONALS + BEFORE
KINDS = 3
SECOND_PASS = [(qc, kt, max(0, kt * P - qc * CH)) for qc in range(T // CH) for kt in range((qc + 1) * TPC)]
STEPS = len(SECOND_PASS)
DIAG_STEPS = [s for s, (qc, kt, _) in enumerate(SECOND_PASS) if kt >= qc * TPC]
TILES = G4 * len(FIRST_PASS)
RING = 3
assert TILES % RING == 0 and STEPS * G4 % RING == 0
IN_A_STEP = (0, "place", 1, "place", 2, "place", 3, "place", "product")
SLOTS_1 = IN_A_STEP.count("place")


LATER = 8
MAX_T = LATER + 1


def interleave():
    weight = [CH - off + P for _, _, off in SECOND_PASS for _ in range(SLOTS_1)]
    order = list(range(LATER * SLOTS_1, STEPS * SLOTS_1)) + list(range(LATER * SLOTS_1))
    out, at, seen = [None] * len(weight), 0, 0
    for place in order:
        seen += weight[place]
        upto = -(-TILES * seen // sum(weight))
        out[place] = (at, upto)
        at = upto
    return out


PLACES = interleave()
EARLY = PLACES[-1][1]


def rope_attention(nc, g):
    with ExitStack() as c:
        sb = lambda name, shape, dt=F32: c.enter_context(nc.sbuf_tensor(name, shape, dt))
        sem = lambda name: g.ctx.enter_context(nc.semaphore(name))
        stack = g.stack
        vu = [sb(f"v_unit{i}", [P, NQ, G4, VW]) for i in range(3)]
        pt = [sb(f"probs{i}", [P, G4, CH]) for i in range(3)]
        mx = sb("row_max", [P, KINDS, G4, NQ])
        m_all = sb("row_max_joined", [P, G4 * NQ])
        mneg = sb("neg_max_parts", [P, 3, G4 * NQ], BF16)
        mrest = sb("max_rest", [P, G4 * NQ])
        mrow = sb("max_rows", [3 * G4 * NQ, P], BF16)
        oT = sb("oT", [P, CH])
        o_raw = sb("o_raw", [P, TPC, G4, VW])
        rden = sb("rden", [P, TPC, G4])

        st_loaded = g.st_loaded
        p1_done, p1_max = sem("p1_done"), sem("p1_max")
        joined, mneg1, mrest1, mneg2, mneg3, m_T, m_row, m_loaded = (
            sem("max_joined"), sem("mneg1"), sem("mrest1"), sem("mneg2"), sem("mneg3"), sem("m_T"), sem("m_row"), sem("m_loaded"))
        mx_set, diag_zeroed = sem("mx_set"), sem("diag_zeroed")
        v_unit, s2_done, exp_done, pv_done = sem("v_unit"), sem("s2_done"), sem("exp_done"), sem("pv_done")
        o_cleared, o_out, o_T, o_in, o_rden, o_norm = (
            sem("o_cleared"), sem("o_out"), sem("o_T"), sem("o_in"), sem("o_rden"), sem("o_norm"))

        bank = lambda n, k=1: g.ps[:, n * CH:(n + k) * CH]
        psS = [bank(n) for n in range(RING)]
        ps1 = [bank(RING + n) for n in range(RING)]
        psO = bank(6)
        psX = bank(7)
        LOADS = 7 * 16

        def q_side(i):
            return stack[i][:, 0, :, :]

        def k_side(i):
            return stack[i][:, 1, :, :]

        with nc.Block() as block:

            @block.sync
            def _(sp):
                for i in range(1, 3):
                    load_stack(sp, g, i, i)

                def max_rows(u, i):
                    sp.wait_ge(m_row, u + 1)
                    sp.dma_start(q_side(i)[ROW_M:ROW_M + 3, :, :], mrow[:, :]).then_inc(m_loaded, 16)

                def half(u, i, ahead):
                    if ahead:
                        max_rows(u + 1, (i + 1) % 3)
                    sp.wait_ge(s2_done, G4 * STEPS * (u + 1))
                    load_stack(sp, g, (u + 3) % UNITS, i)

                max_rows(0, 0)
                half(0, 0, True)
                with sp.Fori(0, (UNITS - 4) // 3) as v:
                    for k in range(3):
                        half(v * 3 + (k + 1), (k + 1) % 3, True)
                half(UNITS - 3, (UNITS - 3) % 3, True)
                half(UNITS - 2, (UNITS - 2) % 3, True)
                for i in range(3):
                    sp.wait_ge(st_loaded[i], 16 * 19 * len([u for u in range(UNITS + 2) if u % 3 == i]))

            @block.gpsimd
            def _(pool):
                def zero_above(u, first):
                    for n, s in enumerate(DIAG_STEPS):
                        off = SECOND_PASS[s][2]
                        for x in range(2):
                            wait_alone(pool, exp_done, u * (G4 * STEPS) + (G4 * s + 2 * x + 2), g.seen_pool)
                            block_ = pt[s % 3][:, 2 * x:2 * x + 2, off:off + P]
                            pool.affine_select(out=block_, in_=block_, compare_op=ALU.is_ge, fill=0.0, base=0,
                                               pattern=[[0, 2], [1, P]], channel_multiplier=-1).then_inc(diag_zeroed, 1)

                        if n == 3 and not first:
                            normalise(u - 1, u * 2 - 1, 1)
                        if n == 5:
                            normalise(u, u * 2, 0)

                def normalise(u, n, qc):
                    wait_alone(pool, o_rden, n + 1, g.seen_pool)
                    first = (u // 4) * (NQ * D) + (u % 4) * (G4 * HD_A) + qc * (TPC * D)
                    out = g.O[:, ds(first, TPC * D)].rearrange("p (t c) -> p t c", t=TPC)[:, :, 0:G4 * HD_A]
                    pool.tensor_tensor(out.rearrange("p t (j d) -> p t j d", j=G4), o_raw[:, :, :, 0:HD_A],
                                       rden[:, :, :].unsqueeze(3).broadcast_to([P, TPC, G4, HD_A]), ALU.mult).then_inc(o_norm, 1)

                zero_above(0, True)
                with pool.Fori(1, UNITS) as u:
                    zero_above(u, False)
                normalise(UNITS - 1, 2 * UNITS - 1, 1)

            @block.scalar
            def _(act):
                def values(u, i):
                    act.wait_ge(pv_done, STEPS * (u - 2) if not isinstance(u, int) else max(0, STEPS * (u - 2)))
                    act.copy(vu[i][:, :, :, :].rearrange("p t j w -> p (t j w)"), g.V[:, ds(u * VU, VU)]).then_inc(v_unit, 1)

                def o_back(n):
                    act.wait_ge(o_T, n + 1)
                    if not (isinstance(n, int) and n == 0):
                        act.wait_ge(o_norm, n)
                    act.copy(o_raw[:, :, :, :], psX.rearrange("p (t j w) -> p t j w", t=TPC, j=G4)[:, :, :, 0:VW]).then_inc(o_in, 1)

                def o_evac(n, pv):
                    act.wait_ge(pv_done, pv)
                    if not (isinstance(n, int) and n == 0):
                        act.wait_ge(o_T, n)
                    act.copy(oT[:, :], psO).then_inc(o_out, 1)

                def half(u, i, first, ahead):
                    if ahead:
                        values(u + 1, (i + 1) % 3)
                    for s, (qc, kt, off) in enumerate(SECOND_PASS):
                        for h in range(G4):
                            act.wait_ge(s2_done, u * (G4 * STEPS) + (G4 * s + h + 1))
                            if h == 0 and not (first and s < 3):
                                act.wait_ge(pv_done, u * STEPS + (s - 2))
                            act.activation(pt[s % 3][:, h, off:CH], psS[(G4 * s + h) % RING][:, off:CH], ACT.Exp,
                                           scale=float(HD_A) ** -0.5).then_inc(exp_done, 1)
                        if s == 0 and not first:
                            o_evac(u * 2 - 1, u * STEPS)
                        if s == 2 and not first:
                            o_back(u * 2 - 1)
                        if s == TPC + 2:
                            o_back(u * 2)
                        if s == TPC:
                            o_evac(u * 2, u * STEPS + TPC)
                        if ahead and s == MAX_T:
                            max_row(u + 1)

                def max_row(u):
                    act.wait_ge(m_T, u + 1)
                    act.wait_ge(m_loaded, 16 * u)
                    act.copy(mrow[:, :], psX[0:3 * G4 * NQ, 0:P // 2].bitcast(BF16)).then_inc(m_row, 1)

                act.copy(vu[0][:, :, :, :].rearrange("p t j w -> p (t j w)"), g.V[:, 0:VU]).then_inc(v_unit, 1)
                max_row(0)
                half(0, 0, True, True)
                with act.Fori(0, (UNITS - 4) // 3) as v:
                    for k in range(3):
                        half(v * 3 + (k + 1), (k + 1) % 3, False, True)
                half(UNITS - 3, (UNITS - 3) % 3, False, True)
                half(UNITS - 2, (UNITS - 2) % 3, False, True)
                half(UNITS - 1, (UNITS - 1) % 3, False, False)
                o_evac(2 * UNITS - 1, UNITS * STEPS)
                o_back(2 * UNITS - 1)

            @block.vector
            def _(dve):
                def banks(u, lo, hi):
                    for n in range(lo, hi):
                        h, (_, reductions) = n // len(FIRST_PASS), FIRST_PASS[n % len(FIRST_PASS)]
                        dve.wait_ge(p1_done, u * TILES + (n + 1))
                        for col, tiles, w, kind, qt in reductions:
                            src = ps1[n % RING][:, col * P:(col + tiles * w) * P].rearrange("p (t k) -> p t k", t=tiles)
                            ins = dve.reduce_max(mx[:, kind, h, qt:qt + tiles], src, AX.X)
                        ins.then_inc(p1_max, 1)

                def split_max(u):
                    dve.wait_ge(p1_max, TILES * (u + 1))
                    dve.reduce_max(m_all[:, :], mx[:, :, :, :].rearrange("p k h q -> p (h q) k"), AX.X).then_inc(joined, 1)
                    dve.wait_ge(joined, u + 1)
                    m = m_all[:, :]
                    if not (isinstance(u, int) and u == 0):
                        dve.wait_ge(m_T, u)
                    dve.tensor_scalar(mneg[:, 0, :], m, -1.0, None, ALU.mult).then_inc(mneg1, 1)
                    dve.wait_ge(mneg1, u + 1)
                    dve.scalar_tensor_tensor(mrest[:, :], m, -1.0, mneg[:, 0, :], ALU.mult, ALU.subtract).then_inc(mrest1, 1)
                    dve.wait_ge(mrest1, u + 1)
                    dve.tensor_copy(mneg[:, 1, :], mrest[:, :]).then_inc(mneg2, 1)
                    dve.wait_ge(mneg2, u + 1)
                    dve.tensor_tensor(mneg[:, 2, :], mrest[:, :], mneg[:, 1, :], ALU.subtract).then_inc(mneg3, 1)

                def reciprocal(n):
                    dve.wait_ge(o_in, n + 1)
                    dve.reciprocal(rden[:, :, :], o_raw[:, :, :, HD_A]).then_inc(o_rden, 1)

                def half(u, first, ahead=True, after=True):
                    for s in range(STEPS):
                        if ahead and s == LATER:
                            split_max(u + 1)
                        for slot in range(SLOTS_1):
                            if ahead if s < LATER else after:
                                banks(u + 1 if s < LATER else u + 2, *PLACES[s * SLOTS_1 + slot])
                            if slot == 0:
                                if s == 3 and not first:
                                    reciprocal(u * 2 - 1)
                                if s == TPC + 3:
                                    reciprocal(u * 2)

                dve.memset(mx[:, :, :, :], LOW).then_inc(mx_set, 1)
                dve.wait_ge(mx_set, 1)
                dve.memset(psO, 0.0).then_inc(o_cleared, 1)
                banks(0, 0, TILES)
                split_max(0)
                banks(1, 0, EARLY)
                half(0, True)
                with dve.Fori(0, (UNITS - 4) // 3) as v:
                    for k in range(3):
                        half(v * 3 + (k + 1), False)
                half(UNITS - 3, False)
                half(UNITS - 2, False, True, False)
                half(UNITS - 1, False, False, False)
                reciprocal(2 * UNITS - 1)

            @block.tensor
            def _(pe):
                def loaded(i, n):
                    pe.wait_ge(st_loaded[i], n * (16 * 19))

                def scores1(u, i, lo, hi):
                    for n in range(lo, hi):
                        h, (products, _) = n // len(FIRST_PASS), FIRST_PASS[n % len(FIRST_PASS)]
                        diagonal = n % len(FIRST_PASS) < len(DIAGONALS)
                        if not (isinstance(u, int) and u == 0 and n < RING):
                            pe.wait_ge(p1_max, u * TILES + (n + 1 - RING))
                        if diagonal:
                            pe.matmul(ps1[n % RING], g.identb[:, :], g.maskq[:, :], start=True, stop=False)
                        for qt, k0, w, col in products:
                            ins = pe.matmul(ps1[n % RING][:, col * P:(col + w) * P], q_side(i)[:, h, qt * P:(qt + 1) * P],
                                            k_side(i)[:, h, k0 * P:(k0 + w) * P], start=not diagonal,
                                            stop=not diagonal or qt == products[-1][0])
                        ins.then_inc(p1_done, 1)

                def scores2(u, i, s, h, first):
                    qc, kt, off = SECOND_PASS[s]
                    n = G4 * s + h
                    if not (first and n < RING):
                        pe.wait_ge(exp_done, u * (G4 * STEPS) + (n + 1 - RING))
                    pe.matmul(psS[n % RING][:, off:CH], k_side(i)[:, h, kt * P:(kt + 1) * P], q_side(i)[:, h, qc * CH + off:(qc + 1) * CH],
                              start=True, stop=True).then_inc(s2_done, 1)

                def weighted(u, i, s, first):
                    qc, kt, off = SECOND_PASS[s]
                    last = (qc + 1) * TPC - 1
                    if s in DIAG_STEPS:
                        pe.wait_ge(diag_zeroed, u * (2 * len(DIAG_STEPS)) + 2 * (DIAG_STEPS.index(s) + 1))
                    else:
                        pe.wait_ge(exp_done, u * (G4 * STEPS) + G4 * (s + 1))
                    if s == 0:
                        pe.wait_ge(v_unit, u + 1)
                    if kt == 0 and not (first and s == 0):
                        pe.wait_ge(o_out, u * 2 + qc)
                    for h in range(G4):
                        ins = pe.matmul(psO[32 * h:32 * h + VW, off:CH], vu[i][:, kt, h, :], pt[s % 3][:, h, off:CH],
                                        start=kt == 0, stop=kt == last)
                    ins.then_inc(pv_done, 1)

                def o_transposed(n, others):
                    pe.wait_ge(o_out, n + 1)
                    others()
                    for t in range(TPC):
                        ins = pe.transpose(psX[:, t * P:(t + 1) * P], oT[:, t * P:(t + 1) * P], g.identf[:, :])
                    ins.then_inc(o_T, 1)

                def max_transposed(u):
                    pe.wait_ge(mneg3, u + 1)
                    if not (isinstance(u, int) and u == 0):
                        pe.wait_ge(o_in, 2 * u - 1)
                    pe.transpose(psX[0:3 * G4 * NQ, 0:P // 2].bitcast(BF16), mneg[:, :, :].rearrange("p s n -> p (s n)"), g.identb[:, :]).then_inc(m_T, 1)

                def half(u, i, first, ahead=True, after=True, filled=0):
                    pe.wait_ge(m_loaded, 16 * (u + 1))
                    for s in range(STEPS):
                        place = 0
                        for what in IN_A_STEP:
                            if isinstance(what, int):
                                scores2(u, i, s, what, first)
                            elif what == "product" and s > 0:
                                weighted(u, i, s - 1, first)
                            elif what == "product" and not first:
                                weighted(u - 1, (i + 2) % 3, STEPS - 1, False)
                            elif what == "place":
                                if ahead and s < LATER:
                                    scores1(u + 1, (i + 1) % 3, *PLACES[s * SLOTS_1 + place])
                                elif after and s >= LATER:
                                    if s == LATER and place == 0:
                                        loaded((i + 2) % 3, filled)
                                    scores1(u + 2, (i + 2) % 3, *PLACES[s * SLOTS_1 + place])
                                place += 1
                        if s == 1 and not first:
                            o_transposed(u * 2 - 1, lambda: pe.wait_ge(m_row, u + 1))
                        if s == TPC + 1:
                            o_transposed(u * 2, (lambda: pe.wait_ge(m_row, u + 1)) if first else (lambda: pe.wait_ge(o_in, u * 2)))
                        if ahead and s == MAX_T:
                            max_transposed(u + 1)

                pe.wait_ge(g.ones_in, 48)
                pe.wait_ge(g.st_zeroed, 3)
                pe.wait_ge(o_cleared, 1)
                pe.wait_ge(g.consts, 3)
                loaded(0, 1)
                scores1(0, 0, 0, TILES)
                max_transposed(0)
                loaded(1, 1)
                scores1(1, 1, 0, EARLY)
                half(0, 0, True, filled=1)
                with pe.Fori(0, (UNITS - 4) // 3) as v:
                    for k in range(3):
                        half(v * 3 + (k + 1), (k + 1) % 3, False, filled=v + ((k + 3) // 3 + 1))
                half(UNITS - 3, (UNITS - 3) % 3, False, filled=(UNITS - 1) // 3 + 1)
                half(UNITS - 2, (UNITS - 2) % 3, False, True, False)
                half(UNITS - 1, (UNITS - 1) % 3, False, False, False)
                weighted(UNITS - 1, (UNITS - 1) % 3, STEPS - 1, False)
                o_transposed(2 * UNITS - 1, lambda: pe.wait_ge(o_in, 2 * UNITS - 1))


def ffn(nc, g, second, out):
    with ExitStack() as c:
        tag = "2" if second else "1"
        sb = lambda name, shape, dt=F32: c.enter_context(nc.sbuf_tensor(name + tag, shape, dt))
        sem = lambda name: g.ctx.enter_context(nc.semaphore(name + tag))
        att = sb("att", [P, CH])
        attT = sb("attT", [P, CH])
        xb = sb("x_bias", [P, TPC, P])
        xc = [sb(f"x_mid{i}", [P, TPC, P]) for i in range(2)]
        x2 = sb("x_end", [P, TPC, P])
        stat = sb("f_stat", [P, TPC, 6])
        mv = sb("f_mean_var", [P, TPC, 2])
        ve = sb("f_var_eps", [P, TPC])
        rstd = sb("f_rstd", [P, TPC])
        stat2 = sb("f_stat_e", [P, TPC, 6])
        mv2 = sb("f_mean_var_e", [P, TPC, 2])
        ve2 = sb("f_var_eps_e", [P, TPC])
        rstd2 = sb("f_rstd_e", [P, TPC])
        xn = sb("f_xn", [P, TPC, P])
        xnT = sb("f_xnT", [P, CH])
        xe = sb("f_xn_e", [P, TPC, P])
        gate = sb("gate", [P, 2, CH])
        h = sb("hidden", [P, NH, CH])
        y = sb("f_yT", [P, CH])

        att_loaded, att_T, attT_ready, added_mm, xb_ready = (
            sem("att_loaded"), sem("att_T"), sem("attT_ready"), sem("added_mm"), sem("xb_ready"))
        xc_ready, stats_done, aggr_done, var_ready, rstd_ready, xn_ready = (
            sem("xc_ready"), sem("f_stats"), sem("f_aggr"), sem("f_var"), sem("f_rstd"), sem("f_xn"))
        xn_T, xnT_ready, gate_mm, up_mm, silu_done, h_ready = (
            sem("f_xn_T"), sem("f_xnT"), sem("gate_mm"), sem("up_mm"), sem("silu_done"), sem("h_ready"))
        y_mm, y_ready, y_T, x2_ready, x_kept = sem("y_mm"), sem("y_ready"), sem("y_T"), sem("x2_ready"), sem("x_kept")
        stats2_done, aggr2_done, var2_ready, rstd2_ready, xe_ready, xe_T, xeT_ready = (
            sem("e_stats"), sem("e_aggr"), sem("e_var"), sem("e_rstd"), sem("e_xn"), sem("e_T"), sem("e_xnT"))
        bank = lambda n: g.ps[:, n * CH:(n + 1) * CH]
        psG, psU = [bank(0), bank(1)], [bank(2), bank(3)]
        psY, psF, psA, psT = bank(4), bank(5), bank(6), bank(7)
        bias = g.bo_b if second else g.bo_a
        tiles = lambda ap: ap.rearrange("p (t d) -> p t d", t=TPC)
        flat = lambda ap: ap.rearrange("p t d -> p (t d)")

        def run(eng, front, body):
            front(0, 0)
            body(0, 0, True, True)
            with eng.Fori(0, (NC - 2) // 2) as v:
                for k in range(2):
                    body(v * 2 + (k + 1), (k + 1) % 2, False, True)
            body(NC - 1, (NC - 1) % 2, False, False)

        with nc.Block() as block:

            @block.sync
            def _(sp):
                def load(n):
                    sp.wait_ge(att_T, n)
                    src = g.yT if second else g.O
                    sp.dma_start(att[:, :], src[:, ds(n * CH, CH)]).then_inc(att_loaded, 16)

                def keep(n):
                    sp.wait_ge(x2_ready, n + 1)
                    if second:
                        dst = tok_tiles(out)[:, ds(n * TPC, TPC), :]
                        sp.dma_start(dst, x2[:, :, :]).then_inc(x_kept, 16)
                    else:
                        sp.dma_start(g.X[:, ds(n * TPC, TPC), :], x2[:, :, :]).then_inc(x_kept, 16)

                load(0)
                with sp.Fori(0, NC - 1) as n:
                    load(n + 1)
                    keep(n)
                keep(NC - 1)
                sp.wait_ge(x_kept, 16 * NC)

            @block.gpsimd
            def _(pool):
                def front(n, i):
                    pool.wait_ge(xc_ready, n)
                    pool.tensor_tensor(xb[:, :, :], g.X[:, ds(n * TPC, TPC), :],
                                       bias[:, :].unsqueeze(1).broadcast_to([P, TPC, P]), ALU.add).then_inc(xb_ready, 1)
                    pool.wait_ge(var_ready, n + 1)
                    pool.tensor_tensor(rstd[:, :], ve[:, :], g.expo[:, :], ALU.pow).then_inc(rstd_ready, 1)

                def body(n, i, first, ahead):
                    if ahead:
                        front(n + 1, 1 - i)
                    if not second:
                        pool.wait_ge(var2_ready, n + 1)
                        pool.tensor_tensor(rstd2[:, :], ve2[:, :], g.expo[:, :], ALU.pow).then_inc(rstd2_ready, 1)

                run(pool, front, body)

            @block.scalar
            def _(act):
                def front_a(n):
                    if not second:
                        act.wait_ge(att_T, n + 1)
                        act.wait_ge(added_mm, n)
                        act.copy(attT[:, :], psF).then_inc(attT_ready, 1)

                def front_b(n):
                    act.wait_ge(xn_T, n + 1)
                    act.copy(xnT[:, :], psT).then_inc(xnT_ready, 1)

                def tail(n):
                    act.wait_ge(xe_T, n + 1)
                    act.copy(g.xnT[:, ds(n * CH, CH)], psT).then_inc(xeT_ready, 1)

                def front(n, i):
                    front_a(n)
                    front_b(n)

                def body(n, i, first, ahead):
                    for j in range(NH):
                        act.wait_ge(gate_mm, n * NH + (j + 1))
                        if not (first and j < 2):
                            act.wait_ge(h_ready, n * NH + (j - 1 if j else 0))
                        act.activation(gate[:, j % 2, :], psG[j % 2], ACT.Silu).then_inc(silu_done, 1)
                    if ahead:
                        front_a(n + 1)
                    if not second and not first:
                        tail(n - 1)
                    act.wait_ge(y_mm, n + 1)
                    act.copy(y[:, :], psY).then_inc(y_ready, 1)
                    if ahead:
                        front_b(n + 1)

                run(act, front, body)
                if not second:
                    tail(NC - 1)

            @block.vector
            def _(dve):
                def stats(n, x, st, m, v, s1, s2, s3):
                    for t in range(TPC):
                        ins = dve.bn_stats(st[:, t, :], x[:, t, :])
                    ins.then_inc(s1, 1)
                    wait_alone(dve, s1, n + 1, g.seen_dve)
                    for t in range(TPC):
                        ins = dve.bn_aggr(m[:, t, :], st[:, t, :])
                    ins.then_inc(s2, 1)
                    dve.wait_ge(s2, n + 1)
                    dve.tensor_scalar_add(v[:, :], m[:, :, 1], EPS).then_inc(s3, 1)

                def norm(dst, x, m, r, done):
                    for t in range(TPC):
                        ins = dve.tensor_scalar(dst[:, t, :], x[:, t, :], m[:, t, 0:1], r[:, t:t + 1], ALU.subtract, ALU.mult)
                    ins.then_inc(done, 1)

                def front_a(n, i):
                    dve.wait_ge(att_T if second else added_mm, n + 1)
                    dve.wait_ge(xb_ready, n + 1)
                    dve.tensor_tensor(xc[i][:, :, :], tiles(psA), xb[:, :, :], ALU.add).then_inc(xc_ready, 1)
                    dve.wait_ge(xc_ready, n + 1)
                    stats(n, xc[i], stat, mv, ve, stats_done, aggr_done, var_ready)

                def front_b(n, i):
                    dve.wait_ge(rstd_ready, n + 1)
                    dve.wait_ge(xn_T, n)
                    norm(xn, xc[i], mv, rstd, xn_ready)

                def tail(n):
                    dve.wait_ge(rstd2_ready, n + 1)
                    dve.wait_ge(xe_T, n)
                    norm(xe, x2, mv2, rstd2, xe_ready)

                def front(n, i):
                    front_a(n, i)
                    front_b(n, i)

                def body(n, i, first, ahead):
                    if not second and not first:
                        tail(n - 1)
                    for j in range(NH):
                        dve.wait_ge(silu_done, n * NH + (j + 1))
                        dve.wait_ge(up_mm, n * NH + (j + 1))
                        if j == 0:
                            dve.wait_ge(y_mm, n)
                        dve.tensor_tensor(h[:, j, :], psU[j % 2], gate[:, j % 2, :], ALU.mult).then_inc(h_ready, 1)
                    if ahead:
                        front_a(n + 1, 1 - i)
                    if ahead:
                        front_b(n + 1, 1 - i)
                    dve.wait_ge(y_T, n + 1)
                    dve.wait_ge(x_kept, 16 * n)
                    if not second and not first:
                        dve.wait_ge(xe_ready, n)
                    dve.tensor_tensor(x2[:, :, :], tiles(psF), xc[i][:, :, :], ALU.add).then_inc(x2_ready, 1)
                    if not second:
                        dve.wait_ge(x2_ready, n + 1)
                        stats(n, x2, stat2, mv2, ve2, stats2_done, aggr2_done, var2_ready)

                run(dve, front, body)
                if not second:
                    tail(NC - 1)

            @block.tensor
            def _(pe):
                def front_a(n, first):
                    pe.wait_ge(att_loaded, 16 * (n + 1))
                    dst = psA if second else psF
                    if not first:
                        pe.wait_ge(x2_ready, n - 1)
                        pe.wait_ge(xc_ready, n)
                    for t in range(TPC):
                        ins = pe.transpose(dst[:, t * P:(t + 1) * P], att[:, t * P:(t + 1) * P], g.identf[:, :])
                    ins.then_inc(att_T, 1)
                    if second:
                        return
                    pe.wait_ge(attT_ready, n + 1)
                    for t in range(TPC):
                        ins = pe.matmul(psA[:, t * P:(t + 1) * P], attT[:, t * P:(t + 1) * P], g.wo_a[:, :], start=True, stop=True)
                    ins.then_inc(added_mm, 1)

                def front_b(n, first):
                    pe.wait_ge(xn_ready, n + 1)
                    if not first:
                        pe.wait_ge(xnT_ready, n)
                        if not second:
                            pe.wait_ge(xeT_ready, n - 1)
                    for t in range(TPC):
                        ins = pe.transpose(psT[:, t * P:(t + 1) * P], xn[:, t, :], g.identf[:, :])
                    ins.then_inc(xn_T, 1)

                def tail(n, last):
                    pe.wait_ge(xe_ready, n + 1)
                    pe.wait_ge(xnT_ready, n + 2 if not last else n + 1)
                    for t in range(TPC):
                        ins = pe.transpose(psT[:, t * P:(t + 1) * P], xe[:, t, :], g.identf[:, :])
                    ins.then_inc(xe_T, 1)

                def front(n, i):
                    front_a(n, True)
                    front_b(n, True)

                def body(n, i, first, ahead):
                    pe.wait_ge(xnT_ready, n + 1)
                    for j in range(NH):
                        if not (first and j < 2):
                            pe.wait_ge(silu_done, n * NH + (j - 1 if j else 0))
                        pe.matmul(psG[j % 2], g.wgT[:, j * P:(j + 1) * P], xnT[:, :], start=True, stop=True).then_inc(gate_mm, 1)
                        if not (first and j < 2):
                            pe.wait_ge(h_ready, n * NH + (j - 1 if j else 0))
                        pe.matmul(psU[j % 2], g.wuT[:, j * P:(j + 1) * P], xnT[:, :], start=True, stop=True).then_inc(up_mm, 1)
                    if ahead:
                        front_a(n + 1, False)
                    pe.wait_ge(h_ready, (n + 1) * NH)
                    pe.wait_ge(y_ready, n)
                    for j in range(NH):
                        ins = pe.matmul(psY, g.wdT[:, j * P:(j + 1) * P], h[:, j, :], start=j == 0, stop=j == NH - 1)
                    ins.then_inc(y_mm, 1)
                    if not second and not first:
                        tail(n - 1, False)
                    if ahead:
                        front_b(n + 1, False)
                    pe.wait_ge(y_ready, n + 1)
                    if second:
                        pe.wait_ge(x2_ready, n)
                    else:
                        pe.wait_ge(attT_ready, n + 2 if ahead else n + 1)
                    for t in range(TPC):
                        ins = pe.transpose(psF[:, t * P:(t + 1) * P], y[:, t * P:(t + 1) * P], g.identf[:, :])
                    ins.then_inc(y_T, 1)

                run(pe, front, body)
                if not second:
                    tail(NC - 1, True)


ORDER = [7, 0, 6, 1, 5, 2, 4, 3]
SLOTS = 4
GROUP = 4
GROUPS = [-(-(qt + 1) // GROUP) for qt in ORDER]
GROUPS_BEFORE = [2 * sum(GROUPS[:t]) for t in range(NQ + 1)]
JOBS = 8
JOB_AT = {0: 0, 1: 1, 3: 2, 5: 3, 7: 4, 8: JOBS, 9: 5, 11: JOBS + 1, 13: 6, 15: 7}
QX, QC, KA, KB, KC = range(5)
PASSES = ((QX, KA), (QX, KB), (QC, KC))


def bias_attention(nc, g, wq, wk, wv, wo):
    with ExitStack() as c:
        sb = lambda name, shape, dt=F32: c.enter_context(nc.sbuf_tensor(name, shape, dt))
        sem = lambda name: g.ctx.enter_context(nc.semaphore(name))
        w3 = sb("w_pair", [P, 3, P])
        wo_p = sb("wo_pair", [P, P])
        nat = sb("pair_parts", [P, 6, T], BF16)
        rest = sb("pair_rest", [P, 2, CH])
        stack = [sb(f"pair_stack{i}", [P, 2, 5, T], BF16) for i in range(2)]
        vT = sb("pair_vT", [P, T])
        v = [sb(f"pair_v{i}", [P, NQ, P]) for i in range(2)]
        band = [sb(f"band{i}", [P, 2, T]) for i in range(2)]
        sc = sb("scores", [P, SLOTS, 2, T])
        pT = [sb(f"probsT{i}", [P, 2, NQ, P]) for i in range(2)]
        oT = [sb(f"pair_oT{i}", [P, T]) for i in range(2)]
        mx = sb("b_max", [P, SLOTS, 2])
        mneg = sb("b_neg_max", [P, SLOTS, 2])
        den = sb("b_den", [P, SLOTS, 2])
        rden = sb("b_rden", [P, SLOTS, 2])

        w_loaded, wo_loaded = sem("b_w_loaded"), sem("b_wo_loaded")
        st_loaded = [sem(f"b_st_loaded{i}") for i in range(2)]
        band_loaded = [sem(f"band_loaded{i}") for i in range(2)]
        band_zeroed, y_zeroed = sem("band_zeroed"), sem("y_zeroed")
        job_mm, job_free = sem("job_mm"), sem("job_free")
        p1_ready, rest_ready, p2_ready, p3_ready, vT_ready = (
            sem("b_p1"), sem("b_rest"), sem("b_p2"), sem("b_p3"), sem("b_vT"))
        s_done, max_done, neg_done, exp_done, rden_done, norm_done = (
            sem("b_scores"), sem("b_max_done"), sem("b_neg_done"), sem("b_exp"), sem("b_rden_done"), sem("b_norm"))
        t_done, pv_done, o_out = sem("b_transposed"), sem("b_pv"), sem("b_o_out")
        t_out = [sem("b_t_out_act"), sem("b_t_out_dve")]
        psS = [g.ps[:, 0:T], g.ps[:, T:2 * T]]
        psT = [g.ps[:, 2 * T:2 * T + CH], g.ps[:, 2 * T + CH:3 * T]]
        psO = g.ps[:, 3 * T:3 * T + CH]
        psJ = g.ps[:, 3 * T + CH:4 * T]
        TILES2 = 2 * NQ
        NG = GROUPS_BEFORE[NQ]

        def jobs_before(i):
            if isinstance(i, int):
                return JOBS if i == 0 else (JOBS + 2) * i + JOBS - 2
            return i * (JOBS + 2) + (JOBS - 2)

        def jobs_of(first, ahead):
            found = [(at, k) for at, k in sorted(JOB_AT.items()) if (ahead if k < JOBS else not first)]
            return {at: (k, n + 1) for n, (at, k) in enumerate(found)}

        def done_with(k, first):
            return next(n for j, n in jobs_of(first, True).values() if j == k)

        def pv_free(i, t):
            return max(0, NQ * i + t - 1) if isinstance(i, int) else i * NQ + (t - 1)

        def run(eng, body):
            body(0, 0, True, True)
            with eng.Fori(0, (ITERS - 2) // 2) as n:
                for k in range(2):
                    body(n * 2 + (k + 1), (k + 1) % 2, False, True)
            body(ITERS - 1, (ITERS - 1) % 2, False, False)

        with nc.Block() as block:

            @block.sync
            def _(sp):
                def load_w(i):
                    cols = ds((i % PAIRS) * P, P)
                    for k, w in enumerate((wq, wk, wv)):
                        sp.dma_start(w3[:, k, :], w[:, cols]).then_inc(w_loaded, 16)

                def load_wo(i):
                    sp.dma_start(wo_p[:, :], wo[ds((i % PAIRS) * P, P), :]).then_inc(wo_loaded, 16)

                def load_band(i, par):
                    for h in range(2):
                        src = g.lrep_flat[ds(((i % PAIRS) * 2 + h) * (P * LROW) + (P - 1), P * (LROW - 1))].rearrange("(q n) -> q n", n=LROW - 1)
                        sp.dma_start(band[par][:, h, T - 2 * P:T], src[:, 0:2 * P]).then_inc(band_loaded[par], 16)

                def gather(par, q_side):
                    for h in range(2):
                        rows = slice(HD_B * h, HD_B * (h + 1))
                        top, low = stack[par][0:HD_B, h, :, :], stack[par][HD_B:P, h, :, :]
                        if q_side:
                            copies = ((top[:, QX, :], 0, 1), (top[:, QC, :], 0, 1), (low[:, QX:QC + 1, :], 1, 2))
                        else:
                            copies = ((top[:, KA:KC + 1, :], 3, 3), (low[:, KA:KB + 1, :], 3, 2), (low[:, KC, :], 3, 1))
                        for dst, part, n in copies:
                            src = nat[rows, part, :] if n == 1 else nat[rows, part:part + n, :]
                            sp.dma_start(dst, src).then_inc(st_loaded[par], 16)

                def next_pair(i, par, v_done):
                    sp.wait_ge(p3_ready, i * 4 + 2)
                    gather(par, True)
                    sp.wait_ge(p3_ready, i * 4 + 4)
                    gather(par, False)
                    sp.wait_ge(job_mm, v_done)

                def body(i, par, first, ahead):
                    if not ahead:
                        return
                    if not first:
                        sp.wait_ge(max_done, i * TILES2)
                        sp.wait_ge(s_done, i * TILES2)
                    load_band(i + 1, 1 - par)
                    next_pair(i + 1, 1 - par, jobs_before(i) + done_with(5, first))
                    load_w(i + 2)
                    if not first:
                        sp.wait_ge(job_mm, jobs_before(i) + done_with(JOBS + 1, first))
                        load_wo(i)

                load_w(0)
                sp.wait_ge(band_zeroed, 2)
                load_band(0, 0)
                load_wo(0)
                next_pair(0, 0, 6)
                load_w(1)
                run(sp, body)
                sp.wait_ge(job_mm, jobs_before(ITERS - 1) + 2)
                load_wo(ITERS - 1)
                sp.wait_ge(w_loaded, 48 * (ITERS + 1))
                sp.wait_ge(wo_loaded, 16 * ITERS)
                for par in range(2):
                    sp.wait_ge(band_loaded[par], 32 * ITERS // 2)

            @block.gpsimd
            def _(pool):
                def third(i, k):
                    pool.wait_ge(p2_ready, i * 4 + (k + 1))
                    x, half = k // 2, k % 2
                    pool.tensor_tensor(nat[:, 3 * x + 2, half * CH:(half + 1) * CH], rest[:, half, :],
                                       nat[:, 3 * x + 1, half * CH:(half + 1) * CH], ALU.subtract).then_inc(p3_ready, 1)

                def divide(n, t):
                    w = (ORDER[t % NQ] + 1) * P
                    for h in range(2):
                        wait_alone(pool, rden_done, n + (h + 1), g.seen_pool)
                        p = sc[:, t % SLOTS, h, 0:w]
                        pool.tensor_scalar(p, p, rden[:, t % SLOTS, h:h + 1], 1.0, ALU.mult, ALU.mult).then_inc(norm_done, 1)

                def body(i, par, first, ahead):
                    for t in range(NQ):
                        if t + 1 < NQ or ahead:
                            divide(i * TILES2 + 2 * (t + 1), t + 1)
                        if ahead and t < 4:
                            third(i + 1, t)

                for par in range(2):
                    pool.memset(band[par][:, :, :], 0.0).then_inc(band_zeroed, 1)
                for k in range(4):
                    third(0, k)
                divide(0, 0)
                run(pool, body)

            @block.scalar
            def _(act):
                def job_out(i, k, count):
                    if k < 6:
                        act.wait_ge(job_mm, count)
                    half = slice((k % 2) * CH, (k % 2 + 1) * CH)
                    if k < 4:
                        if k == 0:
                            if not (isinstance(i, int) and i == 0):
                                act.wait_ge(st_loaded[0], gathered(0, i))
                                act.wait_ge(st_loaded[1], gathered(1, i))
                        act.copy(nat[:, 3 * (k // 2), half], psJ).then_inc(p1_ready, 1)
                    elif k < 6:
                        act.copy(vT[:, half], psJ).then_inc(job_free, 1)

                def gathered(par, i):
                    if par == 0:
                        return ((i + 1) // 2) * (12 * 16)
                    return (i // 2) * (12 * 16)

                def exponent(n, t, h):
                    w = (ORDER[t % NQ] + 1) * P
                    act.wait_ge(neg_done, n + 1)
                    p = sc[:, t % SLOTS, h, 0:w]
                    act.activation(p, p, ACT.Exp, bias=mneg[:, t % SLOTS, h:h + 1], scale=1.0 / HD_B,
                                   accum_out=den[:, t % SLOTS, h:h + 1]).then_inc(exp_done, 1)

                def evac(i, t, h, mine=0):
                    g0 = GROUPS_BEFORE[t] + h * GROUPS[t]
                    for q in range(GROUPS[t]):
                        if (g0 + q) % 2 != mine:
                            continue
                        nb = min(GROUP, ORDER[t] + 1 - q * GROUP)
                        act.wait_ge(t_done, i * NG + (g0 + q + 1))
                        act.wait_ge(pv_done, pv_free(i, t))
                        act.copy(pT[t % 2][:, h, q * GROUP:q * GROUP + nb, :].rearrange("p n q -> p (n q)"),
                                 psT[(g0 + q) % 2][:, 0:nb * P]).then_inc(t_out[mine], 1)

                def body(i, par, first, ahead):
                    base = jobs_before(i)
                    jobs = jobs_of(first, ahead)
                    for t in range(NQ):
                        for h in range(2):
                            if 2 * t + h in jobs:
                                k, n = jobs[2 * t + h]
                                job_out(i + 1, k, base + n)
                            evac(i, t, h)
                            if t + 2 < NQ or ahead:
                                exponent(i * TILES2 + (2 * (t + 2) + h), t + 2, h)

                for k in range(6):
                    job_out(0, k, k + 1)
                for t in range(2):
                    for h in range(2):
                        exponent(2 * t + h, t, h)
                run(act, body)

            @block.vector
            def _(dve):
                def job_out(i, k, count, q4):
                    half = slice((k % 2) * CH, (k % 2 + 1) * CH)
                    x = k // 2
                    if k < 4:
                        n = i * 4 + k
                        dve.wait_ge(p1_ready, n + 1)
                        dve.wait_ge(p3_ready, max(0, n - 1) if isinstance(n, int) else n - 1)
                        dve.tensor_tensor(rest[:, k % 2, :], psJ, nat[:, 3 * x, half], ALU.subtract).then_inc(job_free, 1)
                        dve.wait_ge(job_free, count)
                        dve.tensor_copy(nat[:, 3 * x + 1, half], rest[:, k % 2, :]).then_inc(p2_ready, 1)
                    elif k >= 6 and k < JOBS:
                        dve.wait_ge(job_mm, count)
                        dve.tensor_copy(q4[:, (k - 6) * TPC:(k - 5) * TPC, :].rearrange("p n d -> p (n d)"), psJ).then_inc(job_free, 1)

                def y_out(i, half, count):
                    dve.wait_ge(job_mm, count)
                    y = g.yT[:, ds((i // PAIRS) * T + half * CH, CH)]
                    dve.tensor_tensor(y, psJ, y, ALU.add).then_inc(job_free, 1)

                def maximum(n, t, h, par):
                    w = (ORDER[t % NQ] + 1) * P
                    slot = t % SLOTS
                    wait_alone(dve, s_done, n + 1, g.seen_dve)
                    dve.tensor_tensor_reduce(out=sc[:, slot, h, 0:w], in0=psS[h][:, 0:w], in1=band[par][:, h, T - w:T],
                                             scale=1.0, scalar=LOW, op0=ALU.add, op1=ALU.max,
                                             accum_out=mx[:, slot, h:h + 1]).then_inc(max_done, 1)
                    dve.wait_ge(max_done, n + 1)
                    dve.tensor_scalar(mneg[:, slot, h:h + 1], mx[:, slot, h:h + 1], -1.0 / HD_B, None, ALU.mult).then_inc(neg_done, 1)

                def reciprocal(n, t, h):
                    dve.wait_ge(exp_done, n + 1)
                    dve.reciprocal(rden[:, t % SLOTS, h:h + 1], den[:, t % SLOTS, h:h + 1]).then_inc(rden_done, 1)

                def evac(i, t, h, mine=1):
                    g0 = GROUPS_BEFORE[t] + h * GROUPS[t]
                    for q in range(GROUPS[t]):
                        if (g0 + q) % 2 != mine:
                            continue
                        nb = min(GROUP, ORDER[t] + 1 - q * GROUP)
                        dve.wait_ge(t_done, i * NG + (g0 + q + 1))
                        dve.wait_ge(pv_done, pv_free(i, t))
                        dve.tensor_copy(pT[t % 2][:, h, q * GROUP:q * GROUP + nb, :].rearrange("p n q -> p (n q)"),
                                        psT[(g0 + q) % 2][:, 0:nb * P]).then_inc(t_out[mine], 1)

                def o_evac(n, t, par):
                    dve.wait_ge(pv_done, n + 1)
                    qt = ORDER[t]
                    dve.tensor_copy(oT[par][:, qt * P:(qt + 1) * P], psO[:, (t % GROUP) * P:(t % GROUP + 1) * P]).then_inc(o_out, 1)

                def body(i, par, first, ahead):
                    base = jobs_before(i)
                    jobs = jobs_of(first, ahead)
                    for t in range(NQ):
                        after = t + 2 < NQ or ahead
                        band_par = par if t + 2 < NQ else 1 - par
                        if t + 1 < NQ or ahead:
                            for h in range(2):
                                reciprocal(i * TILES2 + (2 * (t + 1) + h), t + 1, h)
                        if ahead and t + 2 == NQ:
                            dve.wait_ge(band_loaded[1 - par], bands(i + 1))
                        for h in range(2):
                            if after:
                                maximum(i * TILES2 + (2 * (t + 2) + h), t + 2, h, band_par)
                            if 2 * t + h in jobs:
                                k, n = jobs[2 * t + h]
                                if k < JOBS:
                                    job_out(i + 1, k, base + n, v[1 - par])
                                else:
                                    y_out(i - 1, k - JOBS, base + n)
                            evac(i, t, h)
                        if t > 0:
                            o_evac(i * NQ + (t - 1), t - 1, par)
                        elif not first:
                            o_evac(i * NQ - 1, NQ - 1, 1 - par)

                def bands(i):
                    return (i // 2 + 1) * 32

                dve.memset(g.yT[:, :], 0.0).then_inc(y_zeroed, 1)
                for k in range(JOBS):
                    job_out(0, k, k + 1, v[0])
                dve.wait_ge(band_zeroed, 2)
                dve.wait_ge(band_loaded[0], 32)
                dve.wait_ge(y_zeroed, 1)
                for t in range(2):
                    for h in range(2):
                        maximum(2 * t + h, t, h, 0)
                for h in range(2):
                    reciprocal(h, 0, h)
                run(dve, body)
                o_evac(ITERS * NQ - 1, NQ - 1, (ITERS - 1) % 2)
                for h in range(2):
                    y_out(ITERS - 1, h, jobs_before(ITERS - 1) + 2 + h + 1)

            @block.tensor
            def _(pe):
                def job(i, k, before):
                    if k == 0:
                        pe.wait_ge(w_loaded, (i + 1) * 48)
                    if not (isinstance(i, int) and i == 0 and k == 0):
                        pe.wait_ge(job_free, before)
                    if k < 6:
                        x = g.xnT[:, ds((i // PAIRS) * T + (k % 2) * CH, CH)]
                        ins = pe.matmul(psJ, w3[:, k // 2, :], x, start=True, stop=True)
                    else:
                        for n in range(TPC):
                            at = (k - 6) * CH + n * P
                            ins = pe.transpose(psJ[:, n * P:(n + 1) * P], vT[:, at:at + P], g.identf[:, :])
                    ins.then_inc(job_mm, 1)

                def out_job(i, par, half, count):
                    if half == 0:
                        pe.wait_ge(wo_loaded, (i + 1) * 16)
                        pe.wait_ge(o_out, (i + 1) * NQ)
                    pe.wait_ge(job_free, count)
                    pe.matmul(psJ, wo_p[:, :], oT[par][:, half * CH:(half + 1) * CH], start=True, stop=True).then_inc(job_mm, 1)

                def scores(n, t, h, par, opening):
                    qt = ORDER[t % NQ]
                    w = (qt + 1) * P
                    if not opening:
                        pe.wait_ge(max_done, n - 1)
                    for lo in range(0, w, CH):
                        hi = min(w, lo + CH)
                        for p, (q, k) in enumerate(PASSES):
                            ins = pe.matmul(psS[h][:, lo:hi], stack[par][:, h, q, qt * P:(qt + 1) * P], stack[par][:, h, k, lo:hi],
                                            start=p == 0, stop=p == len(PASSES) - 1)
                    ins.then_inc(s_done, 1)

                def transposed(i, t, h, first):
                    pe.wait_ge(norm_done, i * TILES2 + (2 * t + h + 1))
                    for q in range(GROUPS[t]):
                        n = GROUPS_BEFORE[t] + h * GROUPS[t] + q
                        if not (first and n < 2):
                            pe.wait_ge(t_out[n % 2], i * (NG // 2) + n // 2)
                        for b in range(q * GROUP, min(ORDER[t] + 1, (q + 1) * GROUP)):
                            ins = pe.transpose(psT[n % 2][:, (b % GROUP) * P:(b % GROUP + 1) * P], sc[:, t % SLOTS, h, b * P:(b + 1) * P], g.identf[:, :])
                        ins.then_inc(t_done, 1)

                def product(i, t, par, first):
                    done = GROUPS_BEFORE[t + 1]
                    pe.wait_ge(t_out[0], i * (NG // 2) + (done + 1) // 2)
                    pe.wait_ge(t_out[1], i * (NG // 2) + done // 2)
                    if not (first and t == 0):
                        pe.wait_ge(o_out, i * NQ + t)
                    at = (t % GROUP) * P
                    for b in range(ORDER[t] + 1):
                        for h in range(2):
                            ins = pe.matmul(psO[h * HD_B:(h + 1) * HD_B, at:at + P], v[par][:, b, h * HD_B:(h + 1) * HD_B], pT[t % 2][:, h, b, :],
                                            start=b == 0, stop=b == ORDER[t])
                    ins.then_inc(pv_done, 1)

                def body(i, par, first, ahead):
                    base = jobs_before(i)
                    jobs = jobs_of(first, ahead)
                    for t in range(NQ):
                        if ahead and t + 2 == NQ:
                            pe.wait_ge(st_loaded[1 - par], stacks(i + 1))
                        for h in range(2):
                            if t + 2 < NQ or ahead:
                                scores(i * TILES2 + (2 * (t + 2) + h), t + 2, h, par if t + 2 < NQ else 1 - par, False)
                            if 2 * t + h in jobs:
                                k, n = jobs[2 * t + h]
                                if k < JOBS:
                                    job(i + 1, k, base + (n - 1))
                                else:
                                    out_job(i - 1, 1 - par, k - JOBS, base + (n - 1))
                            transposed(i, t, h, first)
                        if t > 0:
                            product(i, t - 1, par, first)
                        elif not first:
                            product(i - 1, NQ - 1, 1 - par, False)

                def stacks(i):
                    return (i // 2 + 1) * (12 * 16)

                for k in range(JOBS):
                    job(0, k, k)
                pe.wait_ge(st_loaded[0], 12 * 16)
                for t in range(2):
                    for h in range(2):
                        scores(2 * t + h, t, h, 0, t == 0)
                run(pe, body)
                product(ITERS - 1, NQ - 1, (ITERS - 1) % 2, False)
                for h in range(2):
                    out_job(ITERS - 1, (ITERS - 1) % 2, h, jobs_before(ITERS - 1) + 2 + h)


def build(nc, x, wqkv, wo_a, bo_a, wq, wk, wv, wo_b, bo_b, rel, w_gate, w_up, w_down, out):
    with ExitStack() as ctx:
        class g:
            pass
        g.ctx = ctx
        g.seen_dve = ctx.enter_context(nc.semaphore("seen_dve"))
        g.seen_pool = ctx.enter_context(nc.semaphore("seen_pool"))
        g.consts = ctx.enter_context(nc.semaphore("consts"))
        sb = lambda name, shape, dt=F32: ctx.enter_context(nc.sbuf_tensor(name, shape, dt))
        g.ps = ctx.enter_context(nc.psum_tensor("ps", [P, 8 * CH], F32))
        g.X = sb("x_stream", [P, NT, P])
        g.identf = sb("identf", [P, P])
        g.identb = sb("identb", [P, P], BF16)
        g.expo = sb("minus_half", [P, TPC])
        g.wgT = sb("w_gateT", [P, HID])
        g.wuT = sb("w_upT", [P, HID])
        g.wdT = sb("w_downT", [P, HID])
        g.wo_a = sb("wo_a", [P, P])
        g.bo_a = sb("bo_a", [P, P])
        g.bo_b = sb("bo_b", [P, P])
        g.st_zeroed = ctx.enter_context(nc.semaphore("st_zeroed"))
        g.zero_one_set = ctx.enter_context(nc.semaphore("zero_one_set"))
        g.ones_in = ctx.enter_context(nc.semaphore("ones_in"))
        g.st_loaded = [ctx.enter_context(nc.semaphore(f"st_loaded{i}")) for i in range(3)]
        g.qs = nc.dram_tensor("qk_parts_dram", (3, 2, P, B * T), BF16, kind="Internal").ap()
        lrep = nc.dram_tensor("bias_rows_dram", (HEADS * P * LROW + P,), F32, kind="Internal").ap()
        g.lrep = lrep[0:HEADS * P * LROW].rearrange("(h q n) -> h q n", h=HEADS, q=P)
        g.lrep_flat = lrep
        tables = nc.inline_tensor(rope_tables(), "rope_tables").ap()
        g.yT = sb("att_bT", [P, B * T])
        with ExitStack() as c1:
            g.xnT = c1.enter_context(nc.sbuf_tensor("x_normT", [P, B * T], F32))
            with ExitStack() as c2:
                g.O = c2.enter_context(nc.sbuf_tensor("att_a", [P, NT * D + D - G4 * HD_A], F32))
                with ExitStack() as c3:
                    sb = lambda name, shape, dt=F32: c3.enter_context(nc.sbuf_tensor(name, shape, dt))
                    g.maskq = sb("mask_query_key", [P, CH], BF16)
                    g.zero_one = sb("zero_one", [3, 2, G4, T], BF16)
                    g.V = sb("values_a", [P, UNITS * VU])
                    g.stack = [sb(f"stack{i}", [ROWS, 2, G4, T], BF16) for i in range(3)]
                    prepare(nc, g, x, wqkv, rel, w_gate, w_up, w_down, wo_a, bo_a, bo_b, tables)
                    rope_attention(nc, g)
                ffn(nc, g, False, out)
            bias_attention(nc, g, wq, wk, wv, wo_b)
        ffn(nc, g, True, out)


_NAMES = ["L0_attn_a_x", "L0_attn_a_Wqkv", "L0_attn_a_Wo", "L0_attn_a_bo", "L0_attn_b_Wq", "L0_attn_b_Wk", "L0_attn_b_Wv",
          "L0_attn_b_Wo", "L0_attn_b_bo", "L0_attn_b_rel_pos_bias", "L0_ffn_w_gate", "L0_ffn_w_up", "L0_ffn_w_down"]


def kernel(**inputs):
    import concourse.bacc as bacc
    from concourse.bass_utils import run_bass_kernel_spmd

    nc = bacc.Bacc("TRN2", target_bir_lowering=False, num_devices=1)
    arrays, args = {}, []
    for name in _NAMES:
        a = np.ascontiguousarray(inputs[name])
        arrays[name] = a
        args.append(nc.dram_tensor(name, a.shape, mybir.dt.from_np(a.dtype), kind="ExternalInput").ap())
    out = nc.dram_tensor("out", (B, T, D), F32, kind="ExternalOutput").ap()
    build(nc, *args, out)
    r = run_bass_kernel_spmd(nc, [arrays], core_ids=[0])
    return r.results[0]["out"]
```

```python
import numpy as np
import concourse.bass as bass
from concourse import mybir
from concourse.alu_op_type import AluOpType as ALU
from contextlib import ExitStack

F32 = mybir.dt.float32
BF16 = mybir.dt.bfloat16
I32 = mybir.dt.int32
ACT = mybir.ActivationFunctionType
AX = mybir.AxisListType
ds = bass.ds

P = 128
B, T, D = 4, 1024, 128
NT = B * T // P
CH = 512
NC = B * T // CH
TPC = CH // P
NQ = T // P
HEADS = 16
TWO_ONES = float(np.array([0x3F803F80], np.uint32).view(np.float32)[0])
LOADS = 7
HD_A = D // HEADS
HD_B = 64
HID = 384
NH = HID // P
EPS = 1e-5
W_SCALE = float(np.float32(1.0 / 127.0))
LOW = -3.0e38
RANGE = 128
LROW = 3 * RANGE

G4 = 4
UNITS = B * HEADS // G4
NPROD = 9
ROW_M = NPROD * HD_A
ROWS = 96
VW = HD_A + 1
VU = NQ * G4 * VW

PAIRS = HEADS // 2
ITERS = B * PAIRS


def tok_tiles(x):
    return x.rearrange("b (n p) d -> p (b n) d", p=P)


def rope_tables():
    half = HD_A // 2
    inv = (np.float32(1.0) / np.power(np.float32(10000.0), np.arange(half, dtype=np.float32) / np.float32(half))).astype(np.float32)
    ang = (np.arange(T, dtype=np.float32)[:, None] * inv[None, :]).astype(np.float32)
    both = np.stack([np.cos(ang.astype(np.float64)), np.sin(ang.astype(np.float64))])
    return np.ascontiguousarray(np.repeat(both, 2, axis=-1).transpose(0, 2, 1)).astype(np.float32)


def wait_alone(eng, sem, value, seen):
    eng.wait_ge(sem, value)
    eng.sem_inc(seen, 1)


def load_ones(sp, g, i):
    sp.dma_start(g.stack[i][ROW_M:ROW_M + 3, 1, :, :], g.zero_one[:, 1, :].unsqueeze(1).broadcast_to([3, G4, T])).then_inc(g.ones_in[i], 16)


def load_stack(sp, g, u, i):
    q = g.qs[ds(u // 4, 1), 0, :, :, :, :].rearrange("b s d h t -> (b s) d h t")[:, :, ds((u % 4) * G4, G4), :]
    k = g.qs[ds(u // 4, 1), 1, :, :, :, :].rearrange("b s d h t -> (b s d) h t")[:, ds((u % 4) * G4, G4), :]
    for qp in range(3):
        rows = slice(qp * 3 * HD_A, (qp + 1) * 3 * HD_A)
        one_q = q[qp, :, :, :].rearrange("d h t -> d (h t)").unsqueeze(0).broadcast_to([3, HD_A, G4 * T])
        sp.dma_start(g.stack[i][rows, 0, :, :].rearrange("r h t -> r (h t)"), one_q).then_inc(g.st_loaded[i], 16)
        sp.dma_start(g.stack[i][rows, 1, :, :].rearrange("r h t -> r (h t)"), k.rearrange("r h t -> r (h t)")).then_inc(g.st_loaded[i], 16)
    sp.dma_start(g.stack[i][ROW_M:ROW_M + 3, 0, :, :], g.zero_one[:, 0, :].unsqueeze(1).broadcast_to([3, G4, T])).then_inc(g.st_loaded[i], 16)


def prepare(nc, g, block, x, wqkv, rel, w_gate, w_up, w_down, wo_a, bo_a, bo_b, tables):
    with ExitStack() as c:
        sb = lambda name, shape, dt=F32: c.enter_context(nc.sbuf_tensor(name, shape, dt))
        sem = lambda name: g.ctx.enter_context(nc.semaphore(name))
        w3 = sb("w_qkv", [P, 3, P])
        wqk = sb("w_qk_by_dim", [P, 2, P])
        wrot = sb("w_rot", [P, 2, P])
        cos, sin = g.O[:, 0:T], g.O[:, T:2 * T]
        wi = sb("w_int", [P, 3, HID], I32)
        wf = sb("w_float", [P, 3, HID])
        relrow = sb("rel_rows", [HEADS, RANGE])
        lrow = g.lrow
        stat = sb("stat", [P, TPC, 6])
        mv = sb("mean_var", [P, TPC, 2])
        ve = sb("var_eps", [P, TPC])
        rstd = sb("rstd", [P, TPC])
        xn = sb("xn", [P, TPC, P])
        xnT = [sb(f"xnT{i}", [P, CH]) for i in range(2)]
        tc = sb("times_cos", [P, 2, CH])
        tsn = sb("times_sin", [P, 2, CH])
        qk = sb("qk_roped", [P, 2, CH])
        rest = [sb(f"qk_rest{i}", [P, 2, CH]) for i in range(2)]
        parts = g.parts

        x_loaded = [sem(f"x_loaded{i}") for i in range(3)]
        w_loaded, tab_loaded = sem("w_loaded"), sem("tab_loaded")
        int_loaded, rel_loaded = sem("int_loaded"), sem("rel_loaded")
        later_loaded = g.later_loaded = sem("later_loaded")
        zeroed, consts, ones_set = sem("zeroed"), g.consts, sem("ones_set")
        rot_ready, wf_ready, ffn_T, ffn_stored = sem("rot_ready"), sem("wf_ready"), sem("ffn_T"), sem("ffn_stored")
        lrow_ready = sem("lrow_ready")
        lrow_stored = g.lrow_stored = sem("lrow_stored")
        stats_done, aggr_done, var_ready, rstd_ready = sem("stats_done"), sem("aggr_done"), sem("var_ready"), sem("rstd_ready")
        xn_ready, xn_T, xnT_ready = sem("xn_ready"), sem("xn_T"), sem("xnT_ready")
        qk_mm, v_mm, v_stored = sem("qk_mm"), sem("v_mm"), sem("v_stored")
        rope_read, q_ready, p1_ready, rest_ready, p2_ready, split_done = (
            sem("rope_read"), sem("q_ready"), sem("p1_ready"), sem("rest_ready"), sem("p2_ready"), sem("split_done"))
        parts_stored = g.parts_stored = [sem(f"parts_stored{i}") for i in range(2)]
        g.qk_read, g.v_in_place, g.ffn_in_place, g.split_done, g.xnT_taken = rope_read, v_stored, ffn_stored, split_done, xnT_ready
        psT = g.ps[:, 0:CH]
        psV = g.ps[:, CH:2 * CH]
        psQ = [g.ps[:, (2 + j) * CH:(3 + j) * CH] for j in range(4)]
        psW = g.ps[:, 6 * CH:8 * CH]

        def run(eng, body, between=lambda n: None):
            for n in range(2):
                body(n, n % 2)
                between(n)
            with eng.Fori(0, (NC - 4) // 2) as m:
                for k in range(2):
                    body(m * 2 + (k + 2), k % 2)
            body(NC - 2, 0)
            body(NC - 1, 1)

        def known(n, least):
            return isinstance(n, int) and n < least

        def is_last(n):
            return isinstance(n, int) and n == NC - 1

        @block.sync
        def _(sp):
            for n in range(2):
                sp.dma_start(g.X[:, n * TPC:(n + 1) * TPC, :], tok_tiles(x)[:, n * TPC:(n + 1) * TPC, :]).then_inc(x_loaded[n], 16)
            for b in range(1, B):
                sp.dma_start(g.X[:, b * NQ:(b + 1) * NQ, :], tok_tiles(x)[:, b * NQ:(b + 1) * NQ, :]).then_inc(x_loaded[2], 16)
            for n, w in enumerate((w_gate, w_up)):
                sp.dma_start(wi[:, n, :].rearrange("p (t d) -> p t d", t=NH), w.rearrange("(t p) d -> p t d", p=P)).then_inc(int_loaded, 16)
            sp.dma_start(wi[:, 2, :], w_down).then_inc(int_loaded, 16)
            sp.dma_start(relrow[:, :], rel).then_inc(rel_loaded, 16)
            sp.dma_start(g.wo_a[:, :], wo_a).then_inc(later_loaded, 16)
            for dst, src in ((g.bo_a, bo_a), (g.bo_b, bo_b)):
                sp.dma_start(dst[:, :], bass.AP(src.tensor, src.offset, [[0, P], [1, P]])).then_inc(later_loaded, 16)

            def store(n, par):
                sp.wait_ge(split_done, n + 1)
                dst = g.qs[ds(n // 2, 1), :, :, :, :, par * CH:(par + 1) * CH]
                sp.dma_start(dst.rearrange("b x s d h t -> (d h) (b x s) t"),
                             parts[par][:, :, :, :].rearrange("p x s t -> p (x s) t")).then_inc(parts_stored[par], 16)

            def between(n):
                if n == 1:
                    for par in range(2):
                        sp.wait_ge(parts_stored[par], 16)
                    sp.wait_ge(g.st_zeroed, 1)
                    sp.wait_ge(g.zero_one_set, 2)
                    load_ones(sp, g, 0)
                    load_stack(sp, g, 0, 0)

            run(sp, store, between)
            sp.wait_ge(lrow_ready, 3)
            sp.dma_start(g.lrep, lrow[:, :].unsqueeze(1).broadcast_to([HEADS, P, LROW])).then_inc(lrow_stored, 16)

        @block.gpsimd
        def _(pool):
            pool.memset(g.identf[:, :], 0.0).then_inc(zeroed, 1)
            pool.memset(g.expo[:, :], -0.5).then_inc(zeroed, 1)
            pool.wait_ge(zeroed, 2)
            pool.affine_select(out=g.identf[:, :], in_=g.identf[:, :], compare_op=ALU.not_equal, fill=1.0, base=0,
                               pattern=[[-1, P]], channel_multiplier=1).then_inc(consts, 1)

            def rstd_of(n):
                pool.wait_ge(var_ready, n + 1)
                pool.tensor_tensor(rstd[:, :], ve[:, :], g.expo[:, :], ALU.pow).then_inc(rstd_ready, 1)

            def rope_sum(n):
                for k in range(2):
                    pool.wait_ge(rope_read, n * 4 + (2 * k + 2))
                    if not known(n, 1):
                        pool.wait_ge(rest_ready, n)
                    pool.tensor_tensor(qk[:, k, :], tc[:, k, :], tsn[:, k, :], ALU.add).then_inc(q_ready, 1)

            def third(n, par):
                pool.wait_ge(p2_ready, n + 1)
                pool.tensor_tensor(parts[par][:, :, 2, :], rest[par][:, :, :], parts[par][:, :, 1, :], ALU.subtract).then_inc(split_done, 1)

            def body(n, par):
                if not is_last(n):
                    rstd_of(n + 1)
                rope_sum(n)
                if not known(n, 1):
                    third(n - 1, 1 - par)

            def between(n):
                if n == 1:
                    return
                pool.memset(g.identb[:, :], 0.0).then_inc(zeroed, 1)
                pool.memset(g.maskq[:, :], 0.0).then_inc(zeroed, 1)
                pool.wait_ge(zeroed, 4)
                pool.affine_select(out=g.identb[:, :], in_=g.identb[:, :], compare_op=ALU.not_equal, fill=1.0, base=0,
                                   pattern=[[-1, P]], channel_multiplier=1).then_inc(consts, 1)
                pool.affine_select(out=g.maskq[:, :], in_=g.maskq[:, :], compare_op=ALU.is_ge, fill=LOW, base=0,
                                   pattern=[[0, TPC], [-1, P]], channel_multiplier=1).then_inc(consts, 1)

            def zero_stack(i):
                pool.memset(g.stack[i][64:ROWS, :, :, :].rearrange("p a h t -> p (a h t)").bitcast(F32), 0.0).then_inc(g.st_zeroed, 1)
                pool.wait_ge(g.st_zeroed, i + 1)

            pool.wait_ge(consts, 1)
            zero_stack(0)
            rstd_of(0)
            pool.memset(g.V[:, :].rearrange("p (n w) -> p n w", w=VW)[:, :, HD_A:VW], 1.0).then_inc(ones_set, 1)
            pool.wait_ge(ones_set, 1)
            for i in range(1, 3):
                zero_stack(i)
            run(pool, body, between)
            third(NC - 1, 1)

        @block.scalar
        def _(act):
            act.dma_start(w3[:, :, :].rearrange("p k m -> p (k m)"), wqkv).then_inc(w_loaded, 16)
            for dst, k in ((cos, 0), (sin, 1)):
                act.dma_start(dst, tables[k, :, :].unsqueeze(1).broadcast_to([HD_A, HEADS, T])).then_inc(tab_loaded, 16)
            act.wait_ge(w_loaded, 16)
            by_dim = w3[:, 0:2, :].rearrange("p k (h i two) -> p k two i h", h=HEADS, two=2)
            straight = wqk[:, :, :].rearrange("p k (i two h) -> p k two i h", h=HEADS, two=2)
            rot = wrot[:, :, :].rearrange("p k (i two h) -> p k two i h", h=HEADS, two=2)
            for k in range(2):
                for odd in range(2):
                    act.copy(straight[:, k, odd, :, :], by_dim[:, k, odd, :, :])
                act.mul(rot[:, k, 0, :, :], by_dim[:, k, 1, :, :], -1.0)
                ins = act.copy(rot[:, k, 1, :, :], by_dim[:, k, 0, :, :])
            ins.then_inc(rot_ready, 1)

            def normal_T(n, par):
                act.wait_ge(xn_T, n + 1)
                if not known(n, 2):
                    act.wait_ge(v_mm, n - 1)
                act.copy(xnT[par][:, :], psT).then_inc(xnT_ready, 1)

            def values(n):
                act.wait_ge(v_mm, n + 1)
                vb = g.V[:, ds((n // 2) * (4 * VU) + (n % 2) * (TPC * G4 * VW), 3 * VU + TPC * G4 * VW)]
                for u in range(4):
                    dst = vb[:, u * VU:u * VU + TPC * G4 * VW].rearrange("p (t j w) -> p t j w", t=TPC, j=G4)[:, :, :, 0:HD_A]
                    src = psV.rearrange("p (t u j d) -> p t u j d", t=TPC, u=4, j=G4)[:, :, u, :, :]
                    ins = act.copy(dst, src)
                ins.then_inc(v_stored, 1)

            def first(n, par, k):
                act.wait_ge(q_ready, n * 2 + (k + 1))
                if not known(n, 2):
                    act.wait_ge(parts_stored[par], (n // 2) * 16)
                act.copy(parts[par][:, k, 0, :], qk[:, k, :]).then_inc(p1_ready, 1)

            def second(n, par):
                act.wait_ge(rest_ready, n + 1)
                act.copy(parts[par][:, :, 1, :], rest[par][:, :, :]).then_inc(p2_ready, 1)

            def body(n, par):
                if not known(n, 1):
                    second(n - 1, 1 - par)
                values(n)
                first(n, par, 0)
                if not is_last(n):
                    normal_T(n + 1, 1 - par)
                first(n, par, 1)

            def between(n):
                for k, dst in enumerate((g.wgT, g.wuT, g.wdT)):
                    if (k == 2) == (n == 1):
                        act.wait_ge(ffn_T, k + 1)
                        act.copy(dst[:, :], psW[:, (k % 2) * CH:(k % 2) * CH + HID]).then_inc(ffn_stored, 1)

            normal_T(0, 0)
            act.wait_ge(ones_set, 1)
            run(act, body, between)
            second(NC - 1, 1)

        @block.vector
        def _(dve):
            def stats(n):
                if known(n, 2):
                    dve.wait_ge(x_loaded[n], 16)
                elif isinstance(n, int) and n == 2:
                    dve.wait_ge(x_loaded[2], 16 * (B - 1))
                for t in range(TPC):
                    ins = dve.bn_stats(stat[:, t, :], g.X[:, ds(n * TPC + t, 1), :].rearrange("p a d -> p (a d)"))
                ins.then_inc(stats_done, 1)
                wait_alone(dve, stats_done, n + 1, g.seen_dve)
                for t in range(TPC):
                    ins = dve.bn_aggr(mv[:, t, :], stat[:, t, :])
                ins.then_inc(aggr_done, 1)
                dve.wait_ge(aggr_done, n + 1)
                dve.tensor_scalar_add(ve[:, :], mv[:, :, 1], EPS).then_inc(var_ready, 1)

            def norm(n):
                dve.wait_ge(rstd_ready, n + 1)
                if not known(n, 1):
                    dve.wait_ge(xn_T, n)
                for t in range(TPC):
                    ins = dve.tensor_scalar(xn[:, t, :], g.X[:, ds(n * TPC + t, 1), :].rearrange("p a d -> p (a d)"),
                                            mv[:, t, 0:1], rstd[:, t:t + 1], ALU.subtract, ALU.mult)
                ins.then_inc(xn_ready, 1)

            def rope(n):
                for j in range(4):
                    dve.wait_ge(qk_mm, n * 4 + (j + 1))
                    if not known(n, 1):
                        dve.wait_ge(q_ready, n * 2 + (j // 2 - 1))
                    dst, table = ((tc, cos), (tsn, sin))[j % 2]
                    dve.tensor_tensor(dst[:, j // 2, :], psQ[j], table[:, ds((n % 2) * CH, CH)], ALU.mult).then_inc(rope_read, 1)

            def split(n, par):
                dve.wait_ge(p1_ready, n * 2 + 2)
                if not known(n, 2):
                    dve.wait_ge(split_done, n - 1)
                dve.tensor_tensor(rest[par][:, :, :], qk[:, :, :], parts[par][:, :, 0, :], ALU.subtract).then_inc(rest_ready, 1)

            def body(n, par):
                if not is_last(n):
                    stats(n + 1)
                if not known(n, 1):
                    split(n - 1, 1 - par)
                rope(n)
                if not is_last(n):
                    norm(n + 1)

            def between(n):
                if n == 1:
                    return
                dve.wait_ge(int_loaded, 48)
                dve.tensor_scalar(wf[:, :, :], wi[:, :, :], W_SCALE, None, ALU.mult).then_inc(wf_ready, 1)
                dve.wait_ge(rel_loaded, 16)
                dve.memset(lrow[:, 0:RANGE], 0.0).then_inc(lrow_ready, 1)
                dve.tensor_scalar(lrow[:, RANGE:2 * RANGE], relrow[:, :], relrow[:, 0:1], None, ALU.subtract).then_inc(lrow_ready, 1)
                dve.memset(lrow[:, 2 * RANGE:LROW], LOW).then_inc(lrow_ready, 1)

            for k, word in enumerate((0.0, TWO_ONES)):
                dve.memset(g.zero_one[:, k, :].bitcast(F32), word).then_inc(g.zero_one_set, 1)
            stats(0)
            norm(0)
            dve.wait_ge(tab_loaded, 32)
            run(dve, body, between)
            split(NC - 1, 1)

        @block.tensor
        def _(pe):
            def transposed(n):
                pe.wait_ge(xn_ready, n + 1)
                if not known(n, 1):
                    pe.wait_ge(xnT_ready, n)
                for t in range(TPC):
                    ins = pe.transpose(psT[:, t * P:(t + 1) * P], xn[:, t, :], g.identf[:, :])
                ins.then_inc(xn_T, 1)

            def rotary(n, par):
                pe.wait_ge(xnT_ready, n + 1)
                for j in range(4):
                    if not known(n, 1):
                        pe.wait_ge(rope_read, n * 4 + (j - 3))
                    w = (wqk, wrot)[j % 2]
                    pe.matmul(psQ[j], w[:, j // 2, :], xnT[par][:, :], start=True, stop=True).then_inc(qk_mm, 1)

            def values(n, par):
                if not known(n, 1):
                    pe.wait_ge(v_stored, n)
                for t in range(TPC):
                    ins = pe.matmul(psV[:, t * P:(t + 1) * P], xnT[par][:, t * P:(t + 1) * P], w3[:, 2, :], start=True, stop=True)
                ins.then_inc(v_mm, 1)

            def body(n, par):
                rotary(n, par)
                values(n, par)
                if not is_last(n):
                    transposed(n + 1)

            def between(n):
                for k in range(3):
                    if (k == 2) == (n == 1):
                        if k == 0:
                            pe.wait_ge(wf_ready, 1)
                        if k == 2:
                            pe.wait_ge(ffn_stored, 1)
                        for t in range(NH):
                            ins = pe.transpose(psW[:, (k % 2) * CH + t * P:(k % 2) * CH + (t + 1) * P], wf[:, k, t * P:(t + 1) * P], g.identf[:, :])
                        ins.then_inc(ffn_T, 1)

            pe.wait_ge(consts, 1)
            transposed(0)
            pe.wait_ge(rot_ready, 1)
            run(pe, body, between)


DIAGONALS = [([(qt, qt, 1, qt % TPC) for qt in range(lo, lo + TPC)], [(0, TPC, 1, 0, lo)]) for lo in (0, TPC)]
BEFORE = [([(1, 0, 1, 0), (3, 0, 3, 1)], [(0, 1, 1, 1, 1), (1, 1, 3, 1, 3)]),
          ([(2, 0, 2, 0), (6, 4, 2, 2)], [(0, 1, 2, 1, 2), (2, 1, 2, 2, 6)]),
          ([(5, 4, 1, 0), (7, 4, 3, 1)], [(0, 1, 1, 2, 5), (1, 1, 3, 2, 7)])]
BEFORE += [([(qt, 0, TPC, 0)], [(0, 1, TPC, 1, qt)]) for qt in range(TPC, NQ)]
FIRST_PASS = DIAGONALS + BEFORE
KINDS = 3
SECOND_PASS = [(qc, kt, max(0, kt * P - qc * CH)) for qc in range(T // CH) for kt in range((qc + 1) * TPC)]
STEPS = len(SECOND_PASS)
DIAG_STEPS = [s for s, (qc, kt, _) in enumerate(SECOND_PASS) if kt >= qc * TPC]
TILES = G4 * len(FIRST_PASS)
RING = 3
assert TILES % RING == 0 and STEPS * G4 % RING == 0
IN_A_STEP = (0, "place", 1, "place", 2, "place", 3, "place", "product")
SLOTS_1 = IN_A_STEP.count("place")


LATER = 7
MAX_T = LATER + 1


def interleave():
    weight = [CH - off + P for _, _, off in SECOND_PASS for _ in range(SLOTS_1)]
    order = list(range(LATER * SLOTS_1, STEPS * SLOTS_1)) + list(range(LATER * SLOTS_1))
    out, at, seen = [None] * len(weight), 0, 0
    for place in order:
        seen += weight[place]
        upto = -(-TILES * seen // sum(weight))
        out[place] = (at, upto)
        at = upto
    return out


PLACES = interleave()
EARLY = PLACES[-1][1]


def rope_attention(nc, g, block, f):
    with ExitStack() as c:
        sb = lambda name, shape, dt=F32: c.enter_context(nc.sbuf_tensor(name, shape, dt))
        sem = lambda name: g.ctx.enter_context(nc.semaphore(name))
        stack, vu, mx, m_all, mneg, mrest, mrow, oT, o_raw, rden = (
            g.stack, g.vu, g.mx, g.m_all, g.mneg, g.mrest, g.mrow, g.oT, g.o_raw, g.rden)
        pt = [sb(f"probs{i}", [P, G4, CH]) for i in range(3)]

        st_loaded = g.st_loaded
        p1_done, p1_max = sem("p1_done"), sem("p1_max")
        joined, mneg1, mrest1, mneg2, mneg3, m_T, m_row, m_loaded = (
            sem("max_joined"), sem("mneg1"), sem("mrest1"), sem("mneg2"), sem("mneg3"), sem("m_T"), sem("m_row"), sem("m_loaded"))
        mx_set, diag_zeroed = sem("mx_set"), sem("diag_zeroed")
        v_unit, s2_done, exp_done, pv_done = sem("v_unit"), sem("s2_done"), sem("exp_done"), sem("pv_done")
        o_cleared, o_out, o_T, o_in, o_rden, o_norm = (
            sem("o_cleared"), sem("o_out"), sem("o_T"), sem("o_in"), sem("o_rden"), sem("o_norm"))

        g.o_norm = o_norm
        bank = lambda n, k=1: g.ps[:, n * CH:(n + k) * CH]
        psS = [bank(n) for n in range(RING)]
        ps1 = [bank(RING + n) for n in range(RING)]
        psO = bank(6)
        psX = bank(7)

        def q_side(i):
            return stack[i][:, 0, :, :]

        def k_side(i):
            return stack[i][:, 1, :, :]

        @block.sync
        def _(sp):
            for i in range(1, 3):
                sp.wait_ge(g.st_zeroed, i + 1)
                load_ones(sp, g, i)
                load_stack(sp, g, i, i)
            for par in range(2):
                sp.wait_ge(g.parts_stored[par], 16 * NC // 2)
            sp.wait_ge(g.lrow_stored, 16)
            sp.wait_ge(g.later_loaded, 48)

            def max_rows(u, i):
                sp.wait_ge(m_row, u + 1)
                sp.dma_start(q_side(i)[ROW_M:ROW_M + 3, :, :], mrow[:, :]).then_inc(m_loaded, 16)

            def half(u, i, ahead):
                if ahead:
                    max_rows(u + 1, (i + 1) % 3)
                sp.wait_ge(s2_done, G4 * STEPS * (u + 1))
                load_stack(sp, g, (u + 3) % UNITS, i)

            max_rows(0, 0)
            half(0, 0, True)
            with sp.Fori(0, (UNITS - 4) // 3) as v:
                for k in range(3):
                    half(v * 3 + (k + 1), (k + 1) % 3, True)
            half(UNITS - 3, (UNITS - 3) % 3, True)
            half(UNITS - 2, (UNITS - 2) % 3, True)
            sp.wait_ge(v_unit, UNITS)
            sp.wait_ge(o_norm, 2 * HEADS // G4)
            front_sync(sp, g, f, False)
            for i in range(3):
                sp.wait_ge(st_loaded[i], LOADS * 16 * len([u for u in range(UNITS + 2) if u % 3 == i]))

        @block.gpsimd
        def _(pool):
            def zero_above(u, first, last=False):
                for n, s in enumerate(DIAG_STEPS):
                    off = SECOND_PASS[s][2]
                    for x in range(2):
                        wait_alone(pool, exp_done, u * (G4 * STEPS) + (G4 * s + 2 * x + 2), g.seen_pool)
                        block_ = pt[s % 3][:, 2 * x:2 * x + 2, off:off + P]
                        pool.affine_select(out=block_, in_=block_, compare_op=ALU.is_ge, fill=0.0, base=0,
                                           pattern=[[0, 2], [1, P]], channel_multiplier=-1).then_inc(diag_zeroed, 1)
                    if n == 3 and not first:
                        normalise(u - 1, u * 2 - 1, 1)
                        if last:
                            front_gpsimd(pool, g, f, False)
                    if n == 5:
                        normalise(u, u * 2, 0)

            def normalise(u, n, qc):
                wait_alone(pool, o_rden, n + 1, g.seen_pool)
                first = (u // 4) * (NQ * D) + (u % 4) * (G4 * HD_A) + qc * (TPC * D)
                out = g.O[:, ds(first, TPC * D)].rearrange("p (t c) -> p t c", t=TPC)[:, :, 0:G4 * HD_A]
                pool.tensor_tensor(out.rearrange("p t (j d) -> p t j d", j=G4), o_raw[:, :, :, 0:HD_A],
                                   rden[:, :, :].unsqueeze(3).broadcast_to([P, TPC, G4, HD_A]), ALU.mult).then_inc(o_norm, 1)

            zero_above(0, True)
            with pool.Fori(1, UNITS - 1) as u:
                zero_above(u, False)
            pool.wait_ge(v_unit, UNITS)
            pool.wait_ge(g.later_loaded, 48)
            zero_above(UNITS - 1, False, True)
            normalise(UNITS - 1, 2 * UNITS - 1, 1)

        @block.scalar
        def _(act):
            def values(u, i):
                if not (isinstance(u, int) and u < 3):
                    act.wait_ge(pv_done, u * STEPS - (2 * STEPS - 1))
                act.copy(vu[i][:, :, :, :].rearrange("p t j w -> p (t j w)"), g.V[:, ds(u * VU, VU)]).then_inc(v_unit, 1)

            def o_back(n):
                act.wait_ge(o_T, n + 1)
                if not (isinstance(n, int) and n == 0):
                    act.wait_ge(o_norm, n)
                act.copy(o_raw[:, :, :, :], psX.rearrange("p (t j w) -> p t j w", t=TPC, j=G4)[:, :, :, 0:VW]).then_inc(o_in, 1)

            def o_evac(n, pv):
                act.wait_ge(pv_done, pv)
                if not (isinstance(n, int) and n == 0):
                    act.wait_ge(o_T, n)
                act.copy(oT[:, :], psO).then_inc(o_out, 1)

            def half(u, i, first, ahead):
                if ahead:
                    values(u + 1, (i + 1) % 3)
                for s, (qc, kt, off) in enumerate(SECOND_PASS):
                    for h in range(G4):
                        act.wait_ge(s2_done, u * (G4 * STEPS) + (G4 * s + h + 1))
                        if h == 0 and not (first and s < 3):
                            act.wait_ge(pv_done, u * STEPS + (s - 2))
                        act.activation(pt[s % 3][:, h, off:CH], psS[(G4 * s + h) % RING][:, off:CH], ACT.Exp,
                                       scale=float(HD_A) ** -0.5).then_inc(exp_done, 1)
                    if s == 0 and not first:
                        o_evac(u * 2 - 1, u * STEPS)
                    if s == 2 and not first:
                        o_back(u * 2 - 1)
                    if s == TPC + 2:
                        o_back(u * 2)
                    if s == TPC:
                        o_evac(u * 2, u * STEPS + TPC)
                    if ahead and s == MAX_T:
                        max_row(u + 1)
                    if not ahead and s == 4:
                        front_scalar_att(act, f)
                    if not ahead and s == 10:
                        front_scalar_normal(act, f)

            def max_row(u):
                act.wait_ge(m_T, u + 1)
                act.wait_ge(m_loaded, 16 * u)
                act.copy(mrow[:, :], psX[0:3 * G4 * NQ, 0:P // 2].bitcast(BF16)).then_inc(m_row, 1)

            act.wait_ge(g.v_in_place, NC)
            act.copy(vu[0][:, :, :, :].rearrange("p t j w -> p (t j w)"), g.V[:, 0:VU]).then_inc(v_unit, 1)
            act.wait_ge(g.split_done, NC)
            max_row(0)
            half(0, 0, True, True)
            with act.Fori(0, (UNITS - 4) // 3) as v:
                for k in range(3):
                    half(v * 3 + (k + 1), (k + 1) % 3, False, True)
            half(UNITS - 3, (UNITS - 3) % 3, False, True)
            half(UNITS - 2, (UNITS - 2) % 3, False, True)
            half(UNITS - 1, (UNITS - 1) % 3, False, False)
            o_evac(2 * UNITS - 1, UNITS * STEPS)
            o_back(2 * UNITS - 1)

        @block.vector
        def _(dve):
            def banks(u, lo, hi):
                for n in range(lo, hi):
                    h, (_, reductions) = n // len(FIRST_PASS), FIRST_PASS[n % len(FIRST_PASS)]
                    dve.wait_ge(p1_done, u * TILES + (n + 1))
                    for col, tiles, w, kind, qt in reductions:
                        src = ps1[n % RING][:, col * P:(col + tiles * w) * P].rearrange("p (t k) -> p t k", t=tiles)
                        ins = dve.reduce_max(mx[:, kind, h, qt:qt + tiles], src, AX.X)
                    ins.then_inc(p1_max, 1)

            def split_max(u):
                dve.wait_ge(p1_max, TILES * (u + 1))
                dve.reduce_max(m_all[:, :], mx[:, :, :, :].rearrange("p k h q -> p (h q) k"), AX.X).then_inc(joined, 1)
                dve.wait_ge(joined, u + 1)
                m = m_all[:, :]
                if not (isinstance(u, int) and u == 0):
                    dve.wait_ge(m_T, u)
                dve.tensor_scalar(mneg[:, 0, :], m, -1.0, None, ALU.mult).then_inc(mneg1, 1)
                dve.wait_ge(mneg1, u + 1)
                dve.scalar_tensor_tensor(mrest[:, :], m, -1.0, mneg[:, 0, :], ALU.mult, ALU.subtract).then_inc(mrest1, 1)
                dve.wait_ge(mrest1, u + 1)
                dve.tensor_copy(mneg[:, 1, :], mrest[:, :]).then_inc(mneg2, 1)
                dve.wait_ge(mneg2, u + 1)
                dve.tensor_tensor(mneg[:, 2, :], mrest[:, :], mneg[:, 1, :], ALU.subtract).then_inc(mneg3, 1)

            def reciprocal(n):
                dve.wait_ge(o_in, n + 1)
                dve.reciprocal(rden[:, :, :], o_raw[:, :, :, HD_A]).then_inc(o_rden, 1)

            def half(u, first, ahead=True, after=True):
                for s in range(STEPS):
                    if ahead and s == LATER:
                        split_max(u + 1)
                    for slot in range(SLOTS_1):
                        if ahead if s < LATER else after:
                            banks(u + 1 if s < LATER else u + 2, *PLACES[s * SLOTS_1 + slot])
                        if slot == 0:
                            if s == 3 and not first:
                                reciprocal(u * 2 - 1)
                            if s == TPC + 3:
                                reciprocal(u * 2)
                    if not ahead and s == 5:
                        front_vector_stream(dve, g, f, False)
                    if not ahead and s == 8:
                        front_vector_normal(dve, f)

            dve.memset(mx[:, :, :, :], LOW).then_inc(mx_set, 1)
            dve.wait_ge(mx_set, 1)
            dve.wait_ge(g.ffn_in_place, 3)
            dve.memset(psO, 0.0).then_inc(o_cleared, 1)
            banks(0, 0, TILES)
            split_max(0)
            banks(1, 0, EARLY)
            half(0, True)
            with dve.Fori(0, (UNITS - 4) // 3) as v:
                for k in range(3):
                    half(v * 3 + (k + 1), False)
            half(UNITS - 3, False)
            half(UNITS - 2, False, True, False)
            half(UNITS - 1, False, False, False)
            reciprocal(2 * UNITS - 1)

        @block.tensor
        def _(pe):
            def loaded(i, n):
                pe.wait_ge(st_loaded[i], n * (LOADS * 16))

            def scores1(u, i, lo, hi):
                for n in range(lo, hi):
                    h, (products, _) = n // len(FIRST_PASS), FIRST_PASS[n % len(FIRST_PASS)]
                    diagonal = n % len(FIRST_PASS) < len(DIAGONALS)
                    if not (isinstance(u, int) and u == 0 and n < RING):
                        pe.wait_ge(p1_max, u * TILES + (n + 1 - RING))
                    if diagonal:
                        pe.matmul(ps1[n % RING], g.identb[:, :], g.maskq[:, :], start=True, stop=False)
                    for qt, k0, w, col in products:
                        ins = pe.matmul(ps1[n % RING][:, col * P:(col + w) * P], q_side(i)[:, h, qt * P:(qt + 1) * P],
                                        k_side(i)[:, h, k0 * P:(k0 + w) * P], start=not diagonal,
                                        stop=not diagonal or qt == products[-1][0])
                    ins.then_inc(p1_done, 1)

            def scores2(u, i, s, h, first):
                qc, kt, off = SECOND_PASS[s]
                n = G4 * s + h
                if not (first and n < RING):
                    pe.wait_ge(exp_done, u * (G4 * STEPS) + (n + 1 - RING))
                pe.matmul(psS[n % RING][:, off:CH], k_side(i)[:, h, kt * P:(kt + 1) * P], q_side(i)[:, h, qc * CH + off:(qc + 1) * CH],
                          start=True, stop=True).then_inc(s2_done, 1)

            def weighted(u, i, s, first):
                qc, kt, off = SECOND_PASS[s]
                last = (qc + 1) * TPC - 1
                if s in DIAG_STEPS:
                    pe.wait_ge(diag_zeroed, u * (2 * len(DIAG_STEPS)) + 2 * (DIAG_STEPS.index(s) + 1))
                else:
                    pe.wait_ge(exp_done, u * (G4 * STEPS) + G4 * (s + 1))
                if s == 0:
                    pe.wait_ge(v_unit, u + 1)
                if kt == 0 and not (first and s == 0):
                    pe.wait_ge(o_out, u * 2 + qc)
                for h in range(G4):
                    ins = pe.matmul(psO[32 * h:32 * h + VW, off:CH], vu[i][:, kt, h, :], pt[s % 3][:, h, off:CH],
                                    start=kt == 0, stop=kt == last)
                ins.then_inc(pv_done, 1)

            def o_transposed(n, others):
                pe.wait_ge(o_out, n + 1)
                others()
                for t in range(TPC):
                    ins = pe.transpose(psX[:, t * P:(t + 1) * P], oT[:, t * P:(t + 1) * P], g.identf[:, :])
                ins.then_inc(o_T, 1)

            def max_transposed(u):
                pe.wait_ge(mneg3, u + 1)
                if not (isinstance(u, int) and u == 0):
                    pe.wait_ge(o_in, 2 * u - 1)
                pe.transpose(psX[0:3 * G4 * NQ, 0:P // 2].bitcast(BF16), mneg[:, :, :].rearrange("p s n -> p (s n)"), g.identb[:, :]).then_inc(m_T, 1)

            def half(u, i, first, ahead=True, after=True, filled=0):
                pe.wait_ge(m_loaded, 16 * (u + 1))
                for s in range(STEPS):
                    place = 0
                    for what in IN_A_STEP:
                        if isinstance(what, int):
                            scores2(u, i, s, what, first)
                        elif what == "product" and s > 0:
                            weighted(u, i, s - 1, first)
                        elif what == "product" and not first:
                            weighted(u - 1, (i + 2) % 3, STEPS - 1, False)
                        elif what == "place":
                            if ahead and s < LATER:
                                scores1(u + 1, (i + 1) % 3, *PLACES[s * SLOTS_1 + place])
                            elif after and s >= LATER:
                                if s == LATER and place == 0:
                                    loaded((i + 2) % 3, filled)
                                scores1(u + 2, (i + 2) % 3, *PLACES[s * SLOTS_1 + place])
                            place += 1
                    if s == 1 and not first:
                        o_transposed(u * 2 - 1, lambda: pe.wait_ge(m_row, u + 1))
                    if s == TPC + 1:
                        o_transposed(u * 2, (lambda: pe.wait_ge(m_row, u + 1)) if first else (lambda: pe.wait_ge(o_in, u * 2)))
                    if ahead and s == MAX_T:
                        max_transposed(u + 1)
                    if not ahead and s == 2:
                        pe.wait_ge(p1_max, UNITS * TILES)
                        front_tensor_att(pe, g, f)
                    if not ahead and s == 5:
                        front_tensor_projected(pe, g, f)
                    if not ahead and s == 9:
                        front_tensor_normal(pe, g, f)

            pe.wait_ge(g.qk_read, 4 * NC)
            pe.wait_ge(g.ffn_in_place, 3)
            pe.wait_ge(g.st_zeroed, 3)
            pe.wait_ge(o_cleared, 1)
            pe.wait_ge(g.consts, 3)
            loaded(0, 1)
            pe.wait_ge(g.ones_in[0], 16)
            scores1(0, 0, 0, TILES)
            pe.wait_ge(g.xnT_taken, NC)
            pe.wait_ge(g.v_in_place, NC)
            max_transposed(0)
            loaded(1, 1)
            for i in range(1, 3):
                pe.wait_ge(g.ones_in[i], 16)
            scores1(1, 1, 0, EARLY)
            half(0, 0, True, filled=1)
            with pe.Fori(0, (UNITS - 4) // 3) as v:
                for k in range(3):
                    half(v * 3 + (k + 1), (k + 1) % 3, False, filled=v + ((k + 3) // 3 + 1))
            half(UNITS - 3, (UNITS - 3) % 3, False, filled=(UNITS - 1) // 3 + 1)
            half(UNITS - 2, (UNITS - 2) % 3, False, True, False)
            half(UNITS - 1, (UNITS - 1) % 3, False, False, False)
            weighted(UNITS - 1, (UNITS - 1) % 3, STEPS - 1, False)
            o_transposed(2 * UNITS - 1, lambda: pe.wait_ge(o_in, 2 * UNITS - 1))


def ffn_buffers(nc, g, second, c, room, hidden_room):
    class f:
        pass
    tag = "2" if second else "1"
    sem = lambda name: g.ctx.enter_context(nc.semaphore(name + tag))
    stats = c.enter_context(nc.sbuf_tensor("f_stats" + tag, [P, 2, TPC * 10], F32))

    def cut(room, sizes):
        ends = [sum(sizes[:n]) for n in range(len(sizes) + 1)]
        return [room[:, lo:hi] for lo, hi in zip(ends, ends[1:])]

    tiles = f.tiles = lambda ap: ap.rearrange("p (t d) -> p t d", t=TPC)
    att, xb, xc0, xc1, x2, xn, xnT, *more = cut(room, [CH] * (7 if second else 9))
    f.att, f.xb, f.xc, f.x2, f.xn, f.xnT = att, tiles(xb), [tiles(xc0), tiles(xc1)], tiles(x2), tiles(xn), xnT
    if not second:
        f.attT, f.xe = more[0], tiles(more[1])
    gate, h, y = cut(hidden_room, (2 * CH, NH * CH, CH))
    f.gate, f.h, f.y = gate.rearrange("p (j t) -> p j t", j=2), h.rearrange("p (j t) -> p j t", j=NH), y
    small = [cut(stats[:, k, :], (TPC * 6, TPC * 2, TPC, TPC)) for k in range(2)]
    (f.stat, f.mv, f.ve, f.rstd), (f.stat2, f.mv2, f.ve2, f.rstd2) = [
        (st.rearrange("p (t s) -> p t s", t=TPC), mv.rearrange("p (t s) -> p t s", t=TPC), ve, rstd) for st, mv, ve, rstd in small]

    f.att_loaded, f.att_T, f.attT_ready, f.added_mm, f.xb_ready = (
        sem("att_loaded"), sem("att_T"), sem("attT_ready"), sem("added_mm"), sem("xb_ready"))
    f.xc_ready, f.stats_done, f.aggr_done, f.var_ready, f.rstd_ready, f.xn_ready = (
        sem("xc_ready"), sem("f_stats"), sem("f_aggr"), sem("f_var"), sem("f_rstd"), sem("f_xn"))
    f.xn_T, f.xnT_ready, f.gate_mm, f.up_mm, f.silu_done, f.h_ready = (
        sem("f_xn_T"), sem("f_xnT"), sem("gate_mm"), sem("up_mm"), sem("silu_done"), sem("h_ready"))
    f.y_mm, f.y_ready, f.y_T, f.x2_ready, f.x_kept = sem("y_mm"), sem("y_ready"), sem("y_T"), sem("x2_ready"), sem("x_kept")
    f.stats2_done, f.aggr2_done, f.var2_ready, f.rstd2_ready, f.xe_ready, f.xe_T, f.xeT_ready = (
        sem("e_stats"), sem("e_aggr"), sem("e_var"), sem("e_rstd"), sem("e_xn"), sem("e_T"), sem("e_xnT"))
    bank = lambda n: g.ps[:, n * CH:(n + 1) * CH]
    f.psA, f.psT = (bank(0), bank(1)) if second else (bank(3), bank(4))
    f.psG, f.psU = ([bank(2), bank(3)], [bank(4), bank(5)]) if second else ([bank(0), bank(1)], [bank(2), bank(5)])
    f.psY, f.psF = bank(6), bank(7)
    return f


def front_sync(sp, g, f, second):
    sp.dma_start(f.att[:, :], (g.yT if second else g.O)[:, 0:CH]).then_inc(f.att_loaded, 16)


def front_gpsimd(pool, g, f, second):
    pool.tensor_tensor(f.xb[:, :, :], g.X[:, 0:TPC, :], (g.bo_b if second else g.bo_a)[:, :].unsqueeze(1).broadcast_to([P, TPC, P]),
                       ALU.add).then_inc(f.xb_ready, 1)
    pool.wait_ge(f.var_ready, 1)
    pool.tensor_tensor(f.rstd[:, :], f.ve[:, :], g.expo[:, :], ALU.pow).then_inc(f.rstd_ready, 1)


def front_scalar_att(act, f):
    act.wait_ge(f.att_T, 1)
    act.copy(f.attT[:, :], f.psA).then_inc(f.attT_ready, 1)


def front_scalar_normal(act, f):
    act.wait_ge(f.xn_T, 1)
    act.copy(f.xnT[:, :], f.psT).then_inc(f.xnT_ready, 1)


def front_vector_stream(dve, g, f, second):
    dve.wait_ge(f.att_T if second else f.added_mm, 1)
    dve.wait_ge(f.xb_ready, 1)
    dve.tensor_tensor(f.xc[0][:, :, :], f.tiles(f.psA), f.xb[:, :, :], ALU.add).then_inc(f.xc_ready, 1)
    dve.wait_ge(f.xc_ready, 1)
    for t in range(TPC):
        ins = dve.bn_stats(f.stat[:, t, :], f.xc[0][:, t, :])
    ins.then_inc(f.stats_done, 1)
    wait_alone(dve, f.stats_done, 1, g.seen_dve)
    for t in range(TPC):
        ins = dve.bn_aggr(f.mv[:, t, :], f.stat[:, t, :])
    ins.then_inc(f.aggr_done, 1)
    dve.wait_ge(f.aggr_done, 1)
    dve.tensor_scalar_add(f.ve[:, :], f.mv[:, :, 1], EPS).then_inc(f.var_ready, 1)


def front_vector_normal(dve, f):
    dve.wait_ge(f.rstd_ready, 1)
    for t in range(TPC):
        ins = dve.tensor_scalar(f.xn[:, t, :], f.xc[0][:, t, :], f.mv[:, t, 0:1], f.rstd[:, t:t + 1], ALU.subtract, ALU.mult)
    ins.then_inc(f.xn_ready, 1)


def front_tensor_att(pe, g, f):
    pe.wait_ge(f.att_loaded, 16)
    for t in range(TPC):
        ins = pe.transpose(f.psA[:, t * P:(t + 1) * P], f.att[:, t * P:(t + 1) * P], g.identf[:, :])
    ins.then_inc(f.att_T, 1)


def front_tensor_projected(pe, g, f):
    pe.wait_ge(f.attT_ready, 1)
    for t in range(TPC):
        ins = pe.matmul(f.psA[:, t * P:(t + 1) * P], f.attT[:, t * P:(t + 1) * P], g.wo_a[:, :], start=True, stop=True)
    ins.then_inc(f.added_mm, 1)


def front_tensor_normal(pe, g, f):
    pe.wait_ge(f.xn_ready, 1)
    for t in range(TPC):
        ins = pe.transpose(f.psT[:, t * P:(t + 1) * P], f.xn[:, t, :], g.identf[:, :])
    ins.then_inc(f.xn_T, 1)


def ffn(nc, g, block, second, out, f, pair_weights=None):
    bias = g.bo_b if second else g.bo_a

    def run(body):
        def numbered(eng):
            for n in range(2):
                body(n, n)
            with eng.Fori(0, (NC - 4) // 2) as v:
                for k in range(2):
                    body(v * 2 + (k + 2), k)
            for n in range(NC - 2, NC):
                body(n, n % 2)
        return numbered

    def known(n, least):
        return isinstance(n, int) and n < least

    def is_last(n):
        return isinstance(n, int) and n == NC - 1

    @block.sync
    def _(sp):
        def load(n):
            if not known(n, 1):
                sp.wait_ge(f.att_T, n)
            src = g.yT if second else g.O
            sp.dma_start(f.att[:, :], src[:, ds(n * CH, CH)]).then_inc(f.att_loaded, 16)

        def keep(n):
            sp.wait_ge(f.x2_ready, n + 1)
            if second:
                dst = tok_tiles(out)[:, ds(n * TPC, TPC), :]
                sp.dma_start(dst, f.x2[:, :, :]).then_inc(f.x_kept, 16)
            else:
                sp.dma_start(g.X[:, ds(n * TPC, TPC), :], f.x2[:, :, :]).then_inc(f.x_kept, 16)

        def body(n, i):
            if not known(n, 1):
                keep(n - 1)
            if not (isinstance(n, int) and n + 2 >= NC):
                load(n + 2)

        load(1)
        if second:
            sp.wait_ge(g.job_free, g.all_jobs)
        else:
            sp.wait_ge(g.o_norm, 2 * UNITS)
        run(body)(sp)
        if not second:
            load_first_pair(sp, g, f, *pair_weights)
        keep(NC - 1)
        sp.wait_ge(f.x_kept, 16 * NC)

    @block.gpsimd
    def _(pool):
        def with_bias(n):
            if not known(n, 1):
                pool.wait_ge(f.xc_ready, n)
            pool.tensor_tensor(f.xb[:, :, :], g.X[:, ds(n * TPC, TPC), :],
                               bias[:, :].unsqueeze(1).broadcast_to([P, TPC, P]), ALU.add).then_inc(f.xb_ready, 1)

        def rstd_of(n):
            pool.wait_ge(f.var_ready, n + 1)
            pool.tensor_tensor(f.rstd[:, :], f.ve[:, :], g.expo[:, :], ALU.pow).then_inc(f.rstd_ready, 1)

        def end_rstd_of(n):
            pool.wait_ge(f.var2_ready, n + 1)
            pool.tensor_tensor(f.rstd2[:, :], f.ve2[:, :], g.expo[:, :], ALU.pow).then_inc(f.rstd2_ready, 1)

        def body(n, i):
            if not is_last(n):
                with_bias(n + 1)
            if not second and not known(n, 1):
                end_rstd_of(n - 1)
            if not is_last(n):
                rstd_of(n + 1)

        run(body)(pool)

    @block.scalar
    def _(act):
        def att_back(n):
            if not second:
                act.wait_ge(f.att_T, n + 1)
                if not known(n, 1):
                    act.wait_ge(f.added_mm, n)
                act.copy(f.attT[:, :], f.psA).then_inc(f.attT_ready, 1)

        def normal_back(n):
            act.wait_ge(f.xn_T, n + 1)
            act.copy(f.xnT[:, :], f.psT).then_inc(f.xnT_ready, 1)

        def end_back(n):
            act.wait_ge(f.xe_T, n + 1)
            act.copy(g.xnT[:, ds(n * CH, CH)], f.psA).then_inc(f.xeT_ready, 1)

        def silu(n, j):
            act.wait_ge(f.gate_mm, n * NH + (j + 1))
            if not (known(n, 1) and j < 2):
                act.wait_ge(f.h_ready, n * NH + (j - 1 if j else 0))
            act.activation(f.gate[:, j % 2, :], f.psG[j % 2], ACT.Silu).then_inc(f.silu_done, 1)

        def body(n, i):
            silu(n, 0)
            if not is_last(n):
                att_back(n + 1)
            silu(n, 1)
            silu(n, 2)
            act.wait_ge(f.y_mm, n + 1)
            act.copy(f.y[:, :], f.psY).then_inc(f.y_ready, 1)
            if not is_last(n):
                normal_back(n + 1)
            if not second and not known(n, 1):
                end_back(n - 1)

        run(body)(act)

    @block.vector
    def _(dve):
        def stats(x, st, done):
            for t in range(TPC):
                ins = dve.bn_stats(st[:, t, :], x[:, t, :])
            ins.then_inc(done, 1)

        def variance(n, st, m, v, s1, s2, s3):
            wait_alone(dve, s1, n + 1, g.seen_dve)
            for t in range(TPC):
                ins = dve.bn_aggr(m[:, t, :], st[:, t, :])
            ins.then_inc(s2, 1)
            dve.wait_ge(s2, n + 1)
            dve.tensor_scalar_add(v[:, :], m[:, :, 1], EPS).then_inc(s3, 1)

        def norm(dst, x, m, r, done):
            for t in range(TPC):
                ins = dve.tensor_scalar(dst[:, t, :], x[:, t, :], m[:, t, 0:1], r[:, t:t + 1], ALU.subtract, ALU.mult)
            ins.then_inc(done, 1)

        def middle(n, i):
            dve.wait_ge(f.att_T if second else f.added_mm, n + 1)
            dve.wait_ge(f.xb_ready, n + 1)
            if not known(n, 2):
                dve.wait_ge(f.x2_ready, n - 1)
            dve.tensor_tensor(f.xc[i][:, :, :], f.tiles(f.psA), f.xb[:, :, :], ALU.add).then_inc(f.xc_ready, 1)
            dve.wait_ge(f.xc_ready, n + 1)
            stats(f.xc[i], f.stat, f.stats_done)

        def middle_variance(n):
            variance(n, f.stat, f.mv, f.ve, f.stats_done, f.aggr_done, f.var_ready)

        def normal(n, i):
            dve.wait_ge(f.rstd_ready, n + 1)
            if not known(n, 1):
                dve.wait_ge(f.xn_T, n)
            norm(f.xn, f.xc[i], f.mv, f.rstd, f.xn_ready)

        def hidden(n, j):
            dve.wait_ge(f.silu_done, n * NH + (j + 1))
            dve.wait_ge(f.up_mm, n * NH + (j + 1))
            if j == 0 and not known(n, 1):
                dve.wait_ge(f.y_mm, n)
            dve.tensor_tensor(f.h[:, j, :], f.psU[j % 2], f.gate[:, j % 2, :], ALU.mult).then_inc(f.h_ready, 1)

        def end(n, i):
            dve.wait_ge(f.y_T, n + 1)
            if not known(n, 1):
                dve.wait_ge(f.x_kept, n * 16)
                if not second:
                    dve.wait_ge(f.xe_ready, n)
            dve.tensor_tensor(f.x2[:, :, :], f.tiles(f.psF), f.xc[i][:, :, :], ALU.add).then_inc(f.x2_ready, 1)
            if not second:
                dve.wait_ge(f.x2_ready, n + 1)
                stats(f.x2, f.stat2, f.stats2_done)
                variance(n, f.stat2, f.mv2, f.ve2, f.stats2_done, f.aggr2_done, f.var2_ready)

        def end_normal(n):
            dve.wait_ge(f.rstd2_ready, n + 1)
            if not known(n, 1):
                dve.wait_ge(f.xe_T, n)
            norm(f.xe, f.x2, f.mv2, f.rstd2, f.xe_ready)

        def body(n, i):
            hidden(n, 0)
            if not known(n, 1):
                end(n - 1, 1 - i)
            if not is_last(n):
                middle(n + 1, 1 - i)
            hidden(n, 1)
            if not is_last(n):
                middle_variance(n + 1)
            hidden(n, 2)
            if not is_last(n):
                normal(n + 1, 1 - i)
            if not second and not known(n, 1):
                end_normal(n - 1)

        run(body)(dve)
        end(NC - 1, 1)

    @block.tensor
    def _(pe):
        def att_transposed(n):
            pe.wait_ge(f.att_loaded, (n + 1) * 16)
            if not known(n, 1):
                pe.wait_ge(f.xc_ready, n)
                if not second and not known(n, 2):
                    pe.wait_ge(f.silu_done, n * NH - (NH - 1))
            for t in range(TPC):
                ins = pe.transpose(f.psA[:, t * P:(t + 1) * P], f.att[:, t * P:(t + 1) * P], g.identf[:, :])
            ins.then_inc(f.att_T, 1)

        def projected(n):
            if second:
                return
            pe.wait_ge(f.attT_ready, n + 1)
            for t in range(TPC):
                ins = pe.matmul(f.psA[:, t * P:(t + 1) * P], f.attT[:, t * P:(t + 1) * P], g.wo_a[:, :], start=True, stop=True)
            ins.then_inc(f.added_mm, 1)

        def normal_transposed(n):
            pe.wait_ge(f.xn_ready, n + 1)
            if not known(n, 1):
                pe.wait_ge(f.xnT_ready, n)
            for t in range(TPC):
                ins = pe.transpose(f.psT[:, t * P:(t + 1) * P], f.xn[:, t, :], g.identf[:, :])
            ins.then_inc(f.xn_T, 1)

        def end_transposed(n, middles):
            pe.wait_ge(f.xe_ready, n + 1)
            pe.wait_ge(f.xc_ready, middles)
            if not known(n, 1):
                pe.wait_ge(f.xeT_ready, n)
            for t in range(TPC):
                ins = pe.transpose(f.psA[:, t * P:(t + 1) * P], f.xe[:, t, :], g.identf[:, :])
            ins.then_inc(f.xe_T, 1)

        def y_transposed(n):
            pe.wait_ge(f.y_ready, n + 1)
            if not known(n, 1):
                pe.wait_ge(f.x2_ready, n)
            for t in range(TPC):
                ins = pe.transpose(f.psF[:, t * P:(t + 1) * P], f.y[:, t * P:(t + 1) * P], g.identf[:, :])
            ins.then_inc(f.y_T, 1)

        def gate_and_up(n, j, between=lambda: None):
            if not (known(n, 1) and j < 2):
                pe.wait_ge(f.silu_done, n * NH + (j - 1 if j else 0))
            pe.matmul(f.psG[j % 2], g.wgT[:, j * P:(j + 1) * P], f.xnT[:, :], start=True, stop=True).then_inc(f.gate_mm, 1)
            between()
            if not (known(n, 1) and j < 2):
                pe.wait_ge(f.h_ready, n * NH + (j - 1 if j else 0))
            pe.matmul(f.psU[j % 2], g.wuT[:, j * P:(j + 1) * P], f.xnT[:, :], start=True, stop=True).then_inc(f.up_mm, 1)

        def body(n, i):
            pe.wait_ge(f.xnT_ready, n + 1)
            gate_and_up(n, 0)
            if not known(n, 1):
                y_transposed(n - 1)
            if not second and not is_last(n):
                att_transposed(n + 1)
            gate_and_up(n, 1, lambda: None if is_last(n) else projected(n + 1))
            gate_and_up(n, 2)
            if not known(n, 1):
                pe.wait_ge(f.y_ready, n)
            for j in range(NH):
                pe.wait_ge(f.h_ready, n * NH + (j + 1))
                ins = pe.matmul(f.psY, g.wdT[:, j * P:(j + 1) * P], f.h[:, j, :], start=j == 0, stop=j == NH - 1)
            ins.then_inc(f.y_mm, 1)
            if not is_last(n):
                normal_transposed(n + 1)
            if second and not (isinstance(n, int) and n + 2 >= NC):
                att_transposed(n + 2)
            if not second and not known(n, 1):
                end_transposed(n - 1, NC if is_last(n) else n + 2)

        if second:
            att_transposed(1)
        run(body)(pe)
        y_transposed(NC - 1)


ORDER = [7, 0, 6, 1, 5, 2, 4, 3]
SLOTS = 4
GROUP = 4
GROUPS = [-(-(qt + 1) // GROUP) for qt in ORDER]
GROUPS_BEFORE = [2 * sum(GROUPS[:t]) for t in range(NQ + 1)]
JOBS = 6
JOB_AT = {0: 0, 1: 1, 3: 2, 5: 3, 7: 4, 9: JOBS, 11: 5, 13: JOBS + 1}
QX, QC, KA, KB, KC = range(5)
GATHERS = 10
PASSES = ((QX, KA), (QX, KB), (QC, KC))


def end_gpsimd(pool, g, f):
    pool.wait_ge(f.var2_ready, NC)
    pool.tensor_tensor(f.rstd2[:, :], f.ve2[:, :], g.expo[:, :], ALU.pow).then_inc(f.rstd2_ready, 1)


def end_vector(dve, f):
    dve.wait_ge(f.rstd2_ready, NC)
    dve.wait_ge(f.xe_T, NC - 1)
    for t in range(TPC):
        ins = dve.tensor_scalar(f.xe[:, t, :], f.x2[:, t, :], f.mv2[:, t, 0:1], f.rstd2[:, t:t + 1], ALU.subtract, ALU.mult)
    ins.then_inc(f.xe_ready, 1)


def end_tensor(pe, g, f):
    pe.wait_ge(f.xe_ready, NC)
    pe.wait_ge(f.xc_ready, NC)
    pe.wait_ge(f.xeT_ready, NC - 1)
    for t in range(TPC):
        ins = pe.transpose(f.psA[:, t * P:(t + 1) * P], f.xe[:, t, :], g.identf[:, :])
    ins.then_inc(f.xe_T, 1)


def end_scalar(act, g, f):
    act.wait_ge(f.xe_T, NC)
    act.copy(g.xnT[:, (NC - 1) * CH:NC * CH], f.psA).then_inc(f.xeT_ready, 1)


def load_first_pair(sp, g, f, wq, wk, wv, wo):
    for k, w in enumerate((wq, wk, wv)):
        sp.dma_start(g.w_pair[:, k, :], w[:, 0:P]).then_inc(g.w_pair_loaded, 16)
    sp.wait_ge(f.xeT_ready, T // CH)
    sp.dma_start(g.batch_xT[:, :], g.xnT[:, 0:T]).then_inc(g.batch_xT_loaded, 16)
    sp.dma_start(g.wo_pair[:, :], wo[0:P, :]).then_inc(g.wo_pair_loaded, 16)


def bias_attention(nc, g, block, wq, wk, wv, wo, room, ffn1, f):
    with ExitStack() as c:
        sb = lambda name, shape, dt=F32: c.enter_context(nc.sbuf_tensor(name, shape, dt))
        sem = lambda name: g.ctx.enter_context(nc.semaphore(name))
        w3, wo_p, xT = g.w_pair, g.wo_pair, g.batch_xT
        nat = g.parts_room.bitcast(BF16).rearrange("p (s t) -> p s t", s=6)
        rest = sb("pair_rest", [P, 2, CH])
        stack = [sb(f"pair_stack{i}", [P, 2, 5, T], BF16) for i in range(2)]
        cut = lambda lo, n: room[:, lo:lo + n]
        sc = cut(0, SLOTS * 2 * T).rearrange("p (s h k) -> p s h k", s=SLOTS, h=2)
        oT = [cut((SLOTS * 2 + i) * T, T) for i in range(2)]
        v = [sb("pair_v0", [P, NQ, P]), cut((SLOTS * 2 + 2) * T, T).rearrange("p (n d) -> p n d", n=NQ)]
        band = [sb(f"band{i}", [P, 2, T]) for i in range(2)]
        pT = [sb(f"probsT{i}", [P, 2, NQ, P]) for i in range(2)]
        mx = sb("b_max", [P, SLOTS, 2])
        mneg = sb("b_neg_max", [P, SLOTS, 2])
        den = sb("b_den", [P, SLOTS, 2])
        rden = sb("b_rden", [P, SLOTS, 2])

        w_loaded, wo_loaded, xT_loaded = g.w_pair_loaded, g.wo_pair_loaded, g.batch_xT_loaded
        st_loaded = [sem(f"b_st_loaded{i}") for i in range(2)]
        band_loaded = [sem(f"band_loaded{i}") for i in range(2)]
        band_zeroed, y_zeroed = sem("band_zeroed"), sem("y_zeroed")
        job_mm, job_free = sem("job_mm"), sem("job_free")
        p1_ready, p2_ready, p3_ready = sem("b_p1"), sem("b_p2"), sem("b_p3")
        s_done, max_done, neg_done, exp_done, rden_done, norm_done = (
            sem("b_scores"), sem("b_max_done"), sem("b_neg_done"), sem("b_exp"), sem("b_rden_done"), sem("b_norm"))
        t_done, pv_done, o_out = sem("b_transposed"), sem("b_pv"), sem("b_o_out")
        t_out = [sem("b_t_out_act"), sem("b_t_out_dve")]
        g.job_free, g.all_jobs = job_free, (JOBS + 2) * ITERS
        psS = [g.ps[:, 0:T], g.ps[:, T:2 * T]]
        psT = [g.ps[:, 2 * T:2 * T + CH], g.ps[:, 2 * T + CH:3 * T]]
        psO = g.ps[:, 3 * T:3 * T + CH]
        psJ = g.ps[:, 3 * T + CH:4 * T]
        psF = psT + [psO]
        TILES2 = 2 * NQ
        NG = GROUPS_BEFORE[NQ]

        def jobs_before(i):
            if isinstance(i, int):
                return JOBS if i == 0 else (JOBS + 2) * i + JOBS - 2
            return i * (JOBS + 2) + (JOBS - 2)

        def jobs_of(first, ahead):
            found = [(at, k) for at, k in sorted(JOB_AT.items()) if (ahead if k < JOBS else not first)]
            return {at: (k, n + 1) for n, (at, k) in enumerate(found)}

        def done_with(k, first):
            return next(n for j, n in jobs_of(first, True).values() if j == k)

        def pv_free(i, t):
            return max(0, NQ * i + t - 1) if isinstance(i, int) else i * NQ + (t - 1)

        def run(eng, body):
            body(0, 0, True, True)
            with eng.Fori(0, (ITERS - 2) // 2) as n:
                for k in range(2):
                    body(n * 2 + (k + 1), (k + 1) % 2, False, True)
            body(ITERS - 1, (ITERS - 1) % 2, False, False)


        @block.sync
        def _(sp):
            def load_w(i):
                cols = ds((i % PAIRS) * P, P)
                for k, w in enumerate((wq, wk, wv)):
                    sp.dma_start(w3[:, k, :], w[:, cols]).then_inc(w_loaded, 16)
                sp.dma_start(xT[:, :], g.xnT[:, ds(((i % ITERS) // PAIRS) * T, T)]).then_inc(xT_loaded, 16)

            def load_wo(i):
                sp.dma_start(wo_p[:, :], wo[ds((i % PAIRS) * P, P), :]).then_inc(wo_loaded, 16)

            def load_band(i, par):
                for h in range(2):
                    src = g.lrep_flat[ds(((i % PAIRS) * 2 + h) * (P * LROW) + (P - 1), P * (LROW - 1))].rearrange("(q n) -> q n", n=LROW - 1)
                    sp.dma_start(band[par][:, h, T - 2 * P:T], src[:, 0:2 * P]).then_inc(band_loaded[par], 16)

            def gather(par, q_side):
                for h in range(2):
                    rows = slice(HD_B * h, HD_B * (h + 1))
                    top, low = stack[par][0:HD_B, h, :, :], stack[par][HD_B:P, h, :, :]
                    if q_side:
                        copies = ((top[:, QX:QC + 1, :], nat[rows, 0, :].unsqueeze(1).broadcast_to([HD_B, 2, T])),
                                  (low[:, QX:QC + 1, :], nat[rows, 1:3, :]))
                    else:
                        copies = ((top[:, KA:KC + 1, :], nat[rows, 3:6, :]), (low[:, KA:KB + 1, :], nat[rows, 3:5, :]),
                                  (low[:, KC, :], nat[rows, 3, :]))
                    for dst, src in copies:
                        sp.dma_start(dst, src).then_inc(st_loaded[par], 16)

            def next_pair(i, par, v_done):
                sp.wait_ge(p3_ready, i * 4 + 2)
                gather(par, True)
                sp.wait_ge(p3_ready, i * 4 + 4)
                gather(par, False)
                sp.wait_ge(job_mm, v_done)

            def body(i, par, first, ahead):
                if not ahead:
                    return
                if not first:
                    sp.wait_ge(max_done, i * TILES2)
                    sp.wait_ge(s_done, i * TILES2)
                load_band(i + 1, 1 - par)
                next_pair(i + 1, 1 - par, jobs_before(i) + done_with(5, first))
                load_w(i + 2)
                if not first:
                    sp.wait_ge(job_mm, jobs_before(i) + done_with(JOBS + 1, first))
                    load_wo(i)

            sp.wait_ge(band_zeroed, 2)
            load_band(0, 0)
            next_pair(0, 0, 6)
            load_w(1)
            run(sp, body)
            sp.wait_ge(xT_loaded, 16 * (ITERS + 1))
            sp.wait_ge(job_free, jobs_before(ITERS - 1))
            front_sync(sp, g, f, True)
            sp.wait_ge(job_mm, jobs_before(ITERS - 1) + 2)
            load_wo(ITERS - 1)
            sp.wait_ge(w_loaded, 48 * (ITERS + 1))
            sp.wait_ge(xT_loaded, 16 * (ITERS + 1))
            sp.wait_ge(wo_loaded, 16 * ITERS)
            for par in range(2):
                sp.wait_ge(band_loaded[par], 32 * ITERS // 2)

        @block.gpsimd
        def _(pool):
            def third(i, k):
                pool.wait_ge(p2_ready, i * 4 + (k + 1))
                x, half = k // 2, k % 2
                pool.tensor_tensor(nat[:, 3 * x + 2, half * CH:(half + 1) * CH], rest[:, half, :],
                                   nat[:, 3 * x + 1, half * CH:(half + 1) * CH], ALU.subtract).then_inc(p3_ready, 1)

            def divide(n, t):
                w = (ORDER[t % NQ] + 1) * P
                for h in range(2):
                    wait_alone(pool, rden_done, n + (h + 1), g.seen_pool)
                    p = sc[:, t % SLOTS, h, 0:w]
                    pool.tensor_scalar(p, p, rden[:, t % SLOTS, h:h + 1], 1.0, ALU.mult, ALU.mult).then_inc(norm_done, 1)

            def body(i, par, first, ahead):
                for t in range(NQ):
                    if t + 1 < NQ or ahead:
                        divide(i * TILES2 + 2 * (t + 1), t + 1)
                    if ahead and t < 4:
                        third(i + 1, t)

            for par in range(2):
                pool.memset(band[par][:, :, :], 0.0).then_inc(band_zeroed, 1)
            end_gpsimd(pool, g, ffn1)
            for k in range(4):
                third(0, k)
            divide(0, 0)
            run(pool, body)
            pool.wait_ge(xT_loaded, 16 * (ITERS + 1))
            front_gpsimd(pool, g, f, True)

        @block.scalar
        def _(act):
            def job_out(i, k, count, values, src=psJ):
                if k < JOBS:
                    act.wait_ge(job_mm, count)
                half = slice((k % 2) * CH, (k % 2 + 1) * CH)
                if k < 4:
                    if k == 0:
                        if not (isinstance(i, int) and i == 0):
                            act.wait_ge(st_loaded[0], gathered(0, i))
                            act.wait_ge(st_loaded[1], gathered(1, i))
                    act.copy(nat[:, 3 * (k // 2), half], src).then_inc(p1_ready, 1)
                elif k < JOBS:
                    act.copy(values[:, (k - 4) * TPC:(k - 3) * TPC, :].rearrange("p n d -> p (n d)"), src).then_inc(job_free, 1)

            def gathered(par, i):
                if par == 0:
                    return ((i + 1) // 2) * (GATHERS * 16)
                return (i // 2) * (GATHERS * 16)

            def exponent(n, t, h):
                w = (ORDER[t % NQ] + 1) * P
                act.wait_ge(neg_done, n + 1)
                p = sc[:, t % SLOTS, h, 0:w]
                act.activation(p, p, ACT.Exp, bias=mneg[:, t % SLOTS, h:h + 1], scale=1.0 / HD_B,
                               accum_out=den[:, t % SLOTS, h:h + 1]).then_inc(exp_done, 1)

            def evac(i, t, h, mine=0):
                g0 = GROUPS_BEFORE[t] + h * GROUPS[t]
                for q in range(GROUPS[t]):
                    if (g0 + q) % 2 != mine:
                        continue
                    nb = min(GROUP, ORDER[t] + 1 - q * GROUP)
                    act.wait_ge(t_done, i * NG + (g0 + q + 1))
                    act.wait_ge(pv_done, pv_free(i, t))
                    act.copy(pT[t % 2][:, h, q * GROUP:q * GROUP + nb, :].rearrange("p n q -> p (n q)"),
                             psT[(g0 + q) % 2][:, 0:nb * P]).then_inc(t_out[mine], 1)

            def body(i, par, first, ahead):
                base = jobs_before(i)
                jobs = jobs_of(first, ahead)
                for t in range(NQ):
                    for h in range(2):
                        if 2 * t + h in jobs:
                            k, n = jobs[2 * t + h]
                            job_out(i + 1, k, base + n, v[1 - par])
                        evac(i, t, h)
                        if t + 2 < NQ or ahead:
                            exponent(i * TILES2 + (2 * (t + 2) + h), t + 2, h)

            for k in range(JOBS):
                job_out(0, k, k + 1, v[0], psF[k % 3])
                if k == 3:
                    end_scalar(act, g, ffn1)
            for t in range(2):
                for h in range(2):
                    exponent(2 * t + h, t, h)
            run(act, body)
            front_scalar_normal(act, f)

        @block.vector
        def _(dve):
            def job_out(i, k, count, src=psJ):
                half = slice((k % 2) * CH, (k % 2 + 1) * CH)
                x = k // 2
                if k < 4:
                    n = i * 4 + k
                    dve.wait_ge(p1_ready, n + 1)
                    dve.wait_ge(p3_ready, max(0, n - 1) if isinstance(n, int) else n - 1)
                    dve.tensor_tensor(rest[:, k % 2, :], src, nat[:, 3 * x, half], ALU.subtract).then_inc(job_free, 1)
                    dve.wait_ge(job_free, count)
                    dve.tensor_copy(nat[:, 3 * x + 1, half], rest[:, k % 2, :]).then_inc(p2_ready, 1)

            def y_out(i, half, count):
                dve.wait_ge(job_mm, count)
                y = g.yT[:, ds((i // PAIRS) * T + half * CH, CH)]
                dve.tensor_tensor(y, psJ, y, ALU.add).then_inc(job_free, 1)

            def maximum(n, t, h, par):
                w = (ORDER[t % NQ] + 1) * P
                slot = t % SLOTS
                wait_alone(dve, s_done, n + 1, g.seen_dve)
                dve.tensor_tensor_reduce(out=sc[:, slot, h, 0:w], in0=psS[h][:, 0:w], in1=band[par][:, h, T - w:T],
                                         scale=1.0, scalar=LOW, op0=ALU.add, op1=ALU.max,
                                         accum_out=mx[:, slot, h:h + 1]).then_inc(max_done, 1)
                dve.wait_ge(max_done, n + 1)
                dve.tensor_scalar(mneg[:, slot, h:h + 1], mx[:, slot, h:h + 1], -1.0 / HD_B, None, ALU.mult).then_inc(neg_done, 1)

            def reciprocal(n, t, h):
                dve.wait_ge(exp_done, n + 1)
                dve.reciprocal(rden[:, t % SLOTS, h:h + 1], den[:, t % SLOTS, h:h + 1]).then_inc(rden_done, 1)

            def evac(i, t, h, mine=1):
                g0 = GROUPS_BEFORE[t] + h * GROUPS[t]
                for q in range(GROUPS[t]):
                    if (g0 + q) % 2 != mine:
                        continue
                    nb = min(GROUP, ORDER[t] + 1 - q * GROUP)
                    dve.wait_ge(t_done, i * NG + (g0 + q + 1))
                    dve.wait_ge(pv_done, pv_free(i, t))
                    dve.tensor_copy(pT[t % 2][:, h, q * GROUP:q * GROUP + nb, :].rearrange("p n q -> p (n q)"),
                                    psT[(g0 + q) % 2][:, 0:nb * P]).then_inc(t_out[mine], 1)

            def o_evac(n, t, par):
                dve.wait_ge(pv_done, n + 1)
                qt = ORDER[t]
                dve.tensor_copy(oT[par][:, qt * P:(qt + 1) * P], psO[:, (t % GROUP) * P:(t % GROUP + 1) * P]).then_inc(o_out, 1)

            def body(i, par, first, ahead):
                base = jobs_before(i)
                jobs = jobs_of(first, ahead)
                for t in range(NQ):
                    after = t + 2 < NQ or ahead
                    band_par = par if t + 2 < NQ else 1 - par
                    if t + 1 < NQ or ahead:
                        for h in range(2):
                            reciprocal(i * TILES2 + (2 * (t + 1) + h), t + 1, h)
                    if ahead and t + 2 == NQ:
                        dve.wait_ge(band_loaded[1 - par], bands(i + 1))
                    for h in range(2):
                        if after:
                            maximum(i * TILES2 + (2 * (t + 2) + h), t + 2, h, band_par)
                        if 2 * t + h in jobs:
                            k, n = jobs[2 * t + h]
                            if k < JOBS:
                                job_out(i + 1, k, base + n)
                            else:
                                y_out(i - 1, k - JOBS, base + n)
                        evac(i, t, h)
                    if t > 0:
                        o_evac(i * NQ + (t - 1), t - 1, par)
                    elif not first:
                        o_evac(i * NQ - 1, NQ - 1, 1 - par)
                    if not ahead and t == NQ - 2:
                        front_vector_stream(dve, g, f, True)

            def bands(i):
                return (i // 2 + 1) * 32

            for k in range(4):
                job_out(0, k, k + 1, psF[k % 3])
                if k == 0:
                    end_vector(dve, ffn1)
            dve.memset(g.yT[:, :], 0.0).then_inc(y_zeroed, 1)
            dve.wait_ge(ffn1.x_kept, 16 * NC)
            dve.wait_ge(band_zeroed, 2)
            dve.wait_ge(band_loaded[0], 32)
            dve.wait_ge(y_zeroed, 1)
            for t in range(2):
                for h in range(2):
                    maximum(2 * t + h, t, h, 0)
            for h in range(2):
                reciprocal(h, 0, h)
            run(dve, body)
            front_vector_normal(dve, f)
            o_evac(ITERS * NQ - 1, NQ - 1, (ITERS - 1) % 2)
            for h in range(2):
                y_out(ITERS - 1, h, jobs_before(ITERS - 1) + 2 + h + 1)

        @block.tensor
        def _(pe):
            def job(i, k, before, dst=psJ):
                if k == 0:
                    pe.wait_ge(w_loaded, (i + 1) * 48)
                if k == 4:
                    pe.wait_ge(xT_loaded, (i + 1) * 16)
                if before is not None:
                    pe.wait_ge(job_free, before)
                if k < 4:
                    x = g.xnT[:, ds((i // PAIRS) * T + (k % 2) * CH, CH)]
                    ins = pe.matmul(dst, w3[:, k // 2, :], x, start=True, stop=True)
                else:
                    for n in range(TPC):
                        at = (k - 4) * CH + n * P
                        ins = pe.matmul(dst[:, n * P:(n + 1) * P], xT[:, at:at + P], w3[:, 2, :], start=True, stop=True)
                ins.then_inc(job_mm, 1)

            def out_job(i, par, half, count):
                if half == 0:
                    pe.wait_ge(wo_loaded, (i + 1) * 16)
                    pe.wait_ge(o_out, (i + 1) * NQ)
                pe.wait_ge(job_free, count)
                pe.matmul(psJ, wo_p[:, :], oT[par][:, half * CH:(half + 1) * CH], start=True, stop=True).then_inc(job_mm, 1)

            def scores(n, t, h, par, opening):
                qt = ORDER[t % NQ]
                w = (qt + 1) * P
                if not opening:
                    pe.wait_ge(max_done, n - 1)
                for lo in range(0, w, CH):
                    hi = min(w, lo + CH)
                    for p, (q, k) in enumerate(PASSES):
                        ins = pe.matmul(psS[h][:, lo:hi], stack[par][:, h, q, qt * P:(qt + 1) * P], stack[par][:, h, k, lo:hi],
                                        start=p == 0, stop=p == len(PASSES) - 1)
                ins.then_inc(s_done, 1)

            def transposed(i, t, h, first):
                pe.wait_ge(norm_done, i * TILES2 + (2 * t + h + 1))
                for q in range(GROUPS[t]):
                    n = GROUPS_BEFORE[t] + h * GROUPS[t] + q
                    if not (first and n < 2):
                        pe.wait_ge(t_out[n % 2], i * (NG // 2) + n // 2)
                    for b in range(q * GROUP, min(ORDER[t] + 1, (q + 1) * GROUP)):
                        ins = pe.transpose(psT[n % 2][:, (b % GROUP) * P:(b % GROUP + 1) * P], sc[:, t % SLOTS, h, b * P:(b + 1) * P], g.identf[:, :])
                    ins.then_inc(t_done, 1)

            def product(i, t, par, first):
                done = GROUPS_BEFORE[t + 1]
                pe.wait_ge(t_out[0], i * (NG // 2) + (done + 1) // 2)
                pe.wait_ge(t_out[1], i * (NG // 2) + done // 2)
                if not (first and t == 0):
                    pe.wait_ge(o_out, i * NQ + t)
                at = (t % GROUP) * P
                for b in range(ORDER[t] + 1):
                    for h in range(2):
                        ins = pe.matmul(psO[h * HD_B:(h + 1) * HD_B, at:at + P], v[par][:, b, h * HD_B:(h + 1) * HD_B], pT[t % 2][:, h, b, :],
                                        start=b == 0, stop=b == ORDER[t])
                ins.then_inc(pv_done, 1)

            def body(i, par, first, ahead):
                base = jobs_before(i)
                jobs = jobs_of(first, ahead)
                for t in range(NQ):
                    if ahead and t + 2 == NQ:
                        pe.wait_ge(st_loaded[1 - par], stacks(i + 1))
                    for h in range(2):
                        if t + 2 < NQ or ahead:
                            scores(i * TILES2 + (2 * (t + 2) + h), t + 2, h, par if t + 2 < NQ else 1 - par, False)
                        if 2 * t + h in jobs:
                            k, n = jobs[2 * t + h]
                            if k < JOBS:
                                job(i + 1, k, base + (n - 1))
                            else:
                                out_job(i - 1, 1 - par, k - JOBS, base + (n - 1))
                        transposed(i, t, h, first)
                    if t > 0:
                        product(i, t - 1, par, first)
                    elif not first:
                        product(i - 1, NQ - 1, 1 - par, False)
                    if not ahead and t == NQ - 3:
                        pe.wait_ge(max_done, ITERS * TILES2)
                        front_tensor_att(pe, g, f)

            def stacks(i):
                return (i // 2 + 1) * (GATHERS * 16)

            pe.wait_ge(ffn1.xeT_ready, T // CH)
            for k, before in enumerate((None, None, None, 1, 4, 4)):
                job(0, k, before, psF[k % 3])
                if k == 3:
                    end_tensor(pe, g, ffn1)
            pe.wait_ge(ffn1.xeT_ready, NC)
            pe.wait_ge(st_loaded[0], GATHERS * 16)
            for t in range(2):
                for h in range(2):
                    scores(2 * t + h, t, h, 0, t == 0)
            run(pe, body)
            front_tensor_normal(pe, g, f)
            product(ITERS - 1, NQ - 1, (ITERS - 1) % 2, False)
            for h in range(2):
                out_job(ITERS - 1, (ITERS - 1) % 2, h, jobs_before(ITERS - 1) + 2 + h)


def build(nc, x, wqkv, wo_a, bo_a, wq, wk, wv, wo_b, bo_b, rel, w_gate, w_up, w_down, out):
    with ExitStack() as ctx:
        class g:
            pass
        g.ctx = ctx
        g.seen_dve = ctx.enter_context(nc.semaphore("seen_dve"))
        g.seen_pool = ctx.enter_context(nc.semaphore("seen_pool"))
        g.consts = ctx.enter_context(nc.semaphore("consts"))
        sb = lambda name, shape, dt=F32: ctx.enter_context(nc.sbuf_tensor(name, shape, dt))
        g.ps = ctx.enter_context(nc.psum_tensor("ps", [P, 8 * CH], F32))
        g.X = sb("x_stream", [P, NT, P])
        g.identf = sb("identf", [P, P])
        g.identb = sb("identb", [P, P], BF16)
        g.expo = sb("minus_half", [P, TPC])
        g.wgT = sb("w_gateT", [P, HID])
        g.wuT = sb("w_upT", [P, HID])
        g.wdT = sb("w_downT", [P, HID])
        g.wo_a = sb("wo_a", [P, P])
        g.bo_a = sb("bo_a", [P, P])
        g.bo_b = sb("bo_b", [P, P])
        g.st_zeroed = ctx.enter_context(nc.semaphore("st_zeroed"))
        g.zero_one_set = ctx.enter_context(nc.semaphore("zero_one_set"))
        g.ones_in = [ctx.enter_context(nc.semaphore(f"ones_in{i}")) for i in range(3)]
        g.st_loaded = [ctx.enter_context(nc.semaphore(f"st_loaded{i}")) for i in range(3)]
        g.qs = nc.dram_tensor("qk_parts_dram", (B, 2, 3, HD_A, HEADS, T), BF16, kind="Internal").ap()
        lrep = nc.dram_tensor("bias_rows_dram", (HEADS * P * LROW + P,), F32, kind="Internal").ap()
        g.lrep = lrep[0:HEADS * P * LROW].rearrange("(h q n) -> h q n", h=HEADS, q=P)
        g.lrep_flat = lrep
        tables = nc.inline_tensor(rope_tables(), "rope_tables").ap()
        g.yT = sb("att_bT", [P, B * T])
        g.w_pair_loaded = ctx.enter_context(nc.semaphore("w_pair_loaded"))
        g.wo_pair_loaded = ctx.enter_context(nc.semaphore("wo_pair_loaded"))
        g.batch_xT_loaded = ctx.enter_context(nc.semaphore("batch_xT_loaded"))
        g.xnT = sb("x_normT", [P, B * T])
        cols = (NT * D + D - G4 * HD_A, UNITS * VU, 2 * 3 * CH)
        room = sb("room", [P, sum(cols)])
        g.O, g.V, parts_room = room[:, 0:cols[0]], room[:, cols[0]:cols[0] + cols[1]], room[:, cols[0] + cols[1]:sum(cols)]
        g.parts = [half.bitcast(BF16).rearrange("p (x s t) -> p x s t", x=2, s=3)
                   for half in (parts_room[:, 0:3 * CH], parts_room[:, 3 * CH:6 * CH])]
        f1 = ffn_buffers(nc, g, False, ctx, g.V, parts_room)
        with nc.Block() as block:
            with ExitStack() as c1:
                sb = lambda name, shape, dt=F32: c1.enter_context(nc.sbuf_tensor(name, shape, dt))
                g.maskq = sb("mask_query_key", [P, CH], BF16)
                g.zero_one = sb("zero_one", [3, 2, T], BF16)
                g.lrow = sb("bias_rows", [HEADS, LROW])
                g.stack = [sb(f"stack{i}", [ROWS, 2, G4, T], BF16) for i in range(3)]
                g.vu = [sb(f"v_unit{i}", [P, NQ, G4, VW]) for i in range(3)]
                g.mx = sb("row_max", [P, KINDS, G4, NQ])
                g.m_all = sb("row_max_joined", [P, G4 * NQ])
                g.mneg = sb("neg_max_parts", [P, 3, G4 * NQ], BF16)
                g.mrest = sb("max_rest", [P, G4 * NQ])
                g.mrow = sb("max_rows", [3 * G4 * NQ, P], BF16)
                g.oT = sb("oT", [P, CH])
                g.o_raw = sb("o_raw", [P, TPC, G4, VW])
                g.rden = sb("rden", [P, TPC, G4])
                prepare(nc, g, block, x, wqkv, rel, w_gate, w_up, w_down, wo_a, bo_a, bo_b, tables)
                rope_attention(nc, g, block, f1)
            sb = lambda name, shape, dt=F32: ctx.enter_context(nc.sbuf_tensor(name, shape, dt))
            g.w_pair = sb("w_pair", [P, 3, P])
            g.wo_pair = sb("wo_pair", [P, P])
            g.batch_xT = sb("batch_xT", [P, T])
            g.parts_room = sb("pair_parts", [P, 6 * CH])
            f2 = ffn_buffers(nc, g, True, ctx, g.xnT, g.parts_room)
            ffn(nc, g, block, False, out, f1, (wq, wk, wv, wo_b))
            bias_attention(nc, g, block, wq, wk, wv, wo_b, room, f1, f2)
            ffn(nc, g, block, True, out, f2)


_NAMES = ["L0_attn_a_x", "L0_attn_a_Wqkv", "L0_attn_a_Wo", "L0_attn_a_bo", "L0_attn_b_Wq", "L0_attn_b_Wk", "L0_attn_b_Wv",
          "L0_attn_b_Wo", "L0_attn_b_bo", "L0_attn_b_rel_pos_bias", "L0_ffn_w_gate", "L0_ffn_w_up", "L0_ffn_w_down"]


def kernel(**inputs):
    import concourse.bacc as bacc
    from concourse.bass_utils import run_bass_kernel_spmd

    nc = bacc.Bacc("TRN2", target_bir_lowering=False, num_devices=1)
    arrays, args = {}, []
    for name in _NAMES:
        a = np.ascontiguousarray(inputs[name])
        arrays[name] = a
        args.append(nc.dram_tensor(name, a.shape, mybir.dt.from_np(a.dtype), kind="ExternalInput").ap())
    out = nc.dram_tensor("out", (B, T, D), F32, kind="ExternalOutput").ap()
    build(nc, *args, out)
    r = run_bass_kernel_spmd(nc, [arrays], core_ids=[0])
    return r.results[0]["out"]
```
